# Optimizing a Trainium2 kernel written in Bass

```python
import numpy as np
import jax
import jax.numpy as jnp

def _softmax(x, axis=-1):
    return jax.nn.softmax(x, axis=axis)

def _gelu(x):
    return jax.nn.gelu(x, approximate=True)

def _silu(x):
    return jax.nn.silu(x)

def _sigmoid(x):
    return jax.nn.sigmoid(x)

def _layernorm(x, axis=-1, eps=1e-05):
    m = jnp.mean(x, axis=axis, keepdims=True)
    v = jnp.var(x, axis=axis, keepdims=True)
    return (x - m) / jnp.sqrt(v + eps)

def _scatter_add(tgt, idx, src, axis=0):
    return tgt.at[idx].add(src)

def _segment_sum(src, seg, n):
    return jax.ops.segment_sum(src, seg, n)
kernel_name = 'mk_gnn_resnorm_d4_gnn_r32_b15f36'

def setup_inputs(seed: int=0):
    np.random.seed(seed)
    _w = jnp.asarray

    def _rec_inputs():
        import jax
        import jax.numpy as jnp
        _gk = jax.random.key(seed)
        x = -0.000202 + 1 * jax.random.normal(jax.random.fold_in(_gk, 1), (3125, 128), jnp.float32)
        src = jax.random.randint(jax.random.fold_in(_gk, 2), (100000,), 0, 3125, jnp.int32)
        dst = jax.random.randint(jax.random.fold_in(_gk, 3), (100000,), 0, 3125, jnp.int32)
        _o = jnp.argsort(dst, stable=True)
        src = src[_o]
        dst = dst[_o]
        edge_attr_3 = 0.000669165 + 0.999965 * jax.random.normal(jax.random.fold_in(_gk, 13), (100000, 3), jnp.float32)
        edge_attr_4 = 0.000227908 + 0.99994 * jax.random.normal(jax.random.fold_in(_gk, 14), (100000, 4), jnp.float32)
        edge_attr_8 = jax.random.uniform(jax.random.fold_in(_gk, 15), (100000, 8), jnp.float32, 0.0, 0.999999)
        node_type_4 = jax.random.randint(jax.random.fold_in(_gk, 17), (3125,), 0, 4, jnp.int32)
        return (x, src, dst, edge_attr_3, edge_attr_4, edge_attr_8, node_type_4)
    x, src, dst, edge_attr_3, edge_attr_4, edge_attr_8, node_type_4 = _rec_inputs()

    def _L0_gnn_setup():
        import jax, jax.numpy as jnp
        import numpy as np
        N_NODES = 50000
        N_EDGES = 25000
        D = 128
        LN_EPS = 1e-05
        key = jax.random.key(seed)
        ks = jax.random.split(key, 8)
        h = jax.random.normal(ks[0], (N_NODES, D), dtype=jnp.float32)
        edge_index = jax.random.randint(ks[1], (2, N_EDGES), 0, N_NODES, dtype=jnp.int32)
        s = 1.0 / np.sqrt(D)
        W1 = jax.random.uniform(ks[2], (D, D), jnp.float32, -s, s)
        b1 = jax.random.uniform(ks[3], (D,), jnp.float32, -s, s)
        W2 = jax.random.uniform(ks[4], (D, D), jnp.float32, -s, s)
        b2 = jax.random.uniform(ks[5], (D,), jnp.float32, -s, s)
        eps = jnp.zeros((), jnp.float32)
        gamma = jnp.ones((D,), jnp.float32)
        beta = jnp.zeros((D,), jnp.float32)
        return {'h': h, 'edge_index': edge_index, 'eps': eps, 'W1': W1, 'b1': b1, 'W2': W2, 'b2': b2, 'gamma': gamma, 'beta': beta}
    _L0_gnn_all = _L0_gnn_setup()
    _L0_gnn_in = {k: v for k, v in _L0_gnn_all.items() if k in ('eps', 'W1', 'b1', 'W2', 'b2', 'gamma', 'beta')}
    del _L0_gnn_all

    def _L1_gnn_setup():
        import jax, jax.numpy as jnp
        import numpy as np
        MUL = 32
        N_NODES = 512
        N_EDGES = 8192
        AVG_NEIGH = 16.0
        N_SPECIES = 4
        RADIAL_DIM = 8
        INV_SQRT3 = 0.5773502691896258
        key = jax.random.key(seed)
        ks = jax.random.split(key, 14)
        f32 = jnp.float32
        return {'node_features': jax.random.normal(ks[0], (N_NODES, 4 * MUL), dtype=f32), 'edge_sh': jax.random.normal(ks[1], (N_EDGES, 4), dtype=f32), 'radial_embedding': jax.random.uniform(ks[2], (N_EDGES, RADIAL_DIM), dtype=f32), 'W_up_s': jax.random.normal(ks[3], (MUL, MUL), dtype=f32), 'W_up_v': jax.random.normal(ks[4], (MUL, MUL), dtype=f32), 'W_r1': jax.random.normal(ks[5], (RADIAL_DIM, RADIAL_DIM), dtype=f32), 'W_r2': jax.random.normal(ks[6], (RADIAL_DIM, 4 * MUL), dtype=f32), 'W_dn_s': jax.random.normal(ks[7], (2 * MUL, 2 * MUL), dtype=f32), 'W_dn_v': jax.random.normal(ks[8], (2 * MUL, MUL), dtype=f32), 'W_sk_s': jax.random.normal(ks[9], (N_SPECIES, MUL, 2 * MUL), dtype=f32), 'W_sk_v': jax.random.normal(ks[10], (N_SPECIES, MUL, MUL), dtype=f32), 'senders': jax.random.randint(ks[11], (N_EDGES,), 0, N_NODES), 'receivers': jax.random.randint(ks[12], (N_EDGES,), 0, N_NODES), 'node_species': jax.random.randint(ks[13], (N_NODES,), 0, N_SPECIES)}
    _L1_gnn_all = _L1_gnn_setup()
    _L1_gnn_in = {k: v for k, v in _L1_gnn_all.items() if k in ('W_up_s', 'W_up_v', 'W_r1', 'W_r2', 'W_dn_s', 'W_dn_v', 'W_sk_s', 'W_sk_v')}
    del _L1_gnn_all

    def _L2_gnn_setup():
        import jax, jax.numpy as jnp
        import numpy as np
        D_MODEL = 128
        N_HEADS = 8
        HEAD_DIM = D_MODEL // N_HEADS
        N_NODES = 50000
        N_EDGES = 20000
        key = jax.random.key(seed)
        ks = jax.random.split(key, 10)
        sd = 1.0 / np.sqrt(D_MODEL)
        return {'node_embeds': jax.random.normal(ks[0], (N_NODES, D_MODEL), dtype=jnp.float32), 'edge_index': jax.random.randint(ks[1], (2, N_EDGES), 0, N_NODES, dtype=jnp.int64), 'Wq': jax.random.uniform(ks[2], (D_MODEL, D_MODEL), jnp.float32, -sd, sd), 'bq': jax.random.uniform(ks[3], (D_MODEL,), jnp.float32, -sd, sd), 'Wk': jax.random.uniform(ks[4], (D_MODEL, D_MODEL), jnp.float32, -sd, sd), 'bk': jax.random.uniform(ks[5], (D_MODEL,), jnp.float32, -sd, sd), 'Wv': jax.random.uniform(ks[6], (D_MODEL, D_MODEL), jnp.float32, -sd, sd), 'bv': jax.random.uniform(ks[7], (D_MODEL,), jnp.float32, -sd, sd), 'gamma': jnp.ones((D_MODEL,), jnp.float32), 'beta': jnp.zeros((D_MODEL,), jnp.float32)}
    _L2_gnn_all = _L2_gnn_setup()
    _L2_gnn_in = {k: v for k, v in _L2_gnn_all.items() if k in ('Wq', 'bq', 'Wk', 'bk', 'Wv', 'bv', 'gamma', 'beta')}
    del _L2_gnn_all

    def _L3_gnn_setup():
        import jax, jax.numpy as jnp
        import numpy as np
        N, E, IN, H, ED = (50000, 25000, 128, 128, 3)
        EPS = 1e-05

        def _gat_conv(x, src, dst, ea, W, a_src, a_dst, We, a_edge, bias):
            n = x.shape[0]
            loops = jnp.arange(n, dtype=src.dtype)
            s = jnp.concatenate([src, loops])
            d = jnp.concatenate([dst, loops])
            ea_full = jnp.concatenate([ea, jnp.broadcast_to(ea.mean(0), (n, ea.shape[1]))], 0)
            h = x @ W
            al_s = h @ a_src
            al_d = h @ a_dst
            al_e = ea_full @ We @ a_edge
            alpha = jax.nn.leaky_relu(al_s[s] + al_d[d] + al_e, 0.2)
            amax = jax.ops.segment_max(alpha, d, num_segments=n)
            ex = jnp.exp(alpha - amax[d])
            denom = jax.ops.segment_sum(ex, d, num_segments=n)
            coef = ex / (denom[d] + 1e-16)
            out = jax.ops.segment_sum(h[s] * coef[:, None], d, num_segments=n)
            return out + bias

        def _bn(x, gamma, beta):
            mu = x.mean(0)
            var = ((x - mu) ** 2).mean(0)
            return (x - mu) * jax.lax.rsqrt(var + EPS) * gamma + beta
        key = jax.random.key(seed)
        ks = jax.random.split(key, 40)
        inp = {'x': jax.random.normal(ks[0], (N, IN), jnp.float32), 'edge_index': jax.random.randint(ks[1], (2, E), 0, N, dtype=jnp.int32), 'batch': jnp.zeros((N,), jnp.int32), 'edge_attr': jax.random.normal(ks[2], (E, ED), jnp.float32)}
        i = 3
        for l, cin in ((1, IN), (2, H), (3, H)):
            s = 1.0 / np.sqrt(cin)
            inp[f'W{l}'] = jax.random.normal(ks[i], (cin, H), jnp.float32) * s
            i += 1
            inp[f'as{l}'] = jax.random.normal(ks[i], (H,), jnp.float32) * 0.1
            i += 1
            inp[f'ad{l}'] = jax.random.normal(ks[i], (H,), jnp.float32) * 0.1
            i += 1
            inp[f'We{l}'] = jax.random.normal(ks[i], (ED, H), jnp.float32) * 0.5
            i += 1
            inp[f'ae{l}'] = jax.random.normal(ks[i], (H,), jnp.float32) * 0.1
            i += 1
            inp[f'b{l}'] = jnp.zeros((H,), jnp.float32)
            inp[f'g{l}'] = jnp.ones((H,), jnp.float32)
            inp[f'be{l}'] = jnp.zeros((H,), jnp.float32)
        return inp
    _L3_gnn_all = _L3_gnn_setup()
    _L3_gnn_in = {k: v for k, v in _L3_gnn_all.items() if k in ('W1', 'as1', 'ad1', 'We1', 'ae1', 'b1', 'g1', 'be1', 'W2', 'as2', 'ad2', 'We2', 'ae2', 'b2', 'g2', 'be2', 'W3', 'as3', 'ad3', 'We3', 'ae3', 'b3', 'g3', 'be3')}
    del _L3_gnn_all
    return {'x': x, 'src': src, 'dst': dst, 'edge_attr_3': edge_attr_3, 'edge_attr_4': edge_attr_4, 'edge_attr_8': edge_attr_8, 'node_type_4': node_type_4, 'L0_gnn_eps': _L0_gnn_in['eps'], 'L0_gnn_W1': _L0_gnn_in['W1'], 'L0_gnn_b1': _L0_gnn_in['b1'], 'L0_gnn_W2': _L0_gnn_in['W2'], 'L0_gnn_b2': _L0_gnn_in['b2'], 'L0_gnn_gamma': _L0_gnn_in['gamma'], 'L0_gnn_beta': _L0_gnn_in['beta'], 'L1_gnn_W_up_s': _L1_gnn_in['W_up_s'], 'L1_gnn_W_up_v': _L1_gnn_in['W_up_v'], 'L1_gnn_W_r1': _L1_gnn_in['W_r1'], 'L1_gnn_W_r2': _L1_gnn_in['W_r2'], 'L1_gnn_W_dn_s': _L1_gnn_in['W_dn_s'], 'L1_gnn_W_dn_v': _L1_gnn_in['W_dn_v'], 'L1_gnn_W_sk_s': _L1_gnn_in['W_sk_s'], 'L1_gnn_W_sk_v': _L1_gnn_in['W_sk_v'], 'L2_gnn_Wq': _L2_gnn_in['Wq'], 'L2_gnn_bq': _L2_gnn_in['bq'], 'L2_gnn_Wk': _L2_gnn_in['Wk'], 'L2_gnn_bk': _L2_gnn_in['bk'], 'L2_gnn_Wv': _L2_gnn_in['Wv'], 'L2_gnn_bv': _L2_gnn_in['bv'], 'L2_gnn_gamma': _L2_gnn_in['gamma'], 'L2_gnn_beta': _L2_gnn_in['beta'], 'L3_gnn_W1': _L3_gnn_in['W1'], 'L3_gnn_as1': _L3_gnn_in['as1'], 'L3_gnn_ad1': _L3_gnn_in['ad1'], 'L3_gnn_We1': _L3_gnn_in['We1'], 'L3_gnn_ae1': _L3_gnn_in['ae1'], 'L3_gnn_b1': _L3_gnn_in['b1'], 'L3_gnn_g1': _L3_gnn_in['g1'], 'L3_gnn_be1': _L3_gnn_in['be1'], 'L3_gnn_W2': _L3_gnn_in['W2'], 'L3_gnn_as2': _L3_gnn_in['as2'], 'L3_gnn_ad2': _L3_gnn_in['ad2'], 'L3_gnn_We2': _L3_gnn_in['We2'], 'L3_gnn_ae2': _L3_gnn_in['ae2'], 'L3_gnn_b2': _L3_gnn_in['b2'], 'L3_gnn_g2': _L3_gnn_in['g2'], 'L3_gnn_be2': _L3_gnn_in['be2'], 'L3_gnn_W3': _L3_gnn_in['W3'], 'L3_gnn_as3': _L3_gnn_in['as3'], 'L3_gnn_ad3': _L3_gnn_in['ad3'], 'L3_gnn_We3': _L3_gnn_in['We3'], 'L3_gnn_ae3': _L3_gnn_in['ae3'], 'L3_gnn_b3': _L3_gnn_in['b3'], 'L3_gnn_g3': _L3_gnn_in['g3'], 'L3_gnn_be3': _L3_gnn_in['be3']}

def reference(x, src, dst, edge_attr_3, edge_attr_4, edge_attr_8, node_type_4, L0_gnn_eps, L0_gnn_W1, L0_gnn_b1, L0_gnn_W2, L0_gnn_b2, L0_gnn_gamma, L0_gnn_beta, L1_gnn_W_up_s, L1_gnn_W_up_v, L1_gnn_W_r1, L1_gnn_W_r2, L1_gnn_W_dn_s, L1_gnn_W_dn_v, L1_gnn_W_sk_s, L1_gnn_W_sk_v, L2_gnn_Wq, L2_gnn_bq, L2_gnn_Wk, L2_gnn_bk, L2_gnn_Wv, L2_gnn_bv, L2_gnn_gamma, L2_gnn_beta, L3_gnn_W1, L3_gnn_as1, L3_gnn_ad1, L3_gnn_We1, L3_gnn_ae1, L3_gnn_b1, L3_gnn_g1, L3_gnn_be1, L3_gnn_W2, L3_gnn_as2, L3_gnn_ad2, L3_gnn_We2, L3_gnn_ae2, L3_gnn_b2, L3_gnn_g2, L3_gnn_be2, L3_gnn_W3, L3_gnn_as3, L3_gnn_ad3, L3_gnn_We3, L3_gnn_ae3, L3_gnn_b3, L3_gnn_g3, L3_gnn_be3):
    import jax
    import jax.numpy as jnp

    def _L0_gnn_ref(h, edge_index, eps, W1, b1, W2, b2, gamma, beta):
        import jax, jax.numpy as jnp
        import numpy as np
        N_NODES = 50000
        N_EDGES = 25000
        D = 128
        LN_EPS = 1e-05
        src, dst = (edge_index[0], edge_index[1])
        agg = jax.ops.segment_sum(h[src], dst, num_segments=h.shape[0])
        z = (1.0 + eps) * h + agg
        z = jax.nn.relu(z @ W1 + b1) @ W2 + b2
        r = z + h
        mu = jnp.mean(r, axis=-1, keepdims=True)
        var = jnp.mean((r - mu) ** 2, axis=-1, keepdims=True)
        ln = (r - mu) * jax.lax.rsqrt(var + LN_EPS) * gamma + beta
        return jax.nn.relu(ln)

    def _L1_gnn_ref(node_features, edge_sh, radial_embedding, W_up_s, W_up_v, W_r1, W_r2, W_dn_s, W_dn_v, W_sk_s, W_sk_v, senders, receivers, node_species):
        import jax, jax.numpy as jnp
        import numpy as np
        MUL = 32
        N_NODES = 512
        N_EDGES = 8192
        AVG_NEIGH = 16.0
        N_SPECIES = 4
        RADIAL_DIM = 8
        INV_SQRT3 = 0.5773502691896258
        n = node_features.shape[0]
        s = node_features[:, :MUL]
        v = node_features[:, MUL:].reshape(n, MUL, 3)
        s1 = s @ W_up_s * MUL ** (-0.5)
        v1 = jnp.einsum('nmi,mk->nki', v, W_up_v) * MUL ** (-0.5)
        ss = s1[senders]
        vs = v1[senders]
        yv = edge_sh[:, 1:4]
        m_v_tp = ss[:, :, None] * yv[:, None, :]
        m_s_tp = jnp.einsum('emi,ei->em', vs, yv) * INV_SQRT3
        h = jax.nn.silu(radial_embedding @ W_r1 * RADIAL_DIM ** (-0.5))
        w = h @ W_r2 * RADIAL_DIM ** (-0.5)
        w_ss, w_vs, w_vt, w_st = jnp.split(w, 4, axis=1)
        m_s = jnp.concatenate([ss * w_ss, m_s_tp * w_st], axis=1)
        m_v = jnp.concatenate([vs * w_vs[:, :, None], m_v_tp * w_vt[:, :, None]], axis=1)
        inv = AVG_NEIGH ** (-0.5)
        S = jax.ops.segment_sum(m_s, receivers, num_segments=n) * inv
        V = jax.ops.segment_sum(m_v.reshape(m_v.shape[0], -1), receivers, num_segments=n).reshape(n, 2 * MUL, 3) * inv
        g_s = S @ W_dn_s * (2 * MUL) ** (-0.5)
        g_v = jnp.einsum('nmi,mk->nki', V, W_dn_v) * (2 * MUL) ** (-0.5)
        sk_s = jnp.einsum('nm,nmk->nk', s, W_sk_s[node_species]) * MUL ** (-0.5)
        sk_v = jnp.einsum('nmi,nmk->nki', v, W_sk_v[node_species]) * MUL ** (-0.5)
        g_s = 0.5 * (g_s + sk_s)
        g_v = 0.5 * (g_v + sk_v)
        feat_s = jax.nn.silu(g_s[:, :MUL])
        gates = jax.nn.silu(g_s[:, MUL:])
        out_v = g_v * gates[:, :, None]
        return jnp.concatenate([feat_s, out_v.reshape(n, 3 * MUL)], axis=1)

    def _L2_gnn_ref(node_embeds, edge_index, Wq, bq, Wk, bk, Wv, bv, gamma, beta):
        import jax, jax.numpy as jnp
        import numpy as np
        D_MODEL = 128
        N_HEADS = 8
        HEAD_DIM = D_MODEL // N_HEADS
        N_NODES = 50000
        N_EDGES = 20000
        num_nodes = node_embeds.shape[0]
        rows, cols = (edge_index[0], edge_index[1])
        src = node_embeds[rows]
        tgt = node_embeds[cols]
        q = (src @ Wq.T + bq).reshape(-1, N_HEADS, HEAD_DIM)
        k = (tgt @ Wk.T + bk).reshape(-1, N_HEADS, HEAD_DIM)
        v = (tgt @ Wv.T + bv).reshape(-1, N_HEADS, HEAD_DIM)
        att = jnp.einsum('ehd,ehd->eh', q, k) / jnp.sqrt(jnp.float32(HEAD_DIM))
        exp_att = jnp.exp(jnp.clip(att, -10.0, 10.0))
        att_sum = jax.ops.segment_sum(exp_att, rows, num_segments=num_nodes)
        att_norm = exp_att / (att_sum[rows] + 1e-08)
        weighted_v = (att_norm[..., None] * v).reshape(-1, D_MODEL)
        out = jax.ops.segment_sum(weighted_v, rows, num_segments=num_nodes)
        out = out + node_embeds
        mu = jnp.mean(out, axis=-1, keepdims=True)
        var = jnp.mean(jnp.square(out - mu), axis=-1, keepdims=True)
        out = (out - mu) * jax.lax.rsqrt(var + 1e-06) * gamma + beta
        return out

    def _L3_gnn_ref(x, edge_index, batch, edge_attr, W1, as1, ad1, We1, ae1, b1, g1, be1, W2, as2, ad2, We2, ae2, b2, g2, be2, W3, as3, ad3, We3, ae3, b3, g3, be3):
        import jax, jax.numpy as jnp
        import numpy as np
        N, E, IN, H, ED = (50000, 25000, 128, 128, 3)
        EPS = 1e-05

        def _gat_conv(x, src, dst, ea, W, a_src, a_dst, We, a_edge, bias):
            n = x.shape[0]
            loops = jnp.arange(n, dtype=src.dtype)
            s = jnp.concatenate([src, loops])
            d = jnp.concatenate([dst, loops])
            ea_full = jnp.concatenate([ea, jnp.broadcast_to(ea.mean(0), (n, ea.shape[1]))], 0)
            h = x @ W
            al_s = h @ a_src
            al_d = h @ a_dst
            al_e = ea_full @ We @ a_edge
            alpha = jax.nn.leaky_relu(al_s[s] + al_d[d] + al_e, 0.2)
            amax = jax.ops.segment_max(alpha, d, num_segments=n)
            ex = jnp.exp(alpha - amax[d])
            denom = jax.ops.segment_sum(ex, d, num_segments=n)
            coef = ex / (denom[d] + 1e-16)
            out = jax.ops.segment_sum(h[s] * coef[:, None], d, num_segments=n)
            return out + bias

        def _bn(x, gamma, beta):
            mu = x.mean(0)
            var = ((x - mu) ** 2).mean(0)
            return (x - mu) * jax.lax.rsqrt(var + EPS) * gamma + beta
        src, dst = (edge_index[0], edge_index[1])
        h = _gat_conv(x, src, dst, edge_attr, W1, as1, ad1, We1, ae1, b1)
        h = _bn(jax.nn.leaky_relu(h, 0.01), g1, be1)
        h = _gat_conv(h, src, dst, edge_attr, W2, as2, ad2, We2, ae2, b2)
        h = _bn(jax.nn.leaky_relu(h, 0.01), g2, be2)
        h = _gat_conv(h, src, dst, edge_attr, W3, as3, ad3, We3, ae3, b3)
        h = _bn(jax.nn.leaky_relu(h, 0.01), g3, be3)
        return h
    edge_index = jnp.stack([src, dst])
    batch0 = jnp.zeros((3125,), jnp.int32)
    x = _layernorm(x + _L0_gnn_ref(x, edge_index, L0_gnn_eps, L0_gnn_W1, L0_gnn_b1, L0_gnn_W2, L0_gnn_b2, L0_gnn_gamma, L0_gnn_beta), axis=-1)
    x = _layernorm(x + _L1_gnn_ref(x, edge_attr_4, edge_attr_8, L1_gnn_W_up_s, L1_gnn_W_up_v, L1_gnn_W_r1, L1_gnn_W_r2, L1_gnn_W_dn_s, L1_gnn_W_dn_v, L1_gnn_W_sk_s, L1_gnn_W_sk_v, src, dst, node_type_4), axis=-1)
    x = _layernorm(x + _L2_gnn_ref(x, edge_index, L2_gnn_Wq, L2_gnn_bq, L2_gnn_Wk, L2_gnn_bk, L2_gnn_Wv, L2_gnn_bv, L2_gnn_gamma, L2_gnn_beta), axis=-1)
    x = _layernorm(x + _L3_gnn_ref(x, edge_index, batch0, edge_attr_3, L3_gnn_W1, L3_gnn_as1, L3_gnn_ad1, L3_gnn_We1, L3_gnn_ae1, L3_gnn_b1, L3_gnn_g1, L3_gnn_be1, L3_gnn_W2, L3_gnn_as2, L3_gnn_ad2, L3_gnn_We2, L3_gnn_ae2, L3_gnn_b2, L3_gnn_g2, L3_gnn_be2, L3_gnn_W3, L3_gnn_as3, L3_gnn_ad3, L3_gnn_We3, L3_gnn_ae3, L3_gnn_b3, L3_gnn_g3, L3_gnn_be3), axis=-1)
    return x

_drawn_inputs = setup_inputs


def setup_inputs(seed=0):
    import zlib

    import numpy as np

    out = dict(_drawn_inputs(seed))
    spreads = {'L0_gnn_gamma': (1.0, 0.2),
     'L0_gnn_beta': (0.0, 0.1),
     'L2_gnn_gamma': (1.0, 0.2),
     'L2_gnn_beta': (0.0, 0.1),
     'L3_gnn_b1': (0.0, 0.1),
     'L3_gnn_g1': (1.0, 0.2),
     'L3_gnn_be1': (0.0, 0.1),
     'L3_gnn_b2': (0.0, 0.1),
     'L3_gnn_g2': (1.0, 0.2),
     'L3_gnn_be2': (0.0, 0.1),
     'L3_gnn_b3': (0.0, 0.1),
     'L3_gnn_g3': (1.0, 0.2),
     'L3_gnn_be3': (0.0, 0.1)}
    factors = {'L2_gnn_bq': 8.0, 'L2_gnn_bk': 200.0}
    for name, (base, spread) in spreads.items():
        noise = np.random.default_rng([zlib.crc32(name.encode()), seed]).standard_normal(out[name].shape)
        drawn = base * np.exp(spread * noise) if base else spread * noise
        out[name] = jnp.asarray(drawn.astype(out[name].dtype))
    for name, factor in factors.items():
        out[name] = (out[name] * factor).astype(out[name].dtype)
    return out
```

```python
from contextlib import ExitStack

import concourse.bass as bass
from concourse import mybir

F32 = mybir.dt.float32
I32 = mybir.dt.int32
ALU = mybir.AluOpType
ACT = mybir.ActivationFunctionType
AX = mybir.AxisListType

NODES = 3125
EDGES = 100000
D = 128
LANES = 125
BLOCKS = NODES // LANES
PER_LANE = EDGES // LANES
SLOTS = 128
GROUP = 4
MOST_TILES = (EDGES + BLOCKS * (SLOTS - 1)) // SLOTS
TILES = -(-MOST_TILES // (2 * GROUP)) * 2 * GROUP
GROUPS = TILES // GROUP
RECORD = 16
CHUNK = 8
HEADS = 8
HEAD = D // HEADS
MUL = 32
SPECIES = 4
RADIAL = 8
FAR = -1e30
RESET = -3e38


def ds(start, size):
    return bass.ds(start, size)


class Chain:

    def __init__(self, engine, done):
        self.engine, self.done, self.n = engine, done, 0

    def __call__(self, instruction):
        instruction.then_inc(self.done, 1)
        self.n += 1
        self.engine.wait_ge(self.done, self.n)


RING = 4
CREDIT = RING


def made(k):
    return k + (CREDIT + 1)


def free(k, ring=RING):
    return k + (CREDIT + 1 - ring)


def is_new(used):
    return isinstance(used, int) and used == 0


def in_steps(engine, count, stages, ring=RING):
    lead = -(-max(max(lag for lag, _ in stages), ring) // ring) * ring

    def step(n):
        for lag, stage in stages:
            if 0 <= n - lag < count:
                stage(n - lag, (n - lag) % ring, (n - lag) // ring)

    for n in range(lead):
        step(n)
    with engine.Fori(lead // ring, count // ring) as i:
        for turn in range(ring):
            for lag, stage in stages:
                q = turn - lag
                stage(i * ring + q, q % ring, i + q // ring)
    for n in range(count // ring * ring, count + lead):
        step(n)


class Phase:

    def __init__(self, nc, name):
        self.nc, self.name, self.stack, self.sems = nc, name, ExitStack(), []

    def __enter__(self):
        self.stack.__enter__()
        return self

    def __exit__(self, *error):
        return self.stack.__exit__(*error)

    def clear(self):
        for sem in self.sems:
            self.nc.sync.sem_clear(sem)

    def sbuf(self, name, shape, dtype=F32):
        return self.stack.enter_context(self.nc.sbuf_tensor(f"{self.name}_{name}", shape, dtype))

    def psum(self, name, shape, dtype=F32):
        return self.stack.enter_context(self.nc.psum_tensor(f"{self.name}_{name}", shape, dtype))

    def sem(self, name):
        self.sems.append(self.stack.enter_context(self.nc.semaphore(f"{self.name}_{name}")))
        return self.sems[-1]

    def block(self):
        self.stack.callback(self.clear)
        return self.stack.enter_context(self.nc.Block())


def software_dma_sems(nc, m, ph, count):
    return [m.kept.enter_context(nc.semaphore(f"{ph.name}_landed{s}")) for s in range(count)]


def row_of(vector, partitions):
    return vector.rearrange("(a n) -> a n", a=1).to_broadcast([partitions, vector.shape[0]])


def constants(nc, m):
    with Phase(nc, "constants") as ph:
        step, whole = ph.sem("step"), ph.sem("whole")
        ramp = ph.sbuf("ramp", [128, TILES], I32)
        block = ph.block()

        @block.gpsimd
        def _(pool):
            chain = Chain(pool, step)
            chain(pool.memset(m.ones[:, :], 1.0))
            chain(pool.memset(m.ident[:, :], 0.0))
            chain(pool.affine_select(out=m.ident[:, :], in_=m.ident[:, :], compare_op=ALU.not_equal, fill=1.0,
                                     base=0, pattern=[[-1, 128]], channel_multiplier=1))
            chain(pool.affine_select(out=m.earlier[:, :], in_=m.ones[:, :], compare_op=ALU.is_gt, fill=0.0,
                                     base=0, pattern=[[1, 128]], channel_multiplier=-1))
            chain(pool.iota(ramp[:, :], pattern=[[1, TILES]], base=0, channel_multiplier=0))
            chain(pool.tensor_copy(m.ramp[:, :], ramp[:, :]))
            pool.sem_inc(whole, 1)

        @block.vector
        def _(dve):
            dve.wait_ge(whole, 1)


def put_in_order(nc, m, name, key, row, place, tile_block, reset=None):
    with Phase(nc, name) as ph:
        loaded, step, counts_ready, sums_ready = (ph.sem(x) for x in ("loaded", "step", "counts", "sums"))
        key_int = ph.sbuf("key_int", [LANES, PER_LANE], I32)
        key_f = ph.sbuf("key_f", [LANES, PER_LANE])
        blk = ph.sbuf("blk", [LANES, PER_LANE])
        inside = ph.sbuf("inside", [LANES, PER_LANE])
        count = ph.sbuf("count", [LANES, PER_LANE])
        position = ph.sbuf("position", [LANES, PER_LANE])
        ones = ph.sbuf("ones", [LANES, PER_LANE])
        low = ph.sbuf("low", [LANES, PER_LANE], I32)
        first_node = ph.sbuf("first_node", [LANES, BLOCKS])
        block_sum = ph.sbuf("block_sum", [LANES, BLOCKS])
        at_least = ph.sbuf("at_least", [LANES, BLOCKS + 1])
        own = ph.sbuf("own", [LANES, BLOCKS])
        tiles_int = ph.sbuf("tiles_int", [128, BLOCKS], I32)
        tiles = ph.sbuf("tiles", [128, BLOCKS])
        tile_end = ph.sbuf("tile_end", [128, BLOCKS])
        base = ph.sbuf("base", [LANES, BLOCKS])
        tile_blk = ph.sbuf("tile_blk", [128, TILES])
        sums = ph.psum("sums", [128, 512])
        block = ph.block()

        @block.sync
        def _(sp):
            sp.dma_start(key_int[:, :], key.rearrange("(p c) -> p c", p=LANES)).then_inc(loaded, 16)

        @block.vector
        def _(dve):
            chain = Chain(dve, step)
            chain(dve.tensor_scalar(first_node[:, :], m.ramp[0:LANES, 0:BLOCKS], float(LANES), None, ALU.mult))
            chain(dve.memset(blk[:, :], 0.0))
            chain(dve.memset(ones[:, :], 1.0))
            chain(dve.memset(position[:, :], 0.0))
            chain(dve.memset(block_sum[:, 0:1], 0.0))
            chain(dve.memset(at_least[:, 0:1], float(PER_LANE)))
            chain(dve.memset(at_least[:, BLOCKS:BLOCKS + 1], 0.0))
            dve.wait_ge(loaded, 16)
            chain(dve.tensor_copy(key_f[:, :], key_int[:, :]))
            before = chain.n
            with dve.Fori(1, BLOCKS) as b:
                dve.wait_ge(step, b + (before - 1))
                dve.scalar_tensor_tensor(blk[:, :], key_f[:, :], first_node[:, ds(b, 1)], blk[:, :], ALU.is_ge,
                                         ALU.add, accum_out=block_sum[:, ds(b, 1)]).then_inc(step, 1)
            chain.n += BLOCKS - 1
            dve.wait_ge(step, chain.n)
            chain(dve.tensor_tensor(at_least[:, 1:BLOCKS], block_sum[:, 1:BLOCKS], block_sum[:, 0:BLOCKS - 1],
                                    ALU.subtract))
            chain(dve.tensor_tensor(own[:, :], at_least[:, 0:BLOCKS], at_least[:, 1:BLOCKS + 1], ALU.subtract))
            dve.sem_inc(counts_ready, 1)
            chain(dve.scalar_tensor_tensor(place[:, :], blk[:, :], -float(LANES), key_f[:, :], ALU.mult, ALU.add))
            chain(dve.tensor_scalar(place[:, :], place[:, :], 1.0, None, ALU.add))
            dve.wait_ge(sums_ready, 1)
            chain(dve.tensor_scalar(tiles_int[:, :], sums[:, 64:64 + BLOCKS], float(SLOTS - 1), None, ALU.add))
            chain(dve.tensor_scalar(tiles_int[:, :], tiles_int[:, :], 7, None, ALU.arith_shift_right))
            chain(dve.tensor_copy(tiles[:, :], tiles_int[:, :]))
            chain(dve.tensor_tensor_scan(tile_end[:, :], m.ones[:, 0:BLOCKS], tiles[:, :], 0.0, ALU.mult, ALU.add))
            chain(dve.tensor_tensor(base[:, :], tile_end[0:LANES, :], tiles[0:LANES, :], ALU.subtract))
            chain(dve.tensor_scalar(base[:, :], base[:, :], float(SLOTS), -1.0, ALU.mult, ALU.add))
            chain(dve.tensor_tensor(base[:, :], base[:, :], sums[0:LANES, 0:BLOCKS], ALU.add))
            before = chain.n
            with dve.Fori(0, BLOCKS) as b:
                dve.wait_ge(step, b * 3 + before)
                dve.tensor_scalar(inside[:, :], blk[:, :], m.ramp[0:LANES, ds(b, 1)], None, ALU.is_equal)\
                    .then_inc(step, 1)
                dve.wait_ge(step, b * 3 + (before + 1))
                dve.tensor_tensor_scan(count[:, :], ones[:, :], inside[:, :], base[:, ds(b, 1)], ALU.mult, ALU.add)\
                    .then_inc(step, 1)
                dve.wait_ge(step, b * 3 + (before + 2))
                dve.nop(nofuse=True)
                dve.copy_predicated(out=position[:, :], mask=inside[:, :].bitcast(I32), data=count[:, :])\
                    .then_inc(step, 1)
            chain.n += 3 * BLOCKS
            dve.wait_ge(step, chain.n)
            chain(dve.tensor_copy(key_int[:, :], position[:, :]))
            chain(dve.tensor_scalar(low[:, :], key_int[:, :], SLOTS - 1, None, ALU.bitwise_and))
            chain(dve.tensor_scalar(key_int[:, :], key_int[:, :], 7, None, ALU.arith_shift_right))
            chain(dve.scalar_tensor_tensor(row[:, :], low[:, :], float(TILES), key_int[:, :], ALU.mult, ALU.add))
            chain(dve.memset(tile_blk[:, :], 0.0))
            before = chain.n
            with dve.Fori(0, BLOCKS - 1) as b:
                dve.wait_ge(step, b + before)
                dve.scalar_tensor_tensor(tile_blk[:, :], m.ramp[:, :], tile_end[:, ds(b, 1)], tile_blk[:, :],
                                         ALU.is_ge, ALU.add).then_inc(step, 1)
            chain.n += BLOCKS - 1
            dve.wait_ge(step, chain.n)
            chain(dve.tensor_copy(tile_block[:, :], tile_blk[0:1, :]))
            if reset is not None:
                chain(dve.tensor_tensor(reset[:, 1:TILES], tile_blk[:, 1:TILES], tile_blk[:, 0:TILES - 1],
                                        ALU.not_equal))
                chain(dve.memset(reset[:, 0:1], 1.0))
                chain(dve.tensor_scalar(reset[:, :], reset[:, :], RESET, None, ALU.mult))

        @block.tensor
        def _(pe):
            pe.wait_ge(counts_ready, 1)
            pe.matmul(sums[0:LANES, 0:BLOCKS], m.earlier[0:LANES, 0:LANES], own[:, :], start=True, stop=True)
            pe.matmul(sums[:, 64:64 + BLOCKS], m.ones[0:LANES, :], own[:, :], start=True, stop=True)\
                .then_inc(sums_ready, 1)


def scatter_records(nc, m, name, table, width, row, parts, clear):
    steps = PER_LANE // CHUNK
    with Phase(nc, name) as ph:
        cleared, zeros_out, table_in = (ph.sem(x) for x in ("cleared", "zeros_out", "table_in"))
        by_act, by_dve = ph.sem("by_act"), ph.sem("by_dve")
        scattered = software_dma_sems(nc, m, ph, 2)
        record = ph.sbuf("record", [LANES, 2, CHUNK, width])
        index = ph.sbuf("index", [LANES, 2, CHUNK], I32)
        block = ph.block()
        mine = {"act": [x for n, x in enumerate(parts) if n % 2 == 0], "dve": [x for n, x in enumerate(parts) if n % 2]}

        @block.vector
        def _(dve):
            dve.memset(clear[:, :], 0.0).then_inc(cleared, 1)

            def fill(k, s, used):
                if not is_new(used):
                    dve.wait_ge(scattered[s], used * (16 * CHUNK))
                    dve.nop(nofuse=True)
                for first, n, source in mine["dve"]:
                    last = dve.tensor_copy(record[:, s, :, first:first + n], source[:, ds(k * CHUNK, CHUNK), :])
                last.then_inc(by_dve, 1)

            in_steps(dve, steps, [(0, fill)], 2)

        @block.scalar
        def _(act):
            def fill(k, s, used):
                if not is_new(used):
                    act.wait_ge(scattered[s], used * (16 * CHUNK))
                    act.nop(nofuse=True)
                act.copy(index[:, s, :], row[:, ds(k * CHUNK, CHUNK)])
                for first, n, source in mine["act"]:
                    last = act.copy(record[:, s, :, first:first + n], source[:, ds(k * CHUNK, CHUNK), :])
                last.then_inc(by_act, 1)

            in_steps(act, steps, [(0, fill)], 2)

        @block.gpsimd
        def _(pool):
            pool.wait_ge(zeros_out, 16)

            def scatter(k, s, used):
                pool.wait_ge(by_act, k + 1)
                pool.nop(nofuse=True)
                pool.wait_ge(by_dve, k + 1)
                pool.nop(nofuse=True)
                for c in range(CHUNK):
                    pool.indirect_dma_start(
                        out=table[:, :], out_offset=bass.IndirectOffsetOnAxis(ap=index[:, s, c:c + 1], axis=0),
                        in_=record[:, s, c, :], in_offset=None).then_inc(scattered[s], 16)

            in_steps(pool, steps, [(0, scatter)], 2)

        @block.sync
        def _(sp):
            view = table.rearrange("(p t) w -> p (t w)", p=SLOTS)
            sp.wait_ge(cleared, 1)
            sp.dma_start(view, clear[:, :]).then_inc(zeros_out, 16)
            for s in range(2):
                sp.wait_ge(scattered[s], 16 * CHUNK * steps // 2)
            sp.dma_start(clear[:, :], view).then_inc(table_in, 16)
            sp.wait_ge(table_in, 16)


def one_hots(dve, m, onehot, place):
    return dve.tensor_tensor(
        onehot, m.ramp[:, 1:1 + LANES].unsqueeze(1).to_broadcast([SLOTS, GROUP, LANES]),
        place.to_broadcast([SLOTS, GROUP, LANES]), ALU.is_equal)


def gathers(pool, table, rows, index, gathered):
    for j in range(GROUP):
        pool.indirect_dma_start(out=rows[:, j, :], out_offset=None, in_=table,
                                in_offset=bass.IndirectOffsetOnAxis(ap=index[:, j:j + 1], axis=0))\
            .then_inc(gathered, 16)


def index_stage(act, m, index, source, gathered, ready):
    def stage(k, s, used):
        if not is_new(used):
            act.wait_ge(gathered[s], used * (16 * GROUP))
            act.nop(nofuse=True)
        act.copy(index[:, s, :], source[:, ds(k * GROUP, GROUP)]).then_inc(ready, 1)
    return stage


def gather_stage(pool, table, rows, index, gathered, index_ready, rows_used):
    def stage(k, s, used):
        pool.wait_ge(index_ready, made(k))
        pool.nop(nofuse=True)
        pool.wait_ge(rows_used, free(k))
        pool.nop(nofuse=True)
        gathers(pool, table, rows[:, s], index[:, s], gathered[s])
    return stage


def match_stage(dve, m, onehot, places, ready, used_by):
    def stage(k, s, used):
        dve.wait_ge(used_by, free(k))
        dve.nop(nofuse=True)
        one_hots(dve, m, onehot[:, s], places[:, ds(k * GROUP, GROUP), 1:2]).then_inc(ready, 1)
    return stage


def add_stage(dve, m, blocks, width, sums_of_tile, summed, added):
    def stage(k, s, used):
        for j in range(GROUP):
            b = dve.value_load(blocks[0:1, ds(k * GROUP + j, 1)], min_val=0, max_val=BLOCKS - 1)
            if j == 0:
                dve.wait_ge(summed, made(k))
                dve.nop(nofuse=True)
            dve.wait_ge(added, k * GROUP + (j + CREDIT * GROUP))
            dve.tensor_tensor(m.acc[:, ds(b, 1), 0:width], m.acc[:, ds(b, 1), 0:width], sums_of_tile(s % 2, j),
                              ALU.add).then_inc(added, 1)
    return stage


def sum_neighbours(nc, m, table):
    with Phase(nc, "gin") as ph:
        gathered = software_dma_sems(nc, m, ph, RING)
        index_ready, onehot_ready, summed, added, cleared = (
            ph.sem(x) for x in ("index_ready", "onehot_ready", "summed", "added", "cleared"))
        index = ph.sbuf("index", [SLOTS, RING, GROUP], I32)
        rows = ph.sbuf("rows", [SLOTS, RING, GROUP, D])
        onehot = ph.sbuf("onehot", [SLOTS, RING, GROUP, LANES])
        sums = ph.psum("sums", [128, 2, GROUP * D])
        block = ph.block()

        @block.scalar
        def _(act):
            act.sem_inc(index_ready, CREDIT)
            in_steps(act, GROUPS, [(0, index_stage(act, m, index, m.sender, gathered, index_ready))])

        @block.gpsimd
        def _(pool):
            in_steps(pool, GROUPS, [(0, gather_stage(pool, table, rows, index, gathered, index_ready, summed))])

        @block.tensor
        def _(pe):
            pe.sem_inc(summed, CREDIT)

            def sum_tiles(k, s, used):
                pe.wait_ge(gathered[s], used * (16 * GROUP) + 16 * GROUP)
                pe.wait_ge(onehot_ready, made(k))
                pe.wait_ge(added, free(k, 2) * GROUP)
                for j in range(GROUP):
                    last = pe.matmul(sums[0:LANES, s % 2, j * D:(j + 1) * D], onehot[:, s, j, :], rows[:, s, j, :],
                                     start=True, stop=True)
                last.then_inc(summed, 1)

            in_steps(pe, GROUPS, [(0, sum_tiles)])

        @block.vector
        def _(dve):
            dve.memset(m.acc[:, :, 0:D], 0.0).then_inc(cleared, 1)
            dve.wait_ge(cleared, 1)
            dve.sem_inc(added, CREDIT * GROUP)
            dve.sem_inc(onehot_ready, CREDIT)
            in_steps(dve, GROUPS, [
                (0, match_stage(dve, m, onehot, m.record, onehot_ready, summed)),
                (1, add_stage(dve, m, m.receiver_block, D,
                              lambda p, j: sums[0:LANES, p, j * D:(j + 1) * D], summed, added)),
            ])


def per_node(vector):
    return vector.unsqueeze(2).to_broadcast([LANES, BLOCKS, D])


def per_column(row):
    return row.unsqueeze(1).to_broadcast([LANES, BLOCKS, D])


class Norms:

    def __init__(self, ph, epsilons):
        self.epsilons = epsilons
        self.var_ready, self.root_ready = ph.sem("var_ready"), ph.sem("root_ready")
        self.square = ph.sbuf("norm_square", [LANES, BLOCKS, D])
        self.total = ph.sbuf("norm_total", [LANES, BLOCKS])
        self.var = ph.sbuf("norm_var", [LANES, BLOCKS])
        self.root = ph.sbuf("norm_root", [LANES, BLOCKS])
        self.inverse = ph.sbuf("norm_inverse", [LANES, BLOCKS])
        self.done = 0

    def roots(self, act):
        for n in range(len(self.epsilons)):
            act.wait_ge(self.var_ready, n + 1)
            act.activation(self.root[:, :], self.var[:, :], ACT.Sqrt).then_inc(self.root_ready, 1)

    def normalize(self, dve, chain, t):
        chain(dve.tensor_reduce(self.total[:, :], t, AX.X, ALU.add))
        chain(dve.tensor_scalar(self.total[:, :], self.total[:, :], 1.0 / D, None, ALU.mult))
        chain(dve.tensor_tensor(t, t, per_node(self.total[:, :]), ALU.subtract))
        chain(dve.tensor_tensor(self.square[:, :, :], t, t, ALU.mult))
        chain(dve.tensor_reduce(self.total[:, :], self.square[:, :, :], AX.X, ALU.add))
        chain(dve.tensor_scalar(self.var[:, :], self.total[:, :], 1.0 / D, self.epsilons[self.done], ALU.mult, ALU.add))
        self.done += 1
        dve.sem_inc(self.var_ready, 1)
        dve.wait_ge(self.root_ready, self.done)
        chain(dve.reciprocal(self.inverse[:, :], self.root[:, :]))
        chain(dve.tensor_tensor(t, t, per_node(self.inverse[:, :]), ALU.mult))


def gin_nodes(nc, m, x, eps, w1, b1, w2, b2, gamma, beta):
    with Phase(nc, "gin_nodes") as ph:
        loaded, step = ph.sem("loaded"), ph.sem("step")
        ready, z_copied, z_turned, zt_ready, h_summed, h_ready, o_summed, o_added = (
            ph.sem(n) for n in ("ready", "z_copied", "z_turned", "zt_ready", "h_summed", "h_ready", "o_summed",
                                "o_added"))
        w1_t, w2_t = ph.sbuf("w1", [D, D]), ph.sbuf("w2", [D, D])
        b1_t = ph.sbuf("b1", [D, 1])
        b2_t, gamma_t, beta_t = (ph.sbuf(n, [LANES, D]) for n in ("b2", "gamma", "beta"))
        eps_t = ph.sbuf("eps", [LANES, 1])
        r = ph.sbuf("r", [LANES, BLOCKS, D])
        z = ph.sbuf("z", [LANES, 2, D])
        zt = ph.sbuf("zt", [D, 2, LANES])
        h = ph.sbuf("h", [D, 2, LANES])
        turned, hidden, outs = (ph.psum(n, [128, 2, 512]) for n in ("turned", "hidden", "outs"))
        norms = Norms(ph, [1e-5, 1e-5])
        block = ph.block()

        @block.sync
        def _(sp):
            for tile, source in ((m.x[:, :, :], x.rearrange("(b p) f -> p b f", p=LANES)), (w1_t[:, :], w1),
                                 (w2_t[:, :], w2), (b1_t[:, :], b1.rearrange("(n a) -> n a", a=1)),
                                 (b2_t[:, :], row_of(b2, LANES)), (gamma_t[:, :], row_of(gamma, LANES)),
                                 (beta_t[:, :], row_of(beta, LANES)), (eps_t[:, :], row_of(eps, LANES))):
                sp.dma_start(tile, source).then_inc(loaded, 16)

        @block.vector
        def _(dve):
            chain = Chain(dve, step)
            for s in (z_copied, o_added):
                dve.sem_inc(s, CREDIT)
            dve.wait_ge(loaded, 128)
            chain(dve.tensor_scalar(eps_t[:, :], eps_t[:, :], 1.0, None, ALU.add))
            chain(dve.scalar_tensor_tensor(m.acc[:, :, 0:D], m.x[:, :, :], eps_t[:, :], m.acc[:, :, 0:D], ALU.mult,
                                           ALU.add))
            chain(dve.tensor_tensor(r[:, :, :], m.x[:, :, :], per_column(b2_t[:, :]), ALU.add))

            def copy_z(b, s, used):
                dve.wait_ge(z_turned, free(b, 2))
                dve.nop(nofuse=True)
                dve.tensor_copy(z[:, s, :], m.acc[:, ds(b, 1), 0:D]).then_inc(z_copied, 1)

            def add_out(b, s, used):
                dve.wait_ge(o_summed, made(b))
                dve.nop(nofuse=True)
                dve.tensor_tensor(r[:, ds(b, 1), :], r[:, ds(b, 1), :], outs[0:LANES, s, 0:D], ALU.add)\
                    .then_inc(o_added, 1)

            in_steps(dve, BLOCKS, [(0, copy_z), (1, add_out)], 2)
            dve.wait_ge(o_added, made(BLOCKS - 1))
            norms.normalize(dve, chain, r[:, :, :])
            chain(dve.tensor_tensor(r[:, :, :], r[:, :, :], per_column(gamma_t[:, :]), ALU.mult))
            chain(dve.tensor_tensor(r[:, :, :], r[:, :, :], per_column(beta_t[:, :]), ALU.add))
            chain(dve.scalar_tensor_tensor(m.x[:, :, :], r[:, :, :], 0.0, m.x[:, :, :], ALU.max, ALU.add))
            norms.normalize(dve, chain, m.x[:, :, :])

        @block.tensor
        def _(pe):
            for s in (z_turned, h_summed, o_summed):
                pe.sem_inc(s, CREDIT)
            pe.wait_ge(loaded, 128)

            def turn(b, s, used):
                pe.wait_ge(z_copied, made(b))
                pe.wait_ge(zt_ready, free(b, 2))
                pe.transpose(turned[:, s, 0:LANES], z[:, s, :], m.ident[0:LANES, 0:LANES]).then_inc(z_turned, 1)

            def first(b, s, used):
                pe.wait_ge(zt_ready, made(b))
                pe.wait_ge(h_ready, free(b, 2))
                pe.matmul(hidden[:, s, 0:LANES], w1_t[:, :], zt[:, s, :], start=True, stop=True).then_inc(h_summed, 1)

            def second(b, s, used):
                pe.wait_ge(h_ready, made(b))
                pe.wait_ge(o_added, free(b, 2))
                pe.matmul(outs[0:LANES, s, 0:D], h[:, s, :], w2_t[:, :], start=True, stop=True).then_inc(o_summed, 1)

            in_steps(pe, BLOCKS, [(0, turn), (0, first), (0, second)], 2)

        @block.scalar
        def _(act):
            for s in (zt_ready, h_ready):
                act.sem_inc(s, CREDIT)
            act.wait_ge(loaded, 128)

            def copy_zt(b, s, used):
                act.wait_ge(z_turned, made(b))
                act.wait_ge(h_summed, free(b, 2))
                act.copy(zt[:, s, :], turned[:, s, 0:LANES]).then_inc(zt_ready, 1)

            def relu(b, s, used):
                act.wait_ge(h_summed, made(b))
                act.wait_ge(o_summed, free(b, 2))
                act.activation(h[:, s, :], hidden[:, s, 0:LANES], ACT.Relu, bias=b1_t[:, :]).then_inc(h_ready, 1)

            in_steps(act, BLOCKS, [(0, copy_zt), (0, relu)], 2)
            norms.roots(act)


def projections(ph, name, src, weights, width, out_banks, evacuate, evacuator):
    chunks = len(weights)
    pieces = -(-width // 512)
    copied, turned_done, xt_ready, multiplied, taken = (
        ph.sem(f"{name}_{n}") for n in ("copied", "turned", "xt_ready", "multiplied", "taken"))
    x = ph.sbuf(f"{name}_x", [LANES, 2, chunks, D])
    xt = ph.sbuf(f"{name}_xt", [D, 2, chunks, LANES])
    turned = ph.psum(f"{name}_turned_banks", [128, 2, 512])
    outs = ph.psum(f"{name}_outs", [128, out_banks, pieces, 512])

    def dve(e, m):
        e.sem_inc(copied, CREDIT)
        if evacuator == "dve":
            e.sem_inc(taken, CREDIT)

        def copy(b, s, used):
            e.wait_ge(turned_done, free(b, 2))
            e.nop(nofuse=True)
            e.tensor_copy(x[:, s, :, :].rearrange("p c f -> p (c f)"), src[:, ds(b, 1), 0:chunks * D])\
                .then_inc(copied, 1)

        def take(b, s, used):
            e.wait_ge(multiplied, made(b))
            e.nop(nofuse=True)
            evacuate(b, s, outs[0:LANES, s % out_banks]).then_inc(taken, 1)

        in_steps(e, BLOCKS, [(0, copy)] + [(1, take)] * (evacuator == "dve"), 2)
        if evacuator == "dve":
            e.wait_ge(taken, made(BLOCKS - 1))

    def act(e, m):
        e.sem_inc(xt_ready, CREDIT)
        if evacuator == "act":
            e.sem_inc(taken, CREDIT)

        def copy_xt(b, s, used):
            e.wait_ge(turned_done, made(b))
            e.wait_ge(multiplied, free(b, 2))
            e.copy(xt[:, s, :, :].rearrange("p c n -> p (c n)"), turned[:, s, 0:chunks * LANES]).then_inc(xt_ready, 1)

        def take(b, s, used):
            e.wait_ge(multiplied, made(b))
            e.nop(nofuse=True)
            evacuate(b, s, outs[0:LANES, s % out_banks]).then_inc(taken, 1)

        in_steps(e, BLOCKS, [(0, copy_xt)] + [(1, take)] * (evacuator == "act"), 2)

    def pe(e, m):
        e.sem_inc(turned_done, CREDIT)
        e.sem_inc(multiplied, CREDIT)

        def turn(b, s, used):
            e.wait_ge(copied, made(b))
            e.wait_ge(xt_ready, free(b, 2))
            for c in range(chunks):
                last = e.transpose(turned[:, s, c * LANES:(c + 1) * LANES], x[:, s, c, :], m.ident[0:LANES, 0:LANES])
            last.then_inc(turned_done, 1)

        def multiply(b, s, used):
            e.wait_ge(xt_ready, made(b))
            e.wait_ge(taken, free(b, out_banks))
            for piece in range(pieces):
                low, high = 512 * piece, min(512 * piece + 512, width)
                for c in range(chunks):
                    last = e.matmul(outs[0:LANES, s % out_banks, piece, 0:high - low], xt[:, s, c, :],
                                    weights[c][:, low:high], start=c == 0, stop=c == chunks - 1)
            last.then_inc(multiplied, 1)

        in_steps(e, BLOCKS, [(0, turn), (0, multiply)], 2)

    return dve, act, pe


SKIP = 5 * MUL


def equivariant_weights(nc, m, up_s, up_v, r1, r2, dn_s, dn_v, sk_s, sk_v, species):
    with Phase(nc, "equivariant_weights") as ph:
        zeroed, loaded, scaled = ph.sem("zeroed"), ph.sem("loaded"), ph.sem("scaled")
        species_int = ph.sbuf("species_int", [LANES, BLOCKS], I32)
        species_f = ph.sbuf("species_f", [LANES, BLOCKS])
        block = ph.block()
        copies = [(m.up_skip[0:MUL, 0:MUL], up_s),
                  (m.up_skip[0:MUL, D:].rearrange("m (z k) -> m z k", z=SPECIES)[:, :, 0:2 * MUL],
                   sk_s.rearrange("z m k -> m z k")),
                  (m.down[0:2 * MUL, 0, 0:2 * MUL], dn_s),
                  (m.down[2 * MUL:4 * MUL, 0, 2 * MUL:3 * MUL], dn_v),
                  (m.down[0:2 * MUL, 1, 3 * MUL:4 * MUL], dn_v),
                  (m.down[2 * MUL:4 * MUL, 1, 4 * MUL:5 * MUL], dn_v),
                  (species_int[:, :], species.rearrange("(b p) -> p b", p=LANES))]
        for i in range(3):
            rows = m.up_skip[MUL + i:D:3, :]
            copies.append((rows[:, MUL * (i + 1):MUL * (i + 2)], up_v))
            copies.append((rows[:, D:].rearrange("m (z k) -> m z k", z=SPECIES)
                           [:, :, MUL * (i + 2):MUL * (i + 3)], sk_v.rearrange("z m k -> m z k")))
        for j in range(GROUP):
            copies.append((m.radial1[RECORD * j + 8:RECORD * j + 8 + RADIAL, RADIAL * j:RADIAL * (j + 1)], r1))
            copies.append((m.radial2[RADIAL * j:RADIAL * (j + 1), D * j:D * (j + 1)], r2))

        @block.vector
        def _(dve):
            dve.memset(m.up_skip[:, :], 0.0).then_inc(zeroed, 1)
            dve.memset(m.down[:, :, :], 0.0).then_inc(zeroed, 1)
            dve.memset(m.radial1[:, :], 0.0).then_inc(zeroed, 1)
            dve.memset(m.radial2[:, :], 0.0).then_inc(zeroed, 1)
            dve.wait_ge(loaded, 16 * len(copies))
            w_st = m.radial2[:, :].rearrange("r (j f) -> r j f", j=GROUP)[:, :, 3 * MUL:4 * MUL]
            dve.tensor_scalar(w_st, w_st, 0.5773502691896258, None, ALU.mult).then_inc(scaled, 1)
            dve.tensor_copy(species_f[:, :], species_int[:, :]).then_inc(scaled, 1)
            dve.wait_ge(scaled, 2)
            for z in range(SPECIES):
                dve.tensor_scalar(m.is_species[:, :, z], species_f[:, :], float(z), None, ALU.is_equal)\
                    .then_inc(scaled, 1)
            dve.wait_ge(scaled, 2 + SPECIES)

        @block.sync
        def _(sp):
            sp.wait_ge(zeroed, 4)
            with nc.allow_non_contiguous_dma("the species of nodes, 12 KB, nodes of a block on partitions"):
                for tile, source in copies:
                    sp.dma_start(tile, source).then_inc(loaded, 16)


def equivariant_sources(nc, m, table):
    with Phase(nc, "equivariant_sources") as ph:
        stored, part = ph.sem("stored"), ph.sem("part")
        up = ph.sbuf("up", [LANES, BLOCKS, D])
        up_done, whole = ph.sem("up_done"), ph.sem("whole")
        block = ph.block()
        holder = {}

        def evacuate(b, s, outs):
            e = holder["dve"]
            e.tensor_scalar(up[:, ds(b, 1), :], outs[:, 0, 0:D], MUL ** -0.5, None, ALU.mult)
            for z in range(SPECIES):
                low = D + z * SKIP
                pieces = [(0, SKIP, low)] if low // 512 == (low + SKIP - 1) // 512 else [
                    (0, 512 - low % 512, low), (512 - low % 512, SKIP, low // 512 * 512 + 512)]
                for first, end, at in pieces:
                    values = outs[:, at // 512, at % 512:at % 512 + end - first]
                    target = m.skip[:, ds(b, 1), first:end]
                    if z == 0:
                        last = e.tensor_scalar(target, values, m.is_species[:, ds(b, 1), z], None, ALU.mult)
                    else:
                        last = e.scalar_tensor_tensor(target, values, m.is_species[:, ds(b, 1), z], target, ALU.mult,
                                                      ALU.add)
                if z < SPECIES - 1:
                    last.then_inc(part, 1)
                    e.wait_ge(part, b * (SPECIES - 1) + (z + 1))
                    e.nop(nofuse=True)
            return last

        dve_steps, act_steps, pe_steps = projections(ph, "up", m.x, [m.up_skip], D + SPECIES * SKIP, 2, evacuate,
                                                     "dve")

        @block.vector
        def _(dve):
            holder["dve"] = dve
            dve_steps(dve, m)
            dve.drain().then_inc(up_done, 1)

        @block.scalar
        def _(act):
            act_steps(act, m)

        @block.tensor
        def _(pe):
            pe_steps(pe, m)

        @block.sync
        def _(sp):
            sp.wait_ge(up_done, 1)
            sp.dma_start(table.rearrange("(b p) f -> p b f", p=LANES), up[:, :, :]).then_inc(stored, 16)
            sp.wait_ge(stored, 16)


def equivariant_messages(nc, m, table):
    with Phase(nc, "equivariant") as ph:
        gathered = software_dma_sems(nc, m, ph, RING)
        (index_ready, onehot_ready, record_ready, record_turned, turned_ready, hidden_summed, hidden_ready,
         weights_made, products, parts, messages_ready, summed, added, cleared) = (
            ph.sem(x) for x in ("index_ready", "onehot_ready", "record_ready", "record_turned", "turned_ready",
                                "hidden_summed", "hidden_ready", "weights_made", "products", "parts",
                                "messages_ready", "summed", "added", "cleared"))
        index = ph.sbuf("index", [SLOTS, RING, GROUP], I32)
        rows = ph.sbuf("rows", [SLOTS, RING, GROUP, D])
        onehot = ph.sbuf("onehot", [SLOTS, RING, GROUP, LANES])
        record = ph.sbuf("record", [SLOTS, RING, GROUP, RECORD])
        turned = ph.sbuf("turned", [GROUP * RECORD, 2, SLOTS])
        hidden = ph.sbuf("hidden", [GROUP * RADIAL, 2, SLOTS])
        scalar_vt = ph.sbuf("scalar_vt", [SLOTS, 2, GROUP, MUL])
        product = ph.sbuf("product", [SLOTS, 2, GROUP, 3, MUL])
        dot = ph.sbuf("dot", [SLOTS, 2, GROUP, MUL])
        message = ph.sbuf("message", [SLOTS, 2, GROUP, 2 * D])
        radial = ph.psum("radial", [128, 1, 512])
        hidden_sum = ph.psum("hidden_sum", [128, 1, 512])
        weight = ph.psum("weight", [128, 2, GROUP, D])
        sums = ph.psum("sums", [128, 2, GROUP, 2 * D])
        block = ph.block()

        @block.scalar
        def _(act):
            for s in (index_ready, record_ready, turned_ready, hidden_ready):
                act.sem_inc(s, CREDIT)

            def copy_record(k, s, used):
                act.wait_ge(products, free(k))
                act.nop(nofuse=True)
                act.copy(record[:, s, :, :], m.record[:, ds(k * GROUP, GROUP), :]).then_inc(record_ready, 1)

            def copy_turned(k, s, used):
                act.wait_ge(record_turned, made(k))
                act.wait_ge(hidden_summed, free(k, 2))
                act.copy(turned[:, s % 2, :], radial[0:GROUP * RECORD, 0, 0:SLOTS]).then_inc(turned_ready, 1)

            def silu(k, s, used):
                act.wait_ge(hidden_summed, made(k))
                act.wait_ge(weights_made, free(k, 2))
                act.activation(hidden[:, s % 2, :], hidden_sum[0:GROUP * RADIAL, 0, 0:SLOTS], ACT.Silu,
                               scale=RADIAL ** -0.5).then_inc(hidden_ready, 1)

            in_steps(act, GROUPS, [(0, index_stage(act, m, index, m.sender, gathered, index_ready)),
                                   (1, copy_record), (1, copy_turned), (1, silu)])

        @block.gpsimd
        def _(pool):
            in_steps(pool, GROUPS, [(0, gather_stage(pool, table, rows, index, gathered, index_ready, products))])

        @block.tensor
        def _(pe):
            for s in (record_turned, hidden_summed, weights_made, summed):
                pe.sem_inc(s, CREDIT)

            def turn_record(k, s, used):
                pe.wait_ge(record_ready, made(k))
                pe.wait_ge(turned_ready, free(k, 1))
                pe.nop(nofuse=True)
                pe.transpose(radial[0:GROUP * RECORD, 0, 0:SLOTS], record[:, s, :, :].rearrange("p j w -> p (j w)"),
                             m.ident[:, :]).then_inc(record_turned, 1)

            def hide(k, s, used):
                pe.wait_ge(turned_ready, made(k))
                pe.wait_ge(hidden_ready, free(k, 1))
                pe.nop(nofuse=True)
                pe.matmul(hidden_sum[0:GROUP * RADIAL, 0, 0:SLOTS], m.radial1[:, :], turned[:, s % 2, :],
                          start=True, stop=True).then_inc(hidden_summed, 1)

            def make_weights(k, s, used):
                pe.wait_ge(hidden_ready, made(k))
                pe.wait_ge(messages_ready, free(k, 2))
                pe.matmul(weight[:, s % 2, :, :].rearrange("p j f -> p (j f)"), hidden[:, s % 2, :], m.radial2[:, :],
                          start=True, stop=True).then_inc(weights_made, 1)

            def sum_tiles(k, s, used):
                pe.wait_ge(messages_ready, made(k))
                pe.wait_ge(onehot_ready, made(k))
                pe.wait_ge(added, free(k, 2) * GROUP)
                for j in range(GROUP):
                    last = pe.matmul(sums[0:LANES, s % 2, j, :], onehot[:, s, j, :], message[:, s % 2, j, :],
                                     start=True, stop=True)
                last.then_inc(summed, 1)

            in_steps(pe, GROUPS, [(1, turn_record), (1, hide), (1, make_weights), (3, sum_tiles)])

        @block.vector
        def _(dve):
            dve.memset(m.acc[:, :, :], 0.0).then_inc(cleared, 1)
            dve.wait_ge(cleared, 1)
            dve.sem_inc(added, CREDIT * GROUP)
            for s in (onehot_ready, products, messages_ready):
                dve.sem_inc(s, CREDIT)

            def messages(k, s, used):
                p = s % 2
                scalars = rows[:, s, :, 0:MUL]
                vectors = rows[:, s, :, MUL:D].rearrange("p j (i k) -> p j i k", i=3)
                y = record[:, s, :, 5:8].unsqueeze(3).to_broadcast([SLOTS, GROUP, 3, MUL])
                w_ss, w_vs, w_vt, w_st = (weight[:, p, :, MUL * n:MUL * (n + 1)] for n in range(4))
                halves = message[:, p, :, 2 * MUL:].rearrange("p j (i h k) -> p j i h k", i=3, h=2)
                dve.wait_ge(gathered[s], used * (16 * GROUP) + 16 * GROUP)
                dve.nop(nofuse=True)
                dve.wait_ge(summed, free(k, 2))
                dve.nop(nofuse=True)
                dve.wait_ge(weights_made, made(k))
                dve.nop(nofuse=True)
                dve.tensor_tensor(product[:, p, :, :, :], vectors, y, ALU.mult).then_inc(parts, 1)
                dve.tensor_tensor(scalar_vt[:, p, :, :], scalars, w_vt, ALU.mult).then_inc(parts, 1)
                dve.wait_ge(parts, k * 4 + 1)
                dve.nop(nofuse=True)
                dve.tensor_tensor(dot[:, p, :, :], product[:, p, :, 0, :], product[:, p, :, 1, :], ALU.add)\
                    .then_inc(parts, 1)
                dve.tensor_tensor(message[:, p, :, 0:MUL], scalars, w_ss, ALU.mult)
                dve.wait_ge(parts, k * 4 + 3)
                dve.nop(nofuse=True)
                dve.tensor_tensor(dot[:, p, :, :], dot[:, p, :, :], product[:, p, :, 2, :], ALU.add)\
                    .then_inc(parts, 1)
                dve.tensor_tensor(halves[:, :, :, 1, :], scalar_vt[:, p, :, :].unsqueeze(2).to_broadcast(
                    [SLOTS, GROUP, 3, MUL]), y, ALU.mult)
                dve.tensor_tensor(halves[:, :, :, 0, :], vectors, w_vs.unsqueeze(2).to_broadcast(
                    [SLOTS, GROUP, 3, MUL]), ALU.mult).then_inc(products, 1)
                dve.wait_ge(parts, k * 4 + 4)
                dve.nop(nofuse=True)
                dve.tensor_tensor(message[:, p, :, MUL:2 * MUL], dot[:, p, :, :], w_st, ALU.mult)\
                    .then_inc(messages_ready, 1)

            in_steps(dve, GROUPS, [
                (2, match_stage(dve, m, onehot, m.record, onehot_ready, summed)),
                (3, messages),
                (4, add_stage(dve, m, m.receiver_block, 2 * D, lambda p, j: sums[0:LANES, p, j, :], summed, added)),
            ])


def equivariant_nodes(nc, m):
    with Phase(nc, "equivariant_nodes") as ph:
        step = ph.sem("step")
        gates_asked, gates_ready = ph.sem("gates_asked"), ph.sem("gates_ready")
        g = ph.sbuf("g", [LANES, BLOCKS, SKIP])
        gated = ph.sbuf("gated", [LANES, BLOCKS, 2 * MUL])
        norms = Norms(ph, [1e-5])
        block = ph.block()
        holder = {}
        down_scale = 0.5 * RADIAL ** -0.5 * 16.0 ** -0.5 * (2 * MUL) ** -0.5

        def evacuate(b, s, outs):
            return holder["dve"].scalar_tensor_tensor(g[:, ds(b, 1), :], outs[:, 0, 0:SKIP], down_scale,
                                                      m.skip[:, ds(b, 1), :], ALU.mult, ALU.add)

        dve_steps, act_steps, pe_steps = projections(ph, "down", m.acc, [m.down[:, 0, :], m.down[:, 1, :]], SKIP, 2,
                                                     evacuate, "dve")

        @block.vector
        def _(dve):
            holder["dve"] = dve
            chain = Chain(dve, step)
            chain(dve.tensor_scalar(m.skip[:, :, :], m.skip[:, :, :], 0.5 * MUL ** -0.5, None, ALU.mult))
            dve_steps(dve, m)
            dve.sem_inc(gates_asked, 1)
            dve.wait_ge(gates_ready, 1)
            chain(dve.tensor_tensor(m.x[:, :, 0:MUL], m.x[:, :, 0:MUL], gated[:, :, 0:MUL], ALU.add))
            for i in range(3):
                vector = g[:, :, MUL * (i + 2):MUL * (i + 3)]
                chain(dve.tensor_tensor(vector, vector, gated[:, :, MUL:2 * MUL], ALU.mult))
                x_i = m.x[:, :, MUL:D].rearrange("p b (k i) -> p b k i", i=3)[:, :, :, i]
                chain(dve.tensor_tensor(x_i, x_i, vector, ALU.add))
            norms.normalize(dve, chain, m.x[:, :, :])

        @block.scalar
        def _(act):
            act_steps(act, m)
            act.wait_ge(gates_asked, 1)
            act.activation(gated[:, :, :], g[:, :, 0:2 * MUL], ACT.Silu).then_inc(gates_ready, 1)
            norms.roots(act)

        @block.tensor
        def _(pe):
            pe_steps(pe, m)


def attention_weights(nc, m, wq, bq, wk, bk, wv, bv):
    with Phase(nc, "attention_weights") as ph:
        loaded, turned, copied = ph.sem("loaded"), ph.sem("turned"), ph.sem("copied")
        raw = ph.sbuf("raw", [D, 3, D])
        bank = ph.psum("bank", [128, 512])
        block = ph.block()

        @block.sync
        def _(sp):
            for n, (w, b) in enumerate(((wq, bq), (wk, bk), (wv, bv))):
                sp.dma_start(raw[:, n, :], w).then_inc(loaded, 16)
                sp.dma_start(m.qkv_bias[:, n * D:(n + 1) * D], row_of(b, LANES)).then_inc(loaded, 16)

        @block.tensor
        def _(pe):
            pe.wait_ge(loaded, 96)
            for n in range(3):
                last = pe.transpose(bank[:, n * D:(n + 1) * D], raw[:, n, :], m.ident[:, :])
            last.then_inc(turned, 1)

        @block.vector
        def _(dve):
            dve.wait_ge(turned, 1)
            dve.tensor_copy(m.qkv[:, :], bank[:, 0:3 * D]).then_inc(copied, 1)
            dve.wait_ge(copied, 1)


def attention_sources(nc, m, table):
    with Phase(nc, "attention_sources") as ph:
        stored, kv_done = ph.sem("stored"), ph.sem("kv_done")
        kv = ph.sbuf("kv", [LANES, BLOCKS, 2 * D])
        block = ph.block()
        holder = {}

        def evacuate(b, s, outs):
            e = holder["dve"]
            e.tensor_tensor(m.query[:, ds(b, 1), :], outs[:, 0, 0:D], m.qkv_bias[:, 0:D], ALU.add)
            return e.tensor_tensor(kv[:, ds(b, 1), :], outs[:, 0, D:3 * D], m.qkv_bias[:, D:3 * D], ALU.add)

        dve_steps, act_steps, pe_steps = projections(ph, "qkv", m.x, [m.qkv], 3 * D, 2, evacuate, "dve")

        @block.vector
        def _(dve):
            holder["dve"] = dve
            dve_steps(dve, m)
            dve.drain().then_inc(kv_done, 1)

        @block.scalar
        def _(act):
            act_steps(act, m)

        @block.tensor
        def _(pe):
            pe_steps(pe, m)

        @block.sync
        def _(sp):
            sp.wait_ge(kv_done, 1)
            sp.dma_start(table.rearrange("(b p) f -> p b f", p=LANES), kv[:, :, :]).then_inc(stored, 16)
            sp.wait_ge(stored, 16)


def attention_messages(nc, m, table):
    wide = D + HEADS
    with Phase(nc, "attention") as ph:
        gathered = software_dma_sems(nc, m, ph, RING)
        (index_ready, onehot_ready, onehot_turned, turned_ready, queries_ready, parts, scores_ready, exp_ready,
         messages_ready, summed, added, cleared) = (
            ph.sem(x) for x in ("index_ready", "onehot_ready", "onehot_turned", "turned_ready", "queries_ready",
                                "parts", "scores_ready", "exp_ready", "messages_ready", "summed", "added", "cleared"))
        index = ph.sbuf("index", [SLOTS, RING, GROUP], I32)
        rows = ph.sbuf("rows", [SLOTS, RING, GROUP, 2 * D])
        onehot = ph.sbuf("onehot", [SLOTS, RING, GROUP, LANES])
        turned = ph.sbuf("turned", [LANES, RING, GROUP, SLOTS])
        product = ph.sbuf("product", [SLOTS, 2, GROUP, D])
        score = ph.sbuf("score", [SLOTS, 2, GROUP, HEADS])
        message = ph.sbuf("message", [SLOTS, RING, GROUP, wide])
        turned_bank = ph.psum("turned_bank", [128, GROUP, SLOTS])
        query_bank = ph.psum("query_bank", [128, 2, GROUP, D])
        sums = ph.psum("sums", [128, 2, GROUP // 2, 512])
        block = ph.block()

        @block.scalar
        def _(act):
            for s in (index_ready, turned_ready, exp_ready):
                act.sem_inc(s, CREDIT)

            def copy_turned(k, s, used):
                act.wait_ge(onehot_turned, made(k))
                act.wait_ge(queries_ready, free(k))
                act.copy(turned[:, s, :, :], turned_bank[0:LANES, :, :]).then_inc(turned_ready, 1)

            def exponentials(k, s, used):
                act.wait_ge(scores_ready, made(k))
                act.wait_ge(summed, free(k))
                act.activation(message[:, s, :, D:wide], score[:, s % 2, :, :], ACT.Exp).then_inc(exp_ready, 1)

            in_steps(act, GROUPS, [(0, index_stage(act, m, index, m.receiver, gathered, index_ready)),
                                   (1, copy_turned), (2, exponentials)])

        @block.gpsimd
        def _(pool):
            in_steps(pool, GROUPS, [(0, gather_stage(pool, table, rows, index, gathered, index_ready,
                                                     messages_ready))])

        @block.tensor
        def _(pe):
            for s in (onehot_turned, queries_ready, summed):
                pe.sem_inc(s, CREDIT)

            def turn(k, s, used):
                pe.wait_ge(onehot_ready, made(k))
                pe.wait_ge(turned_ready, free(k, 1))
                for j in range(GROUP):
                    last = pe.transpose(turned_bank[0:LANES, j, :], onehot[:, s, j, :], m.ident[:, :])
                last.then_inc(onehot_turned, 1)

            def queries(k, s, used):
                for j in range(GROUP):
                    b = pe.value_load(m.sender_block[0:1, ds(k * GROUP + j, 1)], min_val=0, max_val=BLOCKS - 1)
                    if j == 0:
                        pe.wait_ge(turned_ready, made(k))
                        pe.nop(nofuse=True)
                        pe.wait_ge(scores_ready, free(k, 2))
                        pe.nop(nofuse=True)
                    last = pe.matmul(query_bank[:, s % 2, j, :], turned[:, s, j, :], m.query[:, ds(b, 1), :],
                                     start=True, stop=True)
                last.then_inc(queries_ready, 1)

            def sum_tiles(k, s, used):
                pe.wait_ge(messages_ready, made(k))
                pe.wait_ge(added, free(k, 2) * GROUP)
                for j in range(GROUP):
                    last = pe.matmul(sums[0:LANES, s % 2, j // 2, j % 2 * wide:(j % 2 + 1) * wide],
                                     onehot[:, s, j, :], message[:, s, j, :], start=True, stop=True)
                last.then_inc(summed, 1)

            in_steps(pe, GROUPS, [(1, turn), (1, queries), (3, sum_tiles)])

        @block.vector
        def _(dve):
            dve.memset(m.acc[:, :, 0:wide], 0.0).then_inc(cleared, 1)
            dve.wait_ge(cleared, 1)
            dve.sem_inc(added, CREDIT * GROUP)
            for s in (onehot_ready, scores_ready, messages_ready):
                dve.sem_inc(s, CREDIT)

            def scores(k, s, used):
                p = s % 2
                dve.wait_ge(gathered[s], used * (16 * GROUP) + 16 * GROUP)
                dve.nop(nofuse=True)
                dve.wait_ge(queries_ready, made(k))
                dve.nop(nofuse=True)
                dve.wait_ge(exp_ready, free(k, 2))
                dve.nop(nofuse=True)
                dve.tensor_tensor(product[:, p, :, :], query_bank[:, p, :, :], rows[:, s, :, 0:D], ALU.mult)                    .then_inc(parts, 1)
                dve.wait_ge(parts, k * 3 + 1)
                dve.nop(nofuse=True)
                dve.tensor_reduce(score[:, p, :, :], product[:, p, :, :].rearrange("p j (h c) -> p j h c", h=HEADS),
                                  AX.X, ALU.add).then_inc(parts, 1)
                dve.wait_ge(parts, k * 3 + 2)
                dve.nop(nofuse=True)
                dve.tensor_scalar(score[:, p, :, :], score[:, p, :, :], HEAD ** -0.5, -10.0, ALU.mult, ALU.max)                    .then_inc(parts, 1)
                dve.wait_ge(parts, k * 3 + 3)
                dve.nop(nofuse=True)
                dve.tensor_scalar(score[:, p, :, :], score[:, p, :, :], 10.0, None, ALU.min).then_inc(scores_ready, 1)

            def messages(k, s, used):
                dve.wait_ge(exp_ready, made(k))
                dve.nop(nofuse=True)
                dve.tensor_tensor(message[:, s, :, 0:D].rearrange("p j (h c) -> p j h c", h=HEADS),
                                  rows[:, s, :, D:2 * D].rearrange("p j (h c) -> p j h c", h=HEADS),
                                  message[:, s, :, D:wide].unsqueeze(3).to_broadcast([SLOTS, GROUP, HEADS, HEAD]),
                                  ALU.mult).then_inc(messages_ready, 1)

            in_steps(dve, GROUPS, [
                (1, match_stage(dve, m, onehot, m.sender_place, onehot_ready, summed)),
                (2, scores), (3, messages),
                (4, add_stage(dve, m, m.sender_block, wide,
                              lambda p, j: sums[0:LANES, p, j // 2, j % 2 * wide:(j % 2 + 1) * wide], summed, added)),
            ])


def attention_nodes(nc, m, gamma, beta):
    with Phase(nc, "attention_nodes") as ph:
        loaded, step = ph.sem("loaded"), ph.sem("step")
        gamma_t, beta_t = (ph.sbuf(n, [LANES, D]) for n in ("gamma", "beta"))
        r = ph.sbuf("r", [LANES, BLOCKS, D])
        norms = Norms(ph, [1e-6, 1e-5])
        block = ph.block()

        @block.sync
        def _(sp):
            sp.dma_start(gamma_t[:, :], row_of(gamma, LANES)).then_inc(loaded, 16)
            sp.dma_start(beta_t[:, :], row_of(beta, LANES)).then_inc(loaded, 16)

        @block.vector
        def _(dve):
            chain = Chain(dve, step)
            sums = m.acc[:, :, D:D + HEADS]
            chain(dve.tensor_scalar(sums, sums, 1e-8, None, ALU.add))
            chain(dve.reciprocal(sums, sums))
            for h in range(HEADS):
                at = slice(h * HEAD, (h + 1) * HEAD)
                chain(dve.tensor_tensor(r[:, :, at], m.acc[:, :, at],
                                        m.acc[:, :, D + h:D + h + 1].to_broadcast([LANES, BLOCKS, HEAD]), ALU.mult))
            chain(dve.tensor_tensor(r[:, :, :], r[:, :, :], m.x[:, :, :], ALU.add))
            norms.normalize(dve, chain, r[:, :, :])
            dve.wait_ge(loaded, 32)
            chain(dve.tensor_tensor(r[:, :, :], r[:, :, :], per_column(gamma_t[:, :]), ALU.mult))
            chain(dve.tensor_tensor(r[:, :, :], r[:, :, :], per_column(beta_t[:, :]), ALU.add))
            chain(dve.tensor_tensor(m.x[:, :, :], m.x[:, :, :], r[:, :, :], ALU.add))
            norms.normalize(dve, chain, m.x[:, :, :])

        @block.scalar
        def _(act):
            norms.roots(act)


WIDE = D + 2


def edge_logits(nc, m, layers):
    with Phase(nc, "edge_logits") as ph:
        loaded, step, spread, asked = (ph.sem(n) for n in ("loaded", "step", "spread", "asked"))
        we_t = ph.sbuf("we", [3, 3, D])
        ae_t = ph.sbuf("ae", [3, 3, D])
        factor = ph.sbuf("factor", [3, 3])
        diagonal = ph.sbuf("diagonal", [3, 3, 3])
        factors = ph.sbuf("factors", [128, 9])
        total = ph.sbuf("total", [SLOTS, 3])
        bank = ph.psum("bank", [128, 2, 512])
        block = ph.block()

        @block.sync
        def _(sp):
            for n, (we, ae) in enumerate(layers):
                sp.dma_start(we_t[:, n, :], we).then_inc(loaded, 16)
                sp.dma_start(ae_t[:, n, :], row_of(ae, 3)).then_inc(loaded, 16)

        @block.vector
        def _(dve):
            chain = Chain(dve, step)
            dve.wait_ge(loaded, 96)
            chain(dve.tensor_tensor(we_t[:, :, :], we_t[:, :, :], ae_t[:, :, :], ALU.mult))
            chain(dve.tensor_reduce(factor[:, :], we_t[:, :, :], AX.X, ALU.add))
            for n in range(3):
                chain(dve.tensor_scalar(diagonal[:, n, :], m.ident[0:3, 0:3], factor[:, n:n + 1], None, ALU.mult))
            dve.sem_inc(asked, 1)
            dve.wait_ge(spread, 1)
            chain(dve.tensor_copy(factors[:, :], bank[:, 0, 0:9]))
            for n in range(3):
                chain(dve.tensor_scalar(m.edge_logit[:, n, :], m.record[:, :, 2], factors[:, 3 * n:3 * n + 1], None,
                                        ALU.mult))
                for a in (1, 2):
                    chain(dve.scalar_tensor_tensor(m.edge_logit[:, n, :], m.record[:, :, 2 + a],
                                                   factors[:, 3 * n + a:3 * n + a + 1], m.edge_logit[:, n, :],
                                                   ALU.mult, ALU.add))
            chain(dve.tensor_reduce(total[:, :], m.edge_logit[:, :, :], AX.X, ALU.add))
            dve.sem_inc(asked, 1)
            dve.wait_ge(spread, 2)
            chain(dve.tensor_scalar(m.mean_logit[:, :], bank[0:LANES, 1, 0:3], 1.0 / EDGES, None, ALU.mult))

        @block.tensor
        def _(pe):
            pe.wait_ge(asked, 1)
            pe.matmul(bank[:, 0, 0:9], m.ones[0:3, :], diagonal[:, :, :].rearrange("p n a -> p (n a)"), start=True,
                      stop=True).then_inc(spread, 1)
            pe.wait_ge(asked, 2)
            pe.matmul(bank[0:LANES, 1, 0:3], m.ones[:, 0:LANES], total[:, :], start=True, stop=True)\
                .then_inc(spread, 1)


def gat_sources(nc, m, source, w, a_src, a_dst, table):
    with Phase(nc, f"gat{m.layer}_sources") as ph:
        stored, loaded, step, h_done = ph.sem("stored"), ph.sem("loaded"), ph.sem("step"), ph.sem("h_done")
        w_t = ph.sbuf("w", [D, D])
        a_src_t, a_dst_t = ph.sbuf("a_src", [LANES, D]), ph.sbuf("a_dst", [LANES, D])
        product = ph.sbuf("product", [LANES, BLOCKS, D])
        block = ph.block()
        holder = {}

        def evacuate(b, s, outs):
            return holder["dve"].tensor_copy(m.h[:, ds(b, 1), 0:D], outs[:, 0, 0:D])

        dve_steps, act_steps, pe_steps = projections(ph, "h", source, [w_t], D, 2, evacuate, "dve")

        @block.vector
        def _(dve):
            holder["dve"] = dve
            chain = Chain(dve, step)
            dve_steps(dve, m)
            dve.wait_ge(loaded, 48)
            for a, target in ((a_src_t, m.h[:, :, D]), (a_dst_t, m.al_d[:, :])):
                chain(dve.tensor_tensor(product[:, :, :], m.h[:, :, 0:D], per_column(a[:, :]), ALU.mult))
                chain(dve.tensor_reduce(target, product[:, :, :], AX.X, ALU.add))
            dve.sem_inc(h_done, 1)

        @block.scalar
        def _(act):
            act_steps(act, m)

        @block.tensor
        def _(pe):
            pe.wait_ge(loaded, 48)
            pe_steps(pe, m)

        @block.sync
        def _(sp):
            sp.dma_start(w_t[:, :], w).then_inc(loaded, 16)
            sp.dma_start(a_src_t[:, :], row_of(a_src, LANES)).then_inc(loaded, 16)
            sp.dma_start(a_dst_t[:, :], row_of(a_dst, LANES)).then_inc(loaded, 16)
            sp.wait_ge(h_done, 1)
            sp.dma_start(table.rearrange("(b p) f -> p b f", p=LANES), m.h[:, :, :]).then_inc(stored, 16)
            sp.wait_ge(stored, 16)


def gat_messages(nc, m, table):
    with Phase(nc, f"gat{m.layer}") as ph:
        gathered = software_dma_sems(nc, m, ph, RING)
        (index_ready, onehot_ready, onehot_turned, turned_ready, al_d_ready, parts, alpha_ready, far_ready,
         masked_ready, masked_turned, tops_found, top_ready, drops, drop_ready, scale_ready, top_spread, shifts,
         shift_ready, exp_ready, weighted, summed, chained, added, stored, cleared) = (
            ph.sem(x) for x in (
                "index_ready", "onehot_ready", "onehot_turned", "turned_ready", "al_d_ready", "parts", "alpha_ready",
                "far_ready", "masked_ready", "masked_turned", "tops_found", "top_ready", "drops", "drop_ready",
                "scale_ready", "top_spread", "shifts", "shift_ready", "exp_ready", "weighted", "summed", "chained",
                "added", "stored", "cleared"))
        index = ph.sbuf("index", [SLOTS, RING, GROUP], I32)
        rows = ph.sbuf("rows", [SLOTS, RING, GROUP, D + 1])
        onehot = ph.sbuf("onehot", [SLOTS, RING, GROUP, LANES])
        turned = ph.sbuf("turned", [LANES, RING, GROUP, SLOTS])
        far = ph.sbuf("far", [SLOTS, 2, GROUP, LANES])
        masked = ph.sbuf("masked", [SLOTS, 2, GROUP, LANES])
        logit = ph.sbuf("logit", [SLOTS, RING, GROUP])
        alpha = ph.sbuf("alpha", [SLOTS, RING, GROUP])
        top = ph.sbuf("top", [LANES, RING, GROUP])
        drop = ph.sbuf("drop", [LANES, RING, GROUP])
        scale = ph.sbuf("scale", [LANES, RING, GROUP])
        shift = ph.sbuf("shift", [SLOTS, RING, GROUP])
        run = ph.sbuf("run", [LANES, RING, GROUP, WIDE])
        turned_bank, masked_bank = ph.psum("turned_bank", [128, GROUP, SLOTS]), ph.psum("masked_bank", [128, GROUP, SLOTS])
        al_d_bank, top_bank = ph.psum("al_d_bank", [128, 512]), ph.psum("top_bank", [128, 512])
        exp_bank = ph.psum("exp_bank", [128, 2, 512])
        sums = ph.psum("sums", [128, 2, GROUP, D])
        block = ph.block()

        def before(s, j):
            return (s, j - 1) if j else ((s - 1) % RING, GROUP - 1)

        @block.scalar
        def _(act):
            act.sem_inc(stored, CREDIT * GROUP)
            for s in (index_ready, turned_ready, far_ready, scale_ready, exp_ready):
                act.sem_inc(s, CREDIT)

            def copy_turned(k, s, used):
                act.wait_ge(onehot_turned, made(k))
                act.wait_ge(top_spread, free(k))
                act.copy(turned[:, s, :, :], turned_bank[0:LANES, :, :]).then_inc(turned_ready, 1)
                act.wait_ge(masked_ready, free(k, 2))
                act.activation(far[:, s % 2, :, :], onehot[:, s, :, :], ACT.Copy, bias=FAR, scale=-FAR)\
                    .then_inc(far_ready, 1)

            def scales(k, s, used):
                act.wait_ge(drop_ready, made(k))
                act.wait_ge(added, free(k) * GROUP)
                act.activation(scale[:, s, :], drop[:, s, :], ACT.Exp).then_inc(scale_ready, 1)

            def exponentials(k, s, used):
                act.wait_ge(shift_ready, made(k))
                act.activation(shift[:, s, :], shift[:, s, :], ACT.Exp).then_inc(exp_ready, 1)

            def store(k, s, used):
                for j in range(GROUP):
                    b = act.value_load(m.receiver_block[0:1, ds(k * GROUP + j, 1)], min_val=0, max_val=BLOCKS - 1)
                    if j == 0:
                        act.wait_ge(added, made(k) * GROUP)
                        act.nop(nofuse=True)
                        act.wait_ge(cleared, 3)
                        act.nop(nofuse=True)
                    act.wait_ge(stored, k * GROUP + (j + CREDIT * GROUP))
                    act.nop(nofuse=True)
                    act.copy(m.acc[:, ds(b, 1), 0:WIDE], run[:, s, j, :]).then_inc(stored, 1)

            in_steps(act, GROUPS, [(0, index_stage(act, m, index, m.sender, gathered, index_ready)),
                                   (2, copy_turned), (4, scales), (5, exponentials), (7, store)])

        @block.gpsimd
        def _(pool):
            in_steps(pool, GROUPS, [(0, gather_stage(pool, table, rows, index, gathered, index_ready, summed))])

        @block.tensor
        def _(pe):
            for s in (onehot_turned, al_d_ready, masked_turned, top_spread, summed):
                pe.sem_inc(s, CREDIT)

            def turn(k, s, used):
                pe.wait_ge(onehot_ready, made(k))
                pe.wait_ge(turned_ready, free(k, 1))
                for j in range(GROUP):
                    last = pe.transpose(turned_bank[0:LANES, j, :], onehot[:, s, j, :], m.ident[:, :])
                last.then_inc(onehot_turned, 1)

            def spread_al_d(k, s, used):
                for j in range(GROUP):
                    b = pe.value_load(m.receiver_block[0:1, ds(k * GROUP + j, 1)], min_val=0, max_val=BLOCKS - 1)
                    if j == 0:
                        pe.wait_ge(turned_ready, made(k))
                        pe.nop(nofuse=True)
                        pe.wait_ge(alpha_ready, free(k, 1))
                        pe.nop(nofuse=True)
                    last = pe.matmul(al_d_bank[:, j:j + 1], turned[:, s, j, :], m.al_d[:, ds(b, 1)], start=True,
                                     stop=True)
                last.then_inc(al_d_ready, 1)

            def turn_masked(k, s, used):
                pe.wait_ge(masked_ready, made(k))
                pe.wait_ge(tops_found, free(k, 1))
                for j in range(GROUP):
                    last = pe.transpose(masked_bank[0:LANES, j, :], masked[:, s % 2, j, :], m.ident[:, :])
                last.then_inc(masked_turned, 1)

            def spread_top(k, s, used):
                pe.wait_ge(top_ready, made(k))
                pe.wait_ge(shift_ready, free(k, 1))
                for j in range(GROUP):
                    last = pe.matmul(top_bank[:, j:j + 1], turned[:, s, j, :], run[:, s, j, D + 1:D + 2], start=True,
                                     stop=True)
                last.then_inc(top_spread, 1)

            def sum_tiles(k, s, used):
                pe.wait_ge(weighted, made(k))
                pe.wait_ge(added, free(k, 2) * GROUP)
                for j in range(GROUP):
                    pe.matmul(sums[0:LANES, s % 2, j, :], onehot[:, s, j, :], rows[:, s, j, 0:D], start=True,
                              stop=True)
                    last = pe.matmul(exp_bank[0:LANES, s % 2, j:j + 1], onehot[:, s, j, :], m.ones[:, 0:1],
                                     start=True, stop=True)
                last.then_inc(summed, 1)

            in_steps(pe, GROUPS, [(2, turn), (2, spread_al_d), (3, turn_masked), (4, spread_top), (5, sum_tiles)])

        @block.vector
        def _(dve):
            dve.memset(m.acc[:, :, 0:D + 1], 0.0).then_inc(cleared, 1)
            dve.memset(m.acc[:, :, D + 1:WIDE], FAR).then_inc(cleared, 1)
            dve.memset(run[:, RING - 1, GROUP - 1, 0:D + 1], 0.0).then_inc(cleared, 1)
            dve.memset(run[:, RING - 1, GROUP - 1, D + 1:WIDE], FAR).then_inc(cleared, 1)
            dve.wait_ge(cleared, 4)
            dve.sem_inc(added, CREDIT * GROUP)
            for s in (onehot_ready, alpha_ready, masked_ready, tops_found, top_ready, drop_ready, shift_ready,
                      weighted):
                dve.sem_inc(s, CREDIT)

            def alphas(k, s, used):
                dve.wait_ge(gathered[s], used * (16 * GROUP) + 16 * GROUP)
                dve.nop(nofuse=True)
                dve.tensor_tensor(logit[:, s, :], rows[:, s, :, D], m.edge_logit[:, m.layer, ds(k * GROUP, GROUP)],
                                  ALU.add).then_inc(parts, 1)
                dve.wait_ge(parts, k * 2 + 1)
                dve.nop(nofuse=True)
                dve.wait_ge(al_d_ready, made(k))
                dve.nop(nofuse=True)
                dve.tensor_tensor(logit[:, s, :], logit[:, s, :], al_d_bank[:, 0:GROUP], ALU.add).then_inc(parts, 1)
                dve.wait_ge(parts, k * 2 + 2)
                dve.nop(nofuse=True)
                dve.scalar_tensor_tensor(alpha[:, s, :], logit[:, s, :], 0.2, logit[:, s, :], ALU.mult, ALU.max)\
                    .then_inc(alpha_ready, 1)

            def mask(k, s, used):
                dve.wait_ge(far_ready, made(k))
                dve.nop(nofuse=True)
                dve.wait_ge(masked_turned, free(k, 2))
                dve.nop(nofuse=True)
                dve.wait_ge(alpha_ready, made(k))
                dve.nop(nofuse=True)
                dve.tensor_tensor(masked[:, s % 2, :, :], far[:, s % 2, :, :],
                                  alpha[:, s, :].unsqueeze(2).to_broadcast([SLOTS, GROUP, LANES]), ALU.add)\
                    .then_inc(masked_ready, 1)

            def tops(k, s, used):
                s0, j0 = before(s, 0)
                dve.wait_ge(masked_turned, made(k))
                dve.nop(nofuse=True)
                dve.tensor_reduce(top[:, s, :], masked_bank[0:LANES, :, :], AX.X, ALU.max).then_inc(tops_found, 1)
                dve.wait_ge(stored, free(k) * GROUP)
                dve.nop(nofuse=True)
                dve.wait_ge(tops_found, made(k))
                dve.nop(nofuse=True)
                dve.tensor_tensor_scan(run[:, s, :, D + 1], m.reset[0:LANES, ds(k * GROUP, GROUP)], top[:, s, :],
                                       run[:, s0, j0, D + 1:WIDE], ALU.add, ALU.max).then_inc(top_ready, 1)
                dve.wait_ge(top_ready, made(k))
                dve.nop(nofuse=True)
                dve.tensor_tensor(drop[:, s, 1:GROUP], run[:, s, 0:GROUP - 1, D + 1], run[:, s, 1:GROUP, D + 1],
                                  ALU.subtract).then_inc(drops, 1)
                dve.tensor_tensor(drop[:, s, 0:1], run[:, s0, j0, D + 1:WIDE], run[:, s, 0, D + 1:WIDE], ALU.subtract)\
                    .then_inc(drops, 1)
                dve.wait_ge(drops, k * 2 + 2)
                dve.nop(nofuse=True)
                dve.tensor_tensor(drop[:, s, :], drop[:, s, :], m.reset[0:LANES, ds(k * GROUP, GROUP)], ALU.add)\
                    .then_inc(drop_ready, 1)

            def shifted(k, s, used):
                dve.wait_ge(top_spread, made(k))
                dve.nop(nofuse=True)
                dve.tensor_tensor(shift[:, s, :], alpha[:, s, :], top_bank[:, 0:GROUP], ALU.subtract)\
                    .then_inc(shifts, 1)
                dve.wait_ge(shifts, k + 1)
                dve.nop(nofuse=True)
                dve.tensor_scalar(shift[:, s, :], shift[:, s, :], 0.0, None, ALU.min).then_inc(shift_ready, 1)

            def weight(k, s, used):
                dve.wait_ge(exp_ready, made(k))
                dve.nop(nofuse=True)
                dve.tensor_tensor(onehot[:, s, :, :], onehot[:, s, :, :],
                                  shift[:, s, :].unsqueeze(2).to_broadcast([SLOTS, GROUP, LANES]), ALU.mult)\
                    .then_inc(weighted, 1)

            def accumulate(k, s, used):
                s0, j0 = before(s, 0)
                dve.wait_ge(summed, made(k))
                dve.nop(nofuse=True)
                dve.wait_ge(scale_ready, made(k))
                dve.nop(nofuse=True)
                dve.tensor_tensor_scan(run[:, s, :, D], scale[:, s, :], exp_bank[0:LANES, s % 2, 0:GROUP],
                                       run[:, s0, j0, D:D + 1], ALU.mult, ALU.add)
                for j in range(GROUP):
                    sj, jj = before(s, j)
                    dve.wait_ge(added, k * GROUP + (j + CREDIT * GROUP))
                    dve.nop(nofuse=True)
                    dve.scalar_tensor_tensor(run[:, s, j, 0:D], run[:, sj, jj, 0:D], scale[:, s, j:j + 1],
                                             sums[0:LANES, s % 2, j, :], ALU.mult, ALU.add).then_inc(added, 1)

            in_steps(dve, GROUPS, [
                (2, match_stage(dve, m, onehot, m.record, onehot_ready, summed)),
                (3, alphas), (3, mask), (4, tops), (5, shifted), (5, weight), (6, accumulate)])


def gat_nodes(nc, m, target, bias, gamma, beta, x_out=None):
    with Phase(nc, f"gat{m.layer}_nodes") as ph:
        loaded, step, asked, answered, stored, x_done = (
            ph.sem(n) for n in ("loaded", "step", "asked", "answered", "stored", "x_done"))
        totals_asked, totals_ready = ph.sem("totals_asked"), ph.sem("totals_ready")
        bias_t, gamma_t, beta_t = (ph.sbuf(n, [LANES, D]) for n in ("bias", "gamma", "beta"))
        own, peak, inverse = (ph.sbuf(n, [LANES, BLOCKS]) for n in ("own", "peak", "inverse"))
        drop = ph.sbuf("drop", [LANES, 2, BLOCKS])
        column = ph.sbuf("column", [LANES, D])
        mean, inv_std, std = (ph.sbuf(n, [LANES, D]) for n in ("mean", "inv_std", "std"))
        square = ph.sbuf("square", [LANES, BLOCKS, D])
        norms = Norms(ph, [1e-5]) if x_out is not None else None
        bank = ph.psum("bank", [128, 512])
        block = ph.block()

        @block.sync
        def _(sp):
            for tile, source in ((bias_t, bias), (gamma_t, gamma), (beta_t, beta)):
                sp.dma_start(tile[:, :], row_of(source, LANES)).then_inc(loaded, 16)
            if x_out is not None:
                sp.wait_ge(x_done, 1)
                sp.dma_start(x_out.rearrange("(b p) f -> p b f", p=LANES), m.x[:, :, :]).then_inc(stored, 16)
                sp.wait_ge(stored, 16)

        @block.vector
        def _(dve):
            chain = Chain(dve, step)
            t = target[:, :, 0:D]
            sums, exps, tops = m.acc[:, :, 0:D], m.acc[:, :, D], m.acc[:, :, D + 1]
            chain(dve.tensor_tensor(own[:, :], m.h[:, :, D], m.al_d[:, :], ALU.add))
            chain(dve.tensor_scalar(own[:, :], own[:, :], m.mean_logit[:, m.layer:m.layer + 1], None, ALU.add))
            chain(dve.scalar_tensor_tensor(own[:, :], own[:, :], 0.2, own[:, :], ALU.mult, ALU.max))
            chain(dve.tensor_tensor(peak[:, :], own[:, :], tops, ALU.max))
            chain(dve.tensor_tensor(drop[:, 0, :], tops, peak[:, :], ALU.subtract))
            chain(dve.tensor_tensor(drop[:, 1, :], own[:, :], peak[:, :], ALU.subtract))
            dve.sem_inc(asked, 1)
            dve.wait_ge(answered, 1)
            chain(dve.tensor_tensor(exps, exps, drop[:, 0, :], ALU.mult))
            chain(dve.tensor_tensor(exps, exps, drop[:, 1, :], ALU.add))
            chain(dve.tensor_scalar(exps, exps, 1e-16, None, ALU.add))
            chain(dve.reciprocal(inverse[:, :], exps))
            chain(dve.tensor_tensor(drop[:, 0, :], drop[:, 0, :], inverse[:, :], ALU.mult))
            chain(dve.tensor_tensor(drop[:, 1, :], drop[:, 1, :], inverse[:, :], ALU.mult))
            chain(dve.tensor_tensor(sums, sums, per_node(drop[:, 0, :]), ALU.mult))
            chain(dve.tensor_tensor(square[:, :, :], m.h[:, :, 0:D], per_node(drop[:, 1, :]), ALU.mult))
            chain(dve.tensor_tensor(t, sums, square[:, :, :], ALU.add))
            dve.wait_ge(loaded, 48)
            chain(dve.tensor_tensor(t, t, per_column(bias_t[:, :]), ALU.add))
            chain(dve.scalar_tensor_tensor(t, t, 0.01, t, ALU.mult, ALU.max))
            chain(dve.tensor_reduce(column[:, :], t.rearrange("p b f -> p f b"), AX.X, ALU.add))
            dve.sem_inc(totals_asked, 1)
            dve.wait_ge(totals_ready, 1)
            chain(dve.tensor_scalar(mean[:, :], bank[0:LANES, 0:D], 1.0 / NODES, None, ALU.mult))
            chain(dve.tensor_tensor(t, t, per_column(mean[:, :]), ALU.subtract))
            chain(dve.tensor_tensor(square[:, :, :], t, t, ALU.mult))
            chain(dve.tensor_reduce(column[:, :], square[:, :, :].rearrange("p b f -> p f b"), AX.X, ALU.add))
            dve.sem_inc(totals_asked, 1)
            dve.wait_ge(totals_ready, 2)
            chain(dve.tensor_scalar(inv_std[:, :], bank[0:LANES, D:2 * D], 1.0 / NODES, 1e-5, ALU.mult, ALU.add))
            dve.sem_inc(asked, 1)
            dve.wait_ge(answered, 2)
            chain(dve.reciprocal(inv_std[:, :], std[:, :]))
            chain(dve.tensor_tensor(inv_std[:, :], inv_std[:, :], gamma_t[:, :], ALU.mult))
            chain(dve.tensor_tensor(t, t, per_column(inv_std[:, :]), ALU.mult))
            chain(dve.tensor_tensor(t, t, per_column(beta_t[:, :]), ALU.add))
            if x_out is not None:
                chain(dve.tensor_tensor(m.x[:, :, :], m.x[:, :, :], t, ALU.add))
                norms.normalize(dve, chain, m.x[:, :, :])
                dve.sem_inc(x_done, 1)

        @block.scalar
        def _(act):
            act.wait_ge(asked, 1)
            act.activation(drop[:, :, :], drop[:, :, :], ACT.Exp).then_inc(answered, 1)
            act.wait_ge(asked, 2)
            act.activation(std[:, :], inv_std[:, :], ACT.Sqrt).then_inc(answered, 1)
            if x_out is not None:
                norms.roots(act)

        @block.tensor
        def _(pe):
            for n in range(2):
                pe.wait_ge(totals_asked, n + 1)
                pe.matmul(bank[0:LANES, n * D:(n + 1) * D], m.ones[0:LANES, 0:LANES], column[:, :], start=True,
                          stop=True).then_inc(totals_ready, 1)


class Memory:
    pass


def gnn(nc, x, src, dst, edge_attr_3, edge_attr_4, edge_attr_8, node_type_4, *rest, stop=99, dump=None):
    *w, out = rest
    stack = ExitStack()
    with stack:
        m = Memory()
        m.kept = stack

        def sbuf(name, shape, dtype=F32):
            return stack.enter_context(nc.sbuf_tensor(name, shape, dtype))

        m.ident = sbuf("ident", [128, 128])
        m.ones = sbuf("ones", [128, 128])
        m.earlier = sbuf("earlier", [128, 128])
        m.ramp = sbuf("ramp", [128, TILES])
        m.record = sbuf("records", [SLOTS, TILES, RECORD])
        m.sender = sbuf("sender", [SLOTS, TILES], I32)
        m.receiver_block = sbuf("receiver_block", [1, TILES], I32)
        m.reset = sbuf("reset", [SLOTS, TILES])
        m.acc = sbuf("acc", [LANES, BLOCKS, 2 * D])
        m.receiver = sbuf("receiver", [SLOTS, TILES], I32)
        m.sender_place = sbuf("by_sender", [SLOTS, TILES, 2])
        m.sender_block = sbuf("sender_block", [1, TILES], I32)
        table1 = nc.dram_tensor("edges_by_receiver", [SLOTS * TILES, RECORD], F32, kind="Internal").ap()
        constants(nc, m)
        with Phase(nc, "edges") as ph:
            row = ph.sbuf("row", [LANES, PER_LANE], I32)
            place = ph.sbuf("place", [LANES, PER_LANE])
            put_in_order(nc, m, "by_receiver", dst, row, place, m.receiver_block, m.reset)
            edge_records(nc, m, ph, table1, row, place, src, edge_attr_3, edge_attr_4, edge_attr_8)
        with Phase(nc, "edges_again") as ph:
            row = ph.sbuf("row", [LANES, PER_LANE], I32)
            place = ph.sbuf("place", [LANES, PER_LANE])
            put_in_order(nc, m, "sender_order", src, row, place, m.sender_block)
            sender_records(nc, m, ph, nc.dram_tensor("edges_by_sender", [SLOTS * TILES, 2], F32, kind="Internal").ap(),
                           row, place, dst)
        m.x = sbuf("nodes", [LANES, BLOCKS, D])
        sum_neighbours(nc, m, x)
        gin_nodes(nc, m, x, *w[0:7])
        if stop == 0:
            return dump(nc, m, out)
        with ExitStack() as layer:
            def own(name, shape, dtype=F32):
                return layer.enter_context(nc.sbuf_tensor(name, shape, dtype))

            m.up_skip = own("up_skip", [D, D + SPECIES * SKIP])
            m.down = own("down", [D, 2, SKIP])
            m.radial1 = own("radial1", [GROUP * RECORD, GROUP * RADIAL])
            m.radial2 = own("radial2", [GROUP * RADIAL, GROUP * D])
            m.is_species = own("is_species", [LANES, BLOCKS, SPECIES])
            m.skip = own("skip", [LANES, BLOCKS, SKIP])
            sources = nc.dram_tensor("equivariant_table", [NODES, D], F32, kind="Internal").ap()
            equivariant_weights(nc, m, *w[7:15], node_type_4)
            equivariant_sources(nc, m, sources)
            equivariant_messages(nc, m, sources)
            equivariant_nodes(nc, m)
        if stop == 1:
            return dump(nc, m, out)
        with ExitStack() as layer:
            m.qkv = layer.enter_context(nc.sbuf_tensor("qkv", [D, 3 * D], F32))
            m.qkv_bias = layer.enter_context(nc.sbuf_tensor("qkv_bias", [LANES, 3 * D], F32))
            m.query = layer.enter_context(nc.sbuf_tensor("query", [LANES, BLOCKS, D], F32))
            sources = nc.dram_tensor("attention_table", [NODES, 2 * D], F32, kind="Internal").ap()
            attention_weights(nc, m, *w[15:21])
            attention_sources(nc, m, sources)
            attention_messages(nc, m, sources)
            attention_nodes(nc, m, *w[21:23])
        if stop == 2:
            return dump(nc, m, out)
        m.edge_logit = sbuf("edge_logit", [SLOTS, 3, TILES])
        m.mean_logit = sbuf("mean_logit", [LANES, 3])
        m.h = sbuf("h", [LANES, BLOCKS, D + 1])
        m.al_d = sbuf("al_d", [LANES, BLOCKS])
        gat_in = sbuf("gat_in", [LANES, BLOCKS, D])
        gat = [w[23 + 8 * n:31 + 8 * n] for n in range(3)]
        edge_logits(nc, m, [(we, ae) for _, _, _, we, ae, _, _, _ in gat])
        for m.layer, (wn, a_src, a_dst, _, _, bias, gamma, beta) in enumerate(gat):
            sources = nc.dram_tensor(f"gat_table{m.layer}", [NODES, D + 1], F32, kind="Internal").ap()
            gat_sources(nc, m, m.x if m.layer == 0 else gat_in, wn, a_src, a_dst, sources)
            gat_messages(nc, m, sources)
            gat_nodes(nc, m, gat_in, bias, gamma, beta, out if m.layer == 2 else None)
def edge_records(nc, m, ph, table, row, place, src, edge_attr_3, edge_attr_4, edge_attr_8):
    src_int = ph.sbuf("src_int", [LANES, PER_LANE], I32)
    src_f = ph.sbuf("src_f", [LANES, PER_LANE])
    attr = [ph.sbuf(f"attr_{n}", [LANES, PER_LANE, n]) for n in (3, 4, 8)]
    with Phase(nc, "raw_edges") as raw:
        loaded, copied = raw.sem("loaded"), raw.sem("copied")
        block = raw.block()

        @block.sync
        def _(sp):
            sp.dma_start(src_int[:, :], src.rearrange("(p c) -> p c", p=LANES)).then_inc(loaded, 16)
            for tile, source in zip(attr, (edge_attr_3, edge_attr_4, edge_attr_8)):
                sp.dma_start(tile[:, :, :].rearrange("p c w -> p (c w)"),
                             source.rearrange("(p c) w -> p (c w)", p=LANES)).then_inc(loaded, 16)

        @block.vector
        def _(dve):
            dve.wait_ge(loaded, 64)
            dve.tensor_copy(src_f[:, :], src_int[:, :]).then_inc(copied, 1)
            dve.wait_ge(copied, 1)
    scatter_records(nc, m, "scatter_by_receiver", table, RECORD, row, [
        (0, 1, src_f[:, :].unsqueeze(2)),
        (1, 1, place[:, :].unsqueeze(2)),
        (8, 8, attr[2][:, :, :]),
        (2, 3, attr[0][:, :, :]),
        (5, 3, attr[1][:, :, 1:4]),
    ], m.record[:, :, :].rearrange("p t w -> p (t w)"))
    with Phase(nc, "sender_index") as last:
        copied = last.sem("copied")
        block = last.block()

        @block.vector
        def _(dve):
            dve.tensor_copy(m.sender[:, :], m.record[:, :, 0]).then_inc(copied, 1)
            dve.wait_ge(copied, 1)


def sender_records(nc, m, ph, table, row, place, dst):
    dst_int = ph.sbuf("dst_int", [LANES, PER_LANE], I32)
    dst_f = ph.sbuf("dst_f", [LANES, PER_LANE])
    with Phase(nc, "raw_receivers") as raw:
        loaded, copied = raw.sem("loaded"), raw.sem("copied")
        block = raw.block()

        @block.sync
        def _(sp):
            sp.dma_start(dst_int[:, :], dst.rearrange("(p c) -> p c", p=LANES)).then_inc(loaded, 16)

        @block.vector
        def _(dve):
            dve.wait_ge(loaded, 16)
            dve.tensor_copy(dst_f[:, :], dst_int[:, :]).then_inc(copied, 1)
            dve.wait_ge(copied, 1)
    scatter_records(nc, m, "scatter_by_sender", table, 2, row, [
        (0, 1, dst_f[:, :].unsqueeze(2)),
        (1, 1, place[:, :].unsqueeze(2)),
    ], m.sender_place[:, :, :].rearrange("p t w -> p (t w)"))
    with Phase(nc, "receiver_index") as last:
        copied = last.sem("copied")
        block = last.block()

        @block.vector
        def _(dve):
            dve.tensor_copy(m.receiver[:, :], m.sender_place[:, :, 0]).then_inc(copied, 1)
            dve.wait_ge(copied, 1)


def kernel(**inputs):
    import numpy as np
    import concourse.bacc as bacc
    from concourse.bass_utils import run_bass_kernel_spmd

    nc = bacc.Bacc("TRN2", target_bir_lowering=False, num_devices=1)
    arrays, args = {}, []
    for name, value in inputs.items():
        a = np.ascontiguousarray(value)
        a = a.reshape(1) if a.ndim == 0 else a
        arrays[f"in_{name}"] = a
        args.append(nc.dram_tensor(f"in_{name}", a.shape, mybir.dt.from_np(a.dtype), kind="ExternalInput").ap())
    args.append(nc.dram_tensor("out_nodes", (NODES, D), F32, kind="ExternalOutput").ap())
    gnn(nc, *args)
    return run_bass_kernel_spmd(nc, [arrays], core_ids=[0]).results[0]["out_nodes"]
```

```python
from contextlib import ExitStack
from itertools import count as numbers

import concourse.bass as bass
from concourse import mybir

F32 = mybir.dt.float32
I32 = mybir.dt.int32
ALU = mybir.AluOpType
ACT = mybir.ActivationFunctionType
AX = mybir.AxisListType

NODES = 3125
EDGES = 100000
D = 128
LANES = 125
BLOCKS = NODES // LANES
PER_LANE = EDGES // LANES
SLOTS = 128
GROUP = 4
PAIR = 2
GROUP_PAIRS = GROUP // PAIR
MOST_PAIRS = (EDGES + BLOCKS * (PAIR * SLOTS - 1)) // (PAIR * SLOTS)
GROUPS = -(-MOST_PAIRS // GROUP_PAIRS)
PAIRS = GROUPS * GROUP_PAIRS
TILES = PAIRS * PAIR
RECORD = 16
CHUNK = 8
HEADS = 8
HEAD = D // HEADS
MUL = 32
SPECIES = 4
RADIAL = 8
FAR = -1e30
RESET = -3e38


def ds(start, size):
    return bass.ds(start.at if isinstance(start, Turn) else start, size)


class Chain:

    def __init__(self, engine, done):
        self.engine, self.done, self.n = engine, done, 0

    def __call__(self, instruction):
        instruction.then_inc(self.done, 1)
        self.n += 1
        self.engine.wait_ge(self.done, self.n)


RING = 4
DEEP = 8
CREDIT = DEEP
REGISTERS = numbers()


def made(k):
    return k + (CREDIT + 1)


def free(k, ring=RING):
    return k + (CREDIT + 1 - ring)


class Turn:

    def __init__(self, i, ring, q, registers):
        self.at, self.q, self.registers = i * ring + q, q, registers

    def __add__(self, c):
        return self.registers.get(self.q + c, self.at + c)

    def __mul__(self, c):
        return self.at * c


def is_new(used):
    return isinstance(used, int) and used == 0


def in_steps(engine, count, stages, ring=RING):
    lead = -(-max(max(lag for lag, _ in stages), ring) // ring) * ring

    def step(n):
        for lag, stage in stages:
            if 0 <= n - lag < count:
                stage(n - lag, (n - lag) % ring, (n - lag) // ring)

    for n in range(lead):
        step(n)
    first, last = CREDIT + 1 - ring - max(lag for lag, _ in stages), CREDIT + ring
    registers = {c: engine.alloc_register(f"count{next(REGISTERS)}")
                 for c in range(max(first, CREDIT + 1 - lead), last + 1)}
    with engine.Fori(lead // ring, count // ring) as i:
        for c, register in registers.items():
            engine.reg_mov(register, i * ring + c)
        for turn in range(ring):
            for lag, stage in stages:
                q = turn - lag
                stage(Turn(i, ring, q, registers), q % ring, i + q // ring)
    for register in registers.values():
        engine.free_register(register)
    for n in range(count // ring * ring, count + lead):
        step(n)


class Phase:

    def __init__(self, nc, name):
        self.nc, self.name, self.stack, self.sems = nc, name, ExitStack(), []

    def __enter__(self):
        self.stack.__enter__()
        return self

    def __exit__(self, *error):
        return self.stack.__exit__(*error)

    def clear(self):
        for sem in self.sems:
            self.nc.sync.sem_clear(sem)

    def sbuf(self, name, shape, dtype=F32):
        return self.stack.enter_context(self.nc.sbuf_tensor(f"{self.name}_{name}", shape, dtype))

    def psum(self, name, shape, dtype=F32):
        return self.stack.enter_context(self.nc.psum_tensor(f"{self.name}_{name}", shape, dtype))

    def sem(self, name):
        self.sems.append(self.stack.enter_context(self.nc.semaphore(f"{self.name}_{name}")))
        return self.sems[-1]

    def block(self):
        self.stack.callback(self.clear)
        return self.stack.enter_context(self.nc.Block())


def software_dma_sems(nc, m, ph, count):
    return [m.kept.enter_context(nc.semaphore(f"{ph.name}_landed{s}")) for s in range(count)]


def row_of(vector, partitions):
    return vector.rearrange("(a n) -> a n", a=1).to_broadcast([partitions, vector.shape[0]])


def constants(nc, m):
    with Phase(nc, "constants") as ph:
        step, whole = ph.sem("step"), ph.sem("whole")
        ramp = ph.sbuf("ramp", [128, PAIRS], I32)
        lane = ph.sbuf("lane", [128, 1], I32)
        block = ph.block()

        @block.gpsimd
        def _(pool):
            chain = Chain(pool, step)
            chain(pool.memset(m.ones[:, :], 1.0))
            chain(pool.memset(m.ident[:, :], 0.0))
            chain(pool.affine_select(out=m.ident[:, :], in_=m.ident[:, :], compare_op=ALU.not_equal, fill=1.0,
                                     base=0, pattern=[[-1, 128]], channel_multiplier=1))
            chain(pool.affine_select(out=m.earlier[:, :], in_=m.ones[:, :], compare_op=ALU.is_gt, fill=0.0,
                                     base=0, pattern=[[1, 128]], channel_multiplier=-1))
            chain(pool.iota(ramp[:, :], pattern=[[1, PAIRS]], base=0, channel_multiplier=0))
            chain(pool.tensor_copy(m.ramp[:, :], ramp[:, :]))
            chain(pool.iota(lane[:, :], pattern=[[1, 1]], base=0, channel_multiplier=1))
            chain(pool.tensor_copy(m.lane[:, :], lane[:, :]))
            pool.sem_inc(whole, 1)

        @block.vector
        def _(dve):
            dve.wait_ge(whole, 1)


def ordering(ph, m, key, row, place, pair_block, runs=False):
    loaded, step, counts_ready, sums_ready = (ph.sem(x) for x in ("key_loaded", "step", "counts", "sums"))
    key_int = ph.sbuf("key_int", [LANES, PER_LANE], I32)
    key_f = ph.sbuf("key_f", [LANES, PER_LANE])
    blk = ph.sbuf("blk", [LANES, PER_LANE])
    inside = ph.sbuf("inside", [LANES, PER_LANE])
    count = ph.sbuf("count", [LANES, PER_LANE])
    position = ph.sbuf("position", [LANES, PER_LANE])
    ones = ph.sbuf("ones", [LANES, PER_LANE])
    low = ph.sbuf("low", [LANES, PER_LANE], I32)
    first_node = ph.sbuf("first_node", [LANES, BLOCKS])
    block_sum = ph.sbuf("block_sum", [LANES, BLOCKS])
    at_least = ph.sbuf("at_least", [LANES, BLOCKS + 1])
    own = ph.sbuf("own", [LANES, BLOCKS])
    pairs_int = ph.sbuf("pairs_int", [128, BLOCKS], I32)
    pairs = ph.sbuf("pairs", [128, BLOCKS])
    pair_end = ph.sbuf("pair_end", [128, BLOCKS])
    base = ph.sbuf("base", [LANES, BLOCKS])
    pair_blk = ph.sbuf("pair_blk", [128, PAIRS])
    sums = ph.psum("sums", [128, 512])

    def on_sync(sp):
        sp.dma_start(key_int[:, :], key.rearrange("(p c) -> p c", p=LANES)).then_inc(loaded, 16)

    def on_vector(dve):
        chain = Chain(dve, step)
        chain(dve.tensor_scalar(first_node[:, :], m.ramp[0:LANES, 0:BLOCKS], float(LANES), None, ALU.mult))
        chain(dve.memset(blk[:, :], 0.0))
        chain(dve.memset(ones[:, :], 1.0))
        chain(dve.memset(position[:, :], 0.0))
        chain(dve.memset(block_sum[:, 0:1], 0.0))
        chain(dve.memset(at_least[:, 0:1], float(PER_LANE)))
        chain(dve.memset(at_least[:, BLOCKS:BLOCKS + 1], 0.0))
        dve.wait_ge(loaded, 16)
        chain(dve.tensor_copy(key_f[:, :], key_int[:, :]))
        before = chain.n
        with dve.Fori(1, BLOCKS) as b:
            dve.wait_ge(step, b + (before - 1))
            dve.scalar_tensor_tensor(blk[:, :], key_f[:, :], first_node[:, ds(b, 1)], blk[:, :], ALU.is_ge,
                                     ALU.add, accum_out=block_sum[:, ds(b, 1)]).then_inc(step, 1)
        chain.n += BLOCKS - 1
        dve.wait_ge(step, chain.n)
        chain(dve.tensor_tensor(at_least[:, 1:BLOCKS], block_sum[:, 1:BLOCKS], block_sum[:, 0:BLOCKS - 1],
                                ALU.subtract))
        chain(dve.tensor_tensor(own[:, :], at_least[:, 0:BLOCKS], at_least[:, 1:BLOCKS + 1], ALU.subtract))
        dve.sem_inc(counts_ready, 1)
        chain(dve.scalar_tensor_tensor(place[:, :], blk[:, :], -float(LANES), key_f[:, :], ALU.mult, ALU.add))
        chain(dve.tensor_scalar(place[:, :], place[:, :], 1.0, None, ALU.add))
        dve.wait_ge(sums_ready, 1)
        chain(dve.tensor_scalar(pairs_int[:, :], sums[:, 64:64 + BLOCKS], float(PAIR * SLOTS - 1), None, ALU.add))
        chain(dve.tensor_scalar(pairs_int[:, :], pairs_int[:, :], 8, None, ALU.arith_shift_right))
        chain(dve.tensor_copy(pairs[:, :], pairs_int[:, :]))
        chain(dve.tensor_tensor_scan(pair_end[:, :], m.ones[:, 0:BLOCKS], pairs[:, :], 0.0, ALU.mult, ALU.add))
        chain(dve.tensor_tensor(base[:, :], pair_end[0:LANES, :], pairs[0:LANES, :], ALU.subtract))
        chain(dve.tensor_scalar(base[:, :], base[:, :], float(PAIR * SLOTS), -1.0, ALU.mult, ALU.add))
        chain(dve.tensor_tensor(base[:, :], base[:, :], sums[0:LANES, 0:BLOCKS], ALU.add))
        before = chain.n
        with dve.Fori(0, BLOCKS) as b:
            dve.wait_ge(step, b * 3 + before)
            dve.tensor_scalar(inside[:, :], blk[:, :], m.ramp[0:LANES, ds(b, 1)], None, ALU.is_equal)\
                .then_inc(step, 1)
            dve.wait_ge(step, b * 3 + (before + 1))
            dve.tensor_tensor_scan(count[:, :], ones[:, :], inside[:, :], base[:, ds(b, 1)], ALU.mult, ALU.add)\
                .then_inc(step, 1)
            dve.wait_ge(step, b * 3 + (before + 2))
            dve.nop(nofuse=True)
            dve.copy_predicated(out=position[:, :], mask=inside[:, :].bitcast(I32), data=count[:, :])\
                .then_inc(step, 1)
        chain.n += 3 * BLOCKS
        dve.wait_ge(step, chain.n)
        chain(dve.tensor_copy(key_int[:, :], position[:, :]))
        chain(dve.tensor_scalar(low[:, :], key_int[:, :], SLOTS - 1, None, ALU.bitwise_and))
        chain(dve.tensor_scalar(key_int[:, :], key_int[:, :], 7, None, ALU.arith_shift_right))
        chain(dve.scalar_tensor_tensor(row[:, :], low[:, :], float(TILES), key_int[:, :], ALU.mult, ALU.add))
        chain(dve.memset(pair_blk[:, :], 0.0))
        before = chain.n
        with dve.Fori(0, BLOCKS - 1) as b:
            dve.wait_ge(step, b + before)
            dve.scalar_tensor_tensor(pair_blk[:, :], m.ramp[:, 0:PAIRS], pair_end[:, ds(b, 1)], pair_blk[:, :],
                                     ALU.is_ge, ALU.add).then_inc(step, 1)
        chain.n += BLOCKS - 1
        dve.wait_ge(step, chain.n)
        chain(dve.tensor_copy(pair_block[:, :], pair_blk[0:1, :]))
        if runs:
            chain(dve.tensor_tensor(m.reset[:, 1:PAIRS], pair_blk[:, 1:PAIRS], pair_blk[:, 0:PAIRS - 1],
                                    ALU.not_equal))
            chain(dve.memset(m.reset[:, 0:1], 1.0))
            chain(dve.tensor_scalar(m.reset[:, :], m.reset[:, :], RESET, None, ALU.mult))
            chain(dve.tensor_scalar(m.pair_is[:, :], pair_blk[0:BLOCKS, :], m.lane[0:BLOCKS, :], None,
                                    ALU.is_equal))

    def on_tensor(pe):
        pe.wait_ge(counts_ready, 1)
        pe.matmul(sums[0:LANES, 0:BLOCKS], m.earlier[0:LANES, 0:LANES], own[:, :], start=True, stop=True)
        pe.matmul(sums[:, 64:64 + BLOCKS], m.ones[0:LANES, :], own[:, :], start=True, stop=True)\
            .then_inc(sums_ready, 1)

    return on_sync, on_vector, on_tensor


def scattering(nc, m, ph, table, width, row, parts, ordered):
    steps = PER_LANE // CHUNK
    table_in, filled = ph.sem("table_in"), ph.sem("filled")
    scattered = software_dma_sems(nc, m, ph, 2)
    record = ph.sbuf("record", [LANES, 2, CHUNK, width])
    index = ph.sbuf("index", [LANES, 2, CHUNK], I32)

    def on_scalar(act):
        def fill(k, s, used):
            if not is_new(used):
                act.wait_ge(scattered[s], used * (16 * CHUNK))
                act.nop(nofuse=True)
            act.copy(index[:, s, :], row[:, ds(k * CHUNK, CHUNK)])
            for first, n, source in parts:
                last = act.copy(record[:, s, :, first:first + n], source[:, ds(k * CHUNK, CHUNK), :])
            last.then_inc(filled, 1)

        in_steps(act, steps, [(0, fill)], 2)

    def on_gpsimd(pool):
        def scatter(k, s, used):
            pool.wait_ge(filled, k + 1)
            pool.nop(nofuse=True)
            for c in range(CHUNK):
                pool.indirect_dma_start(
                    out=table[:, :], out_offset=bass.IndirectOffsetOnAxis(ap=index[:, s, c:c + 1], axis=0),
                    in_=record[:, s, c, :], in_offset=None).then_inc(scattered[s], 16)

        in_steps(pool, steps, [(0, scatter)], 2)

    def on_sync(sp):
        for s in range(2):
            sp.wait_ge(scattered[s], 16 * CHUNK * steps // 2)
        sp.dma_start(ordered, table.rearrange("(p t) w -> p (t w)", p=SLOTS)).then_inc(table_in, 16)
        sp.wait_ge(table_in, 16)

    return on_scalar, on_gpsimd, on_sync


def order_edges(nc, m, src, dst, edge_attr_3, edge_attr_4, edge_attr_8):
    by_receiver = nc.dram_tensor("edges_by_receiver", [SLOTS * TILES, RECORD], F32, kind="Internal").ap()
    by_sender = nc.dram_tensor("edges_by_sender", [SLOTS * TILES, 2], F32, kind="Internal").ap()
    tables = ((by_receiver, m.record), (by_sender, m.sender_place))
    with ExitStack() as stack:
        def sbuf(name, shape, dtype=F32):
            return stack.enter_context(nc.sbuf_tensor(name, shape, dtype))

        row, sender_row = (sbuf(n, [LANES, PER_LANE], I32) for n in ("row", "sender_row"))
        place, sender_place = (sbuf(n, [LANES, PER_LANE]) for n in ("place", "sender_place"))
        ends = sbuf("ends", [LANES, PER_LANE], I32)
        end_f = sbuf("end_f", [LANES, PER_LANE])
        with ExitStack() as attributes:
            attr = [attributes.enter_context(nc.sbuf_tensor(f"attr_{n}", [LANES, PER_LANE, n], F32))
                    for n in (3, 4, 8)]
            with Phase(nc, "receiver_order") as ph:
                cleared, loaded, zeroed, copied = (ph.sem(x) for x in ("cleared", "loaded", "zeroed", "copied"))
                order_sync, order_vector, order_tensor = ordering(ph, m, dst, row, place, m.receiver_block, True)
                block = ph.block()

                @block.gpsimd
                def _(pool):
                    for _, ordered in tables:
                        pool.memset(ordered[:, :, :], 0.0).then_inc(cleared, 1)

                @block.sync
                def _(sp):
                    order_sync(sp)
                    sp.dma_start(ends[:, :], src.rearrange("(p c) -> p c", p=LANES)).then_inc(loaded, 16)
                    for tile, source in zip(attr, (edge_attr_3, edge_attr_4, edge_attr_8)):
                        sp.dma_start(tile[:, :, :].rearrange("p c w -> p (c w)"),
                                     source.rearrange("(p c) w -> p (c w)", p=LANES)).then_inc(loaded, 16)
                    sp.wait_ge(cleared, 2)
                    for table, ordered in tables:
                        sp.dma_start(table.rearrange("(p t) w -> p (t w)", p=SLOTS),
                                     ordered[:, :, :].rearrange("p t w -> p (t w)")).then_inc(zeroed, 16)
                    sp.wait_ge(zeroed, 32)
                    sp.wait_ge(loaded, 64)

                @block.vector
                def _(dve):
                    order_vector(dve)
                    dve.wait_ge(loaded, 64)
                    dve.tensor_copy(end_f[:, :], ends[:, :]).then_inc(copied, 1)
                    dve.wait_ge(copied, 1)

                @block.tensor
                def _(pe):
                    order_tensor(pe)

            with Phase(nc, "sender_order") as ph:
                order_sync, order_vector, order_tensor = ordering(ph, m, src, sender_row, sender_place,
                                                                  m.sender_block)
                scatter_scalar, scatter_gpsimd, scatter_sync = scattering(nc, m, ph, by_receiver, RECORD, row, [
                    (0, 1, end_f[:, :].unsqueeze(2)),
                    (1, 1, place[:, :].unsqueeze(2)),
                    (2, 3, attr[0][:, :, :]),
                    (5, 3, attr[1][:, :, 1:4]),
                    (8, 8, attr[2][:, :, :]),
                ], m.record[:, :, :].rearrange("p t w -> p (t w)"))
                block = ph.block()

                @block.gpsimd
                def _(pool):
                    scatter_gpsimd(pool)

                @block.scalar
                def _(act):
                    scatter_scalar(act)

                @block.sync
                def _(sp):
                    order_sync(sp)
                    scatter_sync(sp)

                @block.vector
                def _(dve):
                    order_vector(dve)

                @block.tensor
                def _(pe):
                    order_tensor(pe)

        with Phase(nc, "by_sender") as ph:
            loaded, copied = ph.sem("loaded"), ph.sem("copied")
            scatter_scalar, scatter_gpsimd, scatter_sync = scattering(nc, m, ph, by_sender, 2, sender_row, [
                (0, 1, end_f[:, :].unsqueeze(2)),
                (1, 1, sender_place[:, :].unsqueeze(2)),
            ], m.sender_place[:, :, :].rearrange("p t w -> p (t w)"))
            block = ph.block()

            @block.gpsimd
            def _(pool):
                scatter_gpsimd(pool)

            @block.scalar
            def _(act):
                act.wait_ge(copied, 2)
                scatter_scalar(act)

            @block.sync
            def _(sp):
                sp.dma_start(ends[:, :], dst.rearrange("(p c) -> p c", p=LANES)).then_inc(loaded, 16)
                scatter_sync(sp)

            @block.vector
            def _(dve):
                dve.wait_ge(loaded, 16)
                dve.tensor_copy(end_f[:, :], ends[:, :]).then_inc(copied, 1)
                dve.tensor_copy(m.sender[:, :], m.record[:, :, 0]).then_inc(copied, 1)
    with Phase(nc, "receivers") as ph:
        copied = ph.sem("copied")
        block = ph.block()

        @block.vector
        def _(dve):
            dve.tensor_copy(m.receiver[:, :], m.sender_place[:, :, 0]).then_inc(copied, 1)
            dve.wait_ge(copied, 1)


def one_hots(dve, m, onehot, place):
    return dve.tensor_tensor(
        onehot, m.ramp[:, 1:1 + LANES].unsqueeze(1).to_broadcast([SLOTS, GROUP, LANES]),
        place.to_broadcast([SLOTS, GROUP, LANES]), ALU.is_equal)


def gathers(pool, table, rows, index, gathered):
    for j in range(GROUP):
        pool.indirect_dma_start(out=rows[:, j, :], out_offset=None, in_=table,
                                in_offset=bass.IndirectOffsetOnAxis(ap=index[:, j:j + 1], axis=0))\
            .then_inc(gathered, 16)


def index_stage(act, m, index, source, gathered, ready):
    def stage(k, s, used):
        if not is_new(used):
            act.wait_ge(gathered[s], used * (16 * GROUP))
            act.nop(nofuse=True)
        act.copy(index[:, s, :], source[:, ds(k * GROUP, GROUP)]).then_inc(ready, 1)
    return stage


def gather_stage(pool, table, rows, index, gathered, index_ready, rows_used, ring=RING):
    def stage(k, s, used):
        pool.wait_ge(index_ready, made(k))
        pool.nop(nofuse=True)
        pool.wait_ge(rows_used, free(k, ring))
        pool.nop(nofuse=True)
        gathers(pool, table, rows[:, s], index[:, s], gathered[s])
    return stage


def match_stage(dve, m, onehot, places, ready, used_by, ring=RING):
    def stage(k, s, used):
        dve.wait_ge(used_by, free(k, ring))
        dve.nop(nofuse=True)
        one_hots(dve, m, onehot[:, s], places[:, ds(k * GROUP, GROUP), 1:2]).then_inc(ready, 1)
    return stage


def add_stages(dve, m, blocks, width, sums_of_pair, summed, first_added, added):
    block_of = {}

    def read(p):
        def stage(k, s, used):
            block_of[p] = dve.value_load(blocks[0:1, ds(k * GROUP_PAIRS + p, 1)], min_val=0, max_val=BLOCKS - 1)
        return stage

    def add(k, s, used):
        dve.wait_ge(summed, made(k))
        dve.nop(nofuse=True)
        for p in range(GROUP_PAIRS):
            dve.wait_ge(*((added, free(k, 1)) if p == 0 else (first_added, made(k))))
            sums = m.acc[:, ds(block_of[p], 1), 0:width]
            dve.tensor_tensor(sums, sums, sums_of_pair(s % 2, p), ALU.add)\
                .then_inc(first_added if p == 0 else added, 1)

    return read(0), read(1), add


def sum_pairs(pe, left, right, sums_of_pair, s):
    for j in range(GROUP):
        last = pe.matmul(sums_of_pair(s % 2, j // PAIR), left(j), right(j), start=j % PAIR == 0,
                         stop=j % PAIR == PAIR - 1)
    return last


def sum_neighbours(nc, m, table):
    with Phase(nc, "gin") as ph:
        gathered = software_dma_sems(nc, m, ph, RING)
        index_ready, onehot_ready, summed, first_added, added, cleared = (
            ph.sem(x) for x in ("index_ready", "onehot_ready", "summed", "first_added", "added", "cleared"))
        index = ph.sbuf("index", [SLOTS, RING, GROUP], I32)
        rows = ph.sbuf("rows", [SLOTS, RING, GROUP, D])
        onehot = ph.sbuf("onehot", [SLOTS, RING, GROUP, LANES])
        sums = ph.psum("sums", [128, 2, 512])
        block = ph.block()

        def sums_of_pair(s, p):
            return sums[0:LANES, s, p * D:(p + 1) * D]

        @block.scalar
        def _(act):
            act.sem_inc(index_ready, CREDIT)
            in_steps(act, GROUPS, [(0, index_stage(act, m, index, m.sender, gathered, index_ready))])

        @block.gpsimd
        def _(pool):
            in_steps(pool, GROUPS, [(0, gather_stage(pool, table, rows, index, gathered, index_ready, summed))])

        @block.tensor
        def _(pe):
            pe.sem_inc(summed, CREDIT)

            def sum_tiles(k, s, used):
                pe.wait_ge(gathered[s], used * (16 * GROUP) + 16 * GROUP)
                pe.wait_ge(onehot_ready, made(k))
                pe.wait_ge(added, free(k, 2))
                sum_pairs(pe, lambda j: onehot[:, s, j, :], lambda j: rows[:, s, j, :], sums_of_pair, s)\
                    .then_inc(summed, 1)

            in_steps(pe, GROUPS, [(0, sum_tiles)])

        @block.vector
        def _(dve):
            dve.memset(m.acc[:, :, 0:D], 0.0).then_inc(cleared, 1)
            dve.wait_ge(cleared, 1)
            for s in (onehot_ready, first_added, added):
                dve.sem_inc(s, CREDIT)
            read_first, read_second, add = add_stages(dve, m, m.receiver_block, D, sums_of_pair, summed, first_added,
                                                      added)
            in_steps(dve, GROUPS, [(0, match_stage(dve, m, onehot, m.record, onehot_ready, summed)),
                                   (1, read_first), (1, read_second), (1, add)])


def per_node(vector):
    return vector.unsqueeze(2).to_broadcast([LANES, BLOCKS, D])


def per_column(row):
    return row.unsqueeze(1).to_broadcast([LANES, BLOCKS, D])


class Norms:

    def __init__(self, ph, epsilons):
        self.epsilons = epsilons
        self.var_ready, self.root_ready = ph.sem("var_ready"), ph.sem("root_ready")
        self.square = ph.sbuf("norm_square", [LANES, BLOCKS, D])
        self.total = ph.sbuf("norm_total", [LANES, BLOCKS])
        self.var = ph.sbuf("norm_var", [LANES, BLOCKS])
        self.root = ph.sbuf("norm_root", [LANES, BLOCKS])
        self.inverse = ph.sbuf("norm_inverse", [LANES, BLOCKS])
        self.done = 0

    def roots(self, act):
        for n in range(len(self.epsilons)):
            act.wait_ge(self.var_ready, n + 1)
            act.activation(self.root[:, :], self.var[:, :], ACT.Sqrt).then_inc(self.root_ready, 1)

    def normalize(self, dve, chain, t):
        chain(dve.tensor_reduce(self.total[:, :], t, AX.X, ALU.add))
        chain(dve.tensor_scalar(self.total[:, :], self.total[:, :], 1.0 / D, None, ALU.mult))
        chain(dve.tensor_tensor(t, t, per_node(self.total[:, :]), ALU.subtract))
        chain(dve.tensor_tensor(self.square[:, :, :], t, t, ALU.mult))
        chain(dve.tensor_reduce(self.total[:, :], self.square[:, :, :], AX.X, ALU.add))
        chain(dve.tensor_scalar(self.var[:, :], self.total[:, :], 1.0 / D, self.epsilons[self.done], ALU.mult, ALU.add))
        self.done += 1
        dve.sem_inc(self.var_ready, 1)
        dve.wait_ge(self.root_ready, self.done)
        chain(dve.reciprocal(self.inverse[:, :], self.root[:, :]))
        chain(dve.tensor_tensor(t, t, per_node(self.inverse[:, :]), ALU.mult))


def gin_nodes(nc, m, x, eps, w1, b1, w2, b2, gamma, beta):
    with Phase(nc, "gin_nodes") as ph:
        loaded, step = ph.sem("loaded"), ph.sem("step")
        ready, z_copied, z_turned, zt_ready, h_summed, h_ready, o_summed, o_added = (
            ph.sem(n) for n in ("ready", "z_copied", "z_turned", "zt_ready", "h_summed", "h_ready", "o_summed",
                                "o_added"))
        w1_t, w2_t = ph.sbuf("w1", [D, D]), ph.sbuf("w2", [D, D])
        b1_t = ph.sbuf("b1", [D, 1])
        b2_t, gamma_t, beta_t = (ph.sbuf(n, [LANES, D]) for n in ("b2", "gamma", "beta"))
        eps_t = ph.sbuf("eps", [LANES, 1])
        r = ph.sbuf("r", [LANES, BLOCKS, D])
        z = ph.sbuf("z", [LANES, 2, D])
        zt = ph.sbuf("zt", [D, 2, LANES])
        h = ph.sbuf("h", [D, 2, LANES])
        turned, hidden, outs = (ph.psum(n, [128, 2, 512]) for n in ("turned", "hidden", "outs"))
        norms = Norms(ph, [1e-5, 1e-5])
        block = ph.block()

        @block.sync
        def _(sp):
            for tile, source in ((m.x[:, :, :], x.rearrange("(b p) f -> p b f", p=LANES)), (w1_t[:, :], w1),
                                 (w2_t[:, :], w2), (b1_t[:, :], b1.rearrange("(n a) -> n a", a=1)),
                                 (b2_t[:, :], row_of(b2, LANES)), (gamma_t[:, :], row_of(gamma, LANES)),
                                 (beta_t[:, :], row_of(beta, LANES)), (eps_t[:, :], row_of(eps, LANES))):
                sp.dma_start(tile, source).then_inc(loaded, 16)

        @block.vector
        def _(dve):
            chain = Chain(dve, step)
            for s in (z_copied, o_added):
                dve.sem_inc(s, CREDIT)
            dve.wait_ge(loaded, 128)
            chain(dve.tensor_scalar(eps_t[:, :], eps_t[:, :], 1.0, None, ALU.add))
            chain(dve.scalar_tensor_tensor(m.acc[:, :, 0:D], m.x[:, :, :], eps_t[:, :], m.acc[:, :, 0:D], ALU.mult,
                                           ALU.add))
            chain(dve.tensor_tensor(r[:, :, :], m.x[:, :, :], per_column(b2_t[:, :]), ALU.add))

            def copy_z(b, s, used):
                dve.wait_ge(z_turned, free(b, 2))
                dve.nop(nofuse=True)
                dve.tensor_copy(z[:, s, :], m.acc[:, ds(b, 1), 0:D]).then_inc(z_copied, 1)

            def add_out(b, s, used):
                dve.wait_ge(o_summed, made(b))
                dve.nop(nofuse=True)
                dve.tensor_tensor(r[:, ds(b, 1), :], r[:, ds(b, 1), :], outs[0:LANES, s, 0:D], ALU.add)\
                    .then_inc(o_added, 1)

            in_steps(dve, BLOCKS, [(0, copy_z), (1, add_out)], 2)
            dve.wait_ge(o_added, made(BLOCKS - 1))
            norms.normalize(dve, chain, r[:, :, :])
            chain(dve.tensor_tensor(r[:, :, :], r[:, :, :], per_column(gamma_t[:, :]), ALU.mult))
            chain(dve.tensor_tensor(r[:, :, :], r[:, :, :], per_column(beta_t[:, :]), ALU.add))
            chain(dve.scalar_tensor_tensor(m.x[:, :, :], r[:, :, :], 0.0, m.x[:, :, :], ALU.max, ALU.add))
            norms.normalize(dve, chain, m.x[:, :, :])

        @block.tensor
        def _(pe):
            for s in (z_turned, h_summed, o_summed):
                pe.sem_inc(s, CREDIT)
            pe.wait_ge(loaded, 128)

            def turn(b, s, used):
                pe.wait_ge(z_copied, made(b))
                pe.wait_ge(zt_ready, free(b, 2))
                pe.transpose(turned[:, s, 0:LANES], z[:, s, :], m.ident[0:LANES, 0:LANES]).then_inc(z_turned, 1)

            def first(b, s, used):
                pe.wait_ge(zt_ready, made(b))
                pe.wait_ge(h_ready, free(b, 2))
                pe.matmul(hidden[:, s, 0:LANES], w1_t[:, :], zt[:, s, :], start=True, stop=True).then_inc(h_summed, 1)

            def second(b, s, used):
                pe.wait_ge(h_ready, made(b))
                pe.wait_ge(o_added, free(b, 2))
                pe.matmul(outs[0:LANES, s, 0:D], h[:, s, :], w2_t[:, :], start=True, stop=True).then_inc(o_summed, 1)

            in_steps(pe, BLOCKS, [(0, turn), (0, first), (0, second)], 2)

        @block.scalar
        def _(act):
            for s in (zt_ready, h_ready):
                act.sem_inc(s, CREDIT)
            act.wait_ge(loaded, 128)

            def copy_zt(b, s, used):
                act.wait_ge(z_turned, made(b))
                act.wait_ge(h_summed, free(b, 2))
                act.copy(zt[:, s, :], turned[:, s, 0:LANES]).then_inc(zt_ready, 1)

            def relu(b, s, used):
                act.wait_ge(h_summed, made(b))
                act.wait_ge(o_summed, free(b, 2))
                act.activation(h[:, s, :], hidden[:, s, 0:LANES], ACT.Relu, bias=b1_t[:, :]).then_inc(h_ready, 1)

            in_steps(act, BLOCKS, [(0, copy_zt), (0, relu)], 2)
            norms.roots(act)


def projections(ph, name, src, weights, width, out_banks, evacuate, evacuator):
    chunks = len(weights)
    pieces = -(-width // 512)
    copied, turned_done, xt_ready, multiplied, taken = (
        ph.sem(f"{name}_{n}") for n in ("copied", "turned", "xt_ready", "multiplied", "taken"))
    x = ph.sbuf(f"{name}_x", [LANES, 2, chunks, D])
    xt = ph.sbuf(f"{name}_xt", [D, 2, chunks, LANES])
    turned = ph.psum(f"{name}_turned_banks", [128, 2, 512])
    outs = ph.psum(f"{name}_outs", [128, out_banks, pieces, 512])

    def dve(e, m):
        e.sem_inc(copied, CREDIT)
        if evacuator == "dve":
            e.sem_inc(taken, CREDIT)

        def copy(b, s, used):
            e.wait_ge(turned_done, free(b, 2))
            e.nop(nofuse=True)
            e.tensor_copy(x[:, s, :, :].rearrange("p c f -> p (c f)"), src[:, ds(b, 1), 0:chunks * D])\
                .then_inc(copied, 1)

        def take(b, s, used):
            e.wait_ge(multiplied, made(b))
            e.nop(nofuse=True)
            evacuate(b, s, outs[0:LANES, s % out_banks]).then_inc(taken, 1)

        in_steps(e, BLOCKS, [(0, copy)] + [(1, take)] * (evacuator == "dve"), 2)
        if evacuator == "dve":
            e.wait_ge(taken, made(BLOCKS - 1))

    def act(e, m):
        e.sem_inc(xt_ready, CREDIT)
        if evacuator == "act":
            e.sem_inc(taken, CREDIT)

        def copy_xt(b, s, used):
            e.wait_ge(turned_done, made(b))
            e.wait_ge(multiplied, free(b, 2))
            e.copy(xt[:, s, :, :].rearrange("p c n -> p (c n)"), turned[:, s, 0:chunks * LANES]).then_inc(xt_ready, 1)

        def take(b, s, used):
            e.wait_ge(multiplied, made(b))
            e.nop(nofuse=True)
            evacuate(b, s, outs[0:LANES, s % out_banks]).then_inc(taken, 1)

        in_steps(e, BLOCKS, [(0, copy_xt)] + [(1, take)] * (evacuator == "act"), 2)

    def pe(e, m):
        e.sem_inc(turned_done, CREDIT)
        e.sem_inc(multiplied, CREDIT)

        def turn(b, s, used):
            e.wait_ge(copied, made(b))
            e.wait_ge(xt_ready, free(b, 2))
            for c in range(chunks):
                last = e.transpose(turned[:, s, c * LANES:(c + 1) * LANES], x[:, s, c, :], m.ident[0:LANES, 0:LANES])
            last.then_inc(turned_done, 1)

        def multiply(b, s, used):
            e.wait_ge(xt_ready, made(b))
            e.wait_ge(taken, free(b, out_banks))
            for piece in range(pieces):
                low, high = 512 * piece, min(512 * piece + 512, width)
                for c in range(chunks):
                    last = e.matmul(outs[0:LANES, s % out_banks, piece, 0:high - low], xt[:, s, c, :],
                                    weights[c][:, low:high], start=c == 0, stop=c == chunks - 1)
            last.then_inc(multiplied, 1)

        in_steps(e, BLOCKS, [(0, turn), (0, multiply)], 2)

    return dve, act, pe


SKIP = 5 * MUL


def equivariant_weights(nc, m, up_s, up_v, r1, r2, dn_s, dn_v, sk_s, sk_v, species):
    with Phase(nc, "equivariant_weights") as ph:
        zeroed, loaded, scaled = ph.sem("zeroed"), ph.sem("loaded"), ph.sem("scaled")
        species_int = ph.sbuf("species_int", [LANES, BLOCKS], I32)
        species_f = ph.sbuf("species_f", [LANES, BLOCKS])
        block = ph.block()
        copies = [(m.up_skip[0:MUL, 0:MUL], up_s),
                  (m.up_skip[0:MUL, D:].rearrange("m (z k) -> m z k", z=SPECIES)[:, :, 0:2 * MUL],
                   sk_s.rearrange("z m k -> m z k")),
                  (m.down[0:2 * MUL, 0, 0:2 * MUL], dn_s),
                  (m.down[2 * MUL:4 * MUL, 0, 2 * MUL:3 * MUL], dn_v),
                  (m.down[0:2 * MUL, 1, 3 * MUL:4 * MUL], dn_v),
                  (m.down[2 * MUL:4 * MUL, 1, 4 * MUL:5 * MUL], dn_v),
                  (species_int[:, :], species.rearrange("(b p) -> p b", p=LANES))]
        for i in range(3):
            rows = m.up_skip[MUL + i:D:3, :]
            copies.append((rows[:, MUL * (i + 1):MUL * (i + 2)], up_v))
            copies.append((rows[:, D:].rearrange("m (z k) -> m z k", z=SPECIES)
                           [:, :, MUL * (i + 2):MUL * (i + 3)], sk_v.rearrange("z m k -> m z k")))
        for j in range(GROUP):
            copies.append((m.radial1[RECORD * j + 8:RECORD * j + 8 + RADIAL, RADIAL * j:RADIAL * (j + 1)], r1))
            copies.append((m.radial2[RADIAL * j:RADIAL * (j + 1), D * j:D * (j + 1)], r2))

        @block.vector
        def _(dve):
            dve.memset(m.up_skip[:, :], 0.0).then_inc(zeroed, 1)
            dve.memset(m.down[:, :, :], 0.0).then_inc(zeroed, 1)
            dve.memset(m.radial1[:, :], 0.0).then_inc(zeroed, 1)
            dve.memset(m.radial2[:, :], 0.0).then_inc(zeroed, 1)
            dve.wait_ge(loaded, 16 * len(copies))
            w_st = m.radial2[:, :].rearrange("r (j f) -> r j f", j=GROUP)[:, :, 3 * MUL:4 * MUL]
            dve.tensor_scalar(w_st, w_st, 0.5773502691896258, None, ALU.mult).then_inc(scaled, 1)
            dve.tensor_copy(species_f[:, :], species_int[:, :]).then_inc(scaled, 1)
            dve.wait_ge(scaled, 2)
            for z in range(SPECIES):
                dve.tensor_scalar(m.is_species[:, :, z], species_f[:, :], float(z), None, ALU.is_equal)\
                    .then_inc(scaled, 1)
            dve.wait_ge(scaled, 2 + SPECIES)

        @block.sync
        def _(sp):
            sp.wait_ge(zeroed, 4)
            with nc.allow_non_contiguous_dma("the species of nodes, 12 KB, nodes of a block on partitions"):
                for tile, source in copies:
                    sp.dma_start(tile, source).then_inc(loaded, 16)


def equivariant_sources(nc, m, table):
    with Phase(nc, "equivariant_sources") as ph:
        stored, part = ph.sem("stored"), ph.sem("part")
        up = ph.sbuf("up", [LANES, BLOCKS, D])
        up_done, whole = ph.sem("up_done"), ph.sem("whole")
        block = ph.block()
        holder = {}

        def evacuate(b, s, outs):
            e = holder["dve"]
            e.tensor_scalar(up[:, ds(b, 1), :], outs[:, 0, 0:D], MUL ** -0.5, None, ALU.mult)
            for z in range(SPECIES):
                low = D + z * SKIP
                pieces = [(0, SKIP, low)] if low // 512 == (low + SKIP - 1) // 512 else [
                    (0, 512 - low % 512, low), (512 - low % 512, SKIP, low // 512 * 512 + 512)]
                for first, end, at in pieces:
                    values = outs[:, at // 512, at % 512:at % 512 + end - first]
                    target = m.skip[:, ds(b, 1), first:end]
                    if z == 0:
                        last = e.tensor_scalar(target, values, m.is_species[:, ds(b, 1), z], None, ALU.mult)
                    else:
                        last = e.scalar_tensor_tensor(target, values, m.is_species[:, ds(b, 1), z], target, ALU.mult,
                                                      ALU.add)
                if z < SPECIES - 1:
                    last.then_inc(part, 1)
                    e.wait_ge(part, b * (SPECIES - 1) + (z + 1))
                    e.nop(nofuse=True)
            return last

        dve_steps, act_steps, pe_steps = projections(ph, "up", m.x, [m.up_skip], D + SPECIES * SKIP, 2, evacuate,
                                                     "dve")

        @block.vector
        def _(dve):
            holder["dve"] = dve
            dve_steps(dve, m)
            dve.drain().then_inc(up_done, 1)

        @block.scalar
        def _(act):
            act_steps(act, m)

        @block.tensor
        def _(pe):
            pe_steps(pe, m)

        @block.sync
        def _(sp):
            sp.wait_ge(up_done, 1)
            sp.dma_start(table.rearrange("(b p) f -> p b f", p=LANES), up[:, :, :]).then_inc(stored, 16)
            sp.wait_ge(stored, 16)


def equivariant_messages(nc, m, table):
    with Phase(nc, "equivariant") as ph:
        gathered = software_dma_sems(nc, m, ph, DEEP)
        (index_ready, onehot_ready, record_ready, record_turned, turned_ready, hidden_summed, hidden_ready,
         weights_made, products, product_ready, dot_begun, dot_ready, messages_ready, summed, first_added, added,
         cleared) = (
            ph.sem(x) for x in ("index_ready", "onehot_ready", "record_ready", "record_turned", "turned_ready",
                                "hidden_summed", "hidden_ready", "weights_made", "products", "product_ready",
                                "dot_begun", "dot_ready", "messages_ready", "summed", "first_added", "added",
                                "cleared"))
        index = ph.sbuf("index", [SLOTS, DEEP, GROUP], I32)
        rows = ph.sbuf("rows", [SLOTS, DEEP, GROUP, D])
        onehot = ph.sbuf("onehot", [SLOTS, DEEP, GROUP, LANES])
        record = ph.sbuf("record", [SLOTS, DEEP, GROUP, RECORD])
        turned = ph.sbuf("turned", [GROUP * RECORD, 2, SLOTS])
        hidden = ph.sbuf("hidden", [GROUP * RADIAL, 2, SLOTS])
        scalar_vt = ph.sbuf("scalar_vt", [SLOTS, 2, GROUP, MUL])
        product = ph.sbuf("product", [SLOTS, 2, GROUP, 3, MUL])
        dot = ph.sbuf("dot", [SLOTS, 2, GROUP, MUL])
        message = ph.sbuf("message", [SLOTS, 2, GROUP, 2 * D])
        radial = ph.psum("radial", [128, 1, 512])
        hidden_sum = ph.psum("hidden_sum", [128, 1, 512])
        weight = ph.psum("weight", [128, 2, GROUP, D])
        sums = ph.psum("sums", [128, 2, GROUP_PAIRS, 2 * D])
        block = ph.block()

        def sums_of_pair(s, p):
            return sums[0:LANES, s, p, :]

        @block.scalar
        def _(act):
            for s in (index_ready, record_ready, turned_ready, hidden_ready):
                act.sem_inc(s, CREDIT)

            def copy_record(k, s, used):
                act.wait_ge(products, free(k, DEEP))
                act.nop(nofuse=True)
                act.copy(record[:, s, :, :], m.record[:, ds(k * GROUP, GROUP), :]).then_inc(record_ready, 1)

            def copy_turned(k, s, used):
                act.wait_ge(record_turned, made(k))
                act.wait_ge(hidden_summed, free(k, 2))
                act.copy(turned[:, s % 2, :], radial[0:GROUP * RECORD, 0, 0:SLOTS]).then_inc(turned_ready, 1)

            def silu(k, s, used):
                act.wait_ge(hidden_summed, made(k))
                act.wait_ge(weights_made, free(k, 2))
                act.activation(hidden[:, s % 2, :], hidden_sum[0:GROUP * RADIAL, 0, 0:SLOTS], ACT.Silu,
                               scale=RADIAL ** -0.5).then_inc(hidden_ready, 1)

            in_steps(act, GROUPS, [(0, index_stage(act, m, index, m.sender, gathered, index_ready)),
                                   (2, copy_record), (3, copy_turned), (4, silu)],
                     DEEP)

        @block.gpsimd
        def _(pool):
            in_steps(pool, GROUPS, [(0, gather_stage(pool, table, rows, index, gathered, index_ready, products, DEEP))],
                     DEEP)

        @block.tensor
        def _(pe):
            for s in (record_turned, hidden_summed, weights_made, summed):
                pe.sem_inc(s, CREDIT)

            def turn_record(k, s, used):
                pe.wait_ge(record_ready, made(k))
                pe.wait_ge(turned_ready, free(k, 1))
                pe.nop(nofuse=True)
                pe.transpose(radial[0:GROUP * RECORD, 0, 0:SLOTS], record[:, s, :, :].rearrange("p j w -> p (j w)"),
                             m.ident[:, :]).then_inc(record_turned, 1)

            def hide(k, s, used):
                pe.wait_ge(turned_ready, made(k))
                pe.wait_ge(hidden_ready, free(k, 1))
                pe.nop(nofuse=True)
                pe.matmul(hidden_sum[0:GROUP * RADIAL, 0, 0:SLOTS], m.radial1[:, :], turned[:, s % 2, :],
                          start=True, stop=True).then_inc(hidden_summed, 1)

            def make_weights(k, s, used):
                pe.wait_ge(hidden_ready, made(k))
                pe.wait_ge(messages_ready, free(k, 2))
                pe.matmul(weight[:, s % 2, :, :].rearrange("p j f -> p (j f)"), hidden[:, s % 2, :], m.radial2[:, :],
                          start=True, stop=True).then_inc(weights_made, 1)

            def sum_tiles(k, s, used):
                pe.wait_ge(messages_ready, made(k))
                pe.wait_ge(onehot_ready, made(k))
                pe.wait_ge(added, free(k, 2))
                sum_pairs(pe, lambda j: onehot[:, s, j, :], lambda j: message[:, s % 2, j, :], sums_of_pair, s)\
                    .then_inc(summed, 1)

            in_steps(pe, GROUPS, [(0, turn_record), (1, hide), (2, make_weights), (4, sum_tiles)], DEEP)

        @block.vector
        def _(dve):
            dve.memset(m.acc[:, :, :], 0.0).then_inc(cleared, 1)
            dve.wait_ge(cleared, 1)
            for s in (onehot_ready, products, product_ready, dot_begun, dot_ready, messages_ready, first_added,
                      added):
                dve.sem_inc(s, CREDIT)

            def parts(k, s):
                p = s % 2
                y = record[:, s, :, 5:8].unsqueeze(3).to_broadcast([SLOTS, GROUP, 3, MUL])
                return (rows[:, s, :, 0:MUL], rows[:, s, :, MUL:D].rearrange("p j (i k) -> p j i k", i=3), y,
                        [weight[:, p, :, MUL * n:MUL * (n + 1)] for n in range(4)],
                        message[:, p, :, 2 * MUL:].rearrange("p j (i h k) -> p j i h k", i=3, h=2))

            def multiply(k, s, used):
                p = s % 2
                scalars, vectors, y, (w_ss, w_vs, w_vt, w_st), halves = parts(k, s)
                dve.wait_ge(gathered[s], used * (16 * GROUP) + 16 * GROUP)
                dve.nop(nofuse=True)
                dve.wait_ge(weights_made, made(k))
                dve.nop(nofuse=True)
                dve.tensor_tensor(product[:, p, :, :, :], vectors, y, ALU.mult).then_inc(product_ready, 1)
                dve.tensor_tensor(scalar_vt[:, p, :, :], scalars, w_vt, ALU.mult)
                dve.wait_ge(summed, free(k, 2))
                dve.nop(nofuse=True)
                dve.tensor_tensor(message[:, p, :, 0:MUL], scalars, w_ss, ALU.mult)

            def begin_dot(k, s, used):
                p = s % 2
                scalars, vectors, y, (w_ss, w_vs, w_vt, w_st), halves = parts(k, s)
                dve.wait_ge(product_ready, made(k))
                dve.nop(nofuse=True)
                dve.tensor_tensor(dot[:, p, :, :], product[:, p, :, 0, :], product[:, p, :, 1, :], ALU.add)\
                    .then_inc(dot_begun, 1)
                dve.tensor_tensor(halves[:, :, :, 0, :], vectors, w_vs.unsqueeze(2).to_broadcast(
                    [SLOTS, GROUP, 3, MUL]), ALU.mult)

            def end_dot(k, s, used):
                p = s % 2
                scalars, vectors, y, (w_ss, w_vs, w_vt, w_st), halves = parts(k, s)
                dve.wait_ge(dot_begun, made(k))
                dve.nop(nofuse=True)
                dve.tensor_tensor(dot[:, p, :, :], dot[:, p, :, :], product[:, p, :, 2, :], ALU.add)\
                    .then_inc(dot_ready, 1)
                dve.tensor_tensor(halves[:, :, :, 1, :], scalar_vt[:, p, :, :].unsqueeze(2).to_broadcast(
                    [SLOTS, GROUP, 3, MUL]), y, ALU.mult).then_inc(products, 1)

            def finish(k, s, used):
                dve.wait_ge(dot_ready, made(k))
                dve.nop(nofuse=True)
                dve.tensor_tensor(message[:, s % 2, :, MUL:2 * MUL], dot[:, s % 2, :, :],
                                  weight[:, s % 2, :, 3 * MUL:4 * MUL], ALU.mult).then_inc(messages_ready, 1)

            read_first, read_second, add = add_stages(dve, m, m.receiver_block, 2 * D, sums_of_pair, summed,
                                                      first_added, added)
            in_steps(dve, GROUPS, [
                (3, multiply), (5, read_first), (3, begin_dot), (5, read_second), (3, end_dot),
                (2, match_stage(dve, m, onehot, m.record, onehot_ready, summed, DEEP)), (3, finish), (5, add)], DEEP)


def equivariant_nodes(nc, m):
    with Phase(nc, "equivariant_nodes") as ph:
        step = ph.sem("step")
        gates_asked, gates_ready = ph.sem("gates_asked"), ph.sem("gates_ready")
        g = ph.sbuf("g", [LANES, BLOCKS, SKIP])
        gated = ph.sbuf("gated", [LANES, BLOCKS, 2 * MUL])
        norms = Norms(ph, [1e-5])
        block = ph.block()
        holder = {}
        down_scale = 0.5 * RADIAL ** -0.5 * 16.0 ** -0.5 * (2 * MUL) ** -0.5

        def evacuate(b, s, outs):
            return holder["dve"].scalar_tensor_tensor(g[:, ds(b, 1), :], outs[:, 0, 0:SKIP], down_scale,
                                                      m.skip[:, ds(b, 1), :], ALU.mult, ALU.add)

        dve_steps, act_steps, pe_steps = projections(ph, "down", m.acc, [m.down[:, 0, :], m.down[:, 1, :]], SKIP, 2,
                                                     evacuate, "dve")

        @block.vector
        def _(dve):
            holder["dve"] = dve
            chain = Chain(dve, step)
            chain(dve.tensor_scalar(m.skip[:, :, :], m.skip[:, :, :], 0.5 * MUL ** -0.5, None, ALU.mult))
            dve_steps(dve, m)
            dve.sem_inc(gates_asked, 1)
            dve.wait_ge(gates_ready, 1)
            chain(dve.tensor_tensor(m.x[:, :, 0:MUL], m.x[:, :, 0:MUL], gated[:, :, 0:MUL], ALU.add))
            for i in range(3):
                vector = g[:, :, MUL * (i + 2):MUL * (i + 3)]
                chain(dve.tensor_tensor(vector, vector, gated[:, :, MUL:2 * MUL], ALU.mult))
                x_i = m.x[:, :, MUL:D].rearrange("p b (k i) -> p b k i", i=3)[:, :, :, i]
                chain(dve.tensor_tensor(x_i, x_i, vector, ALU.add))
            norms.normalize(dve, chain, m.x[:, :, :])

        @block.scalar
        def _(act):
            act_steps(act, m)
            act.wait_ge(gates_asked, 1)
            act.activation(gated[:, :, :], g[:, :, 0:2 * MUL], ACT.Silu).then_inc(gates_ready, 1)
            norms.roots(act)

        @block.tensor
        def _(pe):
            pe_steps(pe, m)


def attention_weights(nc, m, wq, bq, wk, bk, wv, bv):
    with Phase(nc, "attention_weights") as ph:
        loaded, turned, copied = ph.sem("loaded"), ph.sem("turned"), ph.sem("copied")
        raw = ph.sbuf("raw", [D, 3, D])
        bank = ph.psum("bank", [128, 512])
        block = ph.block()

        @block.sync
        def _(sp):
            for n, (w, b) in enumerate(((wq, bq), (wk, bk), (wv, bv))):
                sp.dma_start(raw[:, n, :], w).then_inc(loaded, 16)
                sp.dma_start(m.qkv_bias[:, n * D:(n + 1) * D], row_of(b, LANES)).then_inc(loaded, 16)

        @block.tensor
        def _(pe):
            pe.wait_ge(loaded, 96)
            for n in range(3):
                last = pe.transpose(bank[:, n * D:(n + 1) * D], raw[:, n, :], m.ident[:, :])
            last.then_inc(turned, 1)

        @block.vector
        def _(dve):
            dve.wait_ge(turned, 1)
            dve.tensor_copy(m.qkv[:, :], bank[:, 0:3 * D]).then_inc(copied, 1)
            dve.wait_ge(copied, 1)


def attention_sources(nc, m, table):
    with Phase(nc, "attention_sources") as ph:
        stored, kv_done = ph.sem("stored"), ph.sem("kv_done")
        kv = ph.sbuf("kv", [LANES, BLOCKS, 2 * D])
        block = ph.block()
        holder = {}

        def evacuate(b, s, outs):
            e = holder["dve"]
            e.tensor_tensor(m.query[:, ds(b, 1), :], outs[:, 0, 0:D], m.qkv_bias[:, 0:D], ALU.add)
            return e.tensor_tensor(kv[:, ds(b, 1), :], outs[:, 0, D:3 * D], m.qkv_bias[:, D:3 * D], ALU.add)

        dve_steps, act_steps, pe_steps = projections(ph, "qkv", m.x, [m.qkv], 3 * D, 2, evacuate, "dve")

        @block.vector
        def _(dve):
            holder["dve"] = dve
            dve_steps(dve, m)
            dve.drain().then_inc(kv_done, 1)

        @block.scalar
        def _(act):
            act_steps(act, m)

        @block.tensor
        def _(pe):
            pe_steps(pe, m)

        @block.sync
        def _(sp):
            sp.wait_ge(kv_done, 1)
            sp.dma_start(table.rearrange("(b p) f -> p b f", p=LANES), kv[:, :, :]).then_inc(stored, 16)
            sp.wait_ge(stored, 16)


def attention_messages(nc, m, table):
    wide = D + HEADS
    with Phase(nc, "attention") as ph:
        gathered = software_dma_sems(nc, m, ph, RING)
        (index_ready, onehot_ready, onehot_turned, turned_ready, queries_ready, product_ready, score_ready, clipped,
         exp_ready, messages_ready, summed, first_added, added, cleared) = (
            ph.sem(x) for x in ("index_ready", "onehot_ready", "onehot_turned", "turned_ready", "queries_ready",
                                "product_ready", "score_ready", "clipped", "exp_ready", "messages_ready", "summed",
                                "first_added", "added", "cleared"))
        index = ph.sbuf("index", [SLOTS, RING, GROUP], I32)
        rows = ph.sbuf("rows", [SLOTS, RING, GROUP, 2 * D])
        onehot = ph.sbuf("onehot", [SLOTS, RING, GROUP, LANES])
        turned = ph.sbuf("turned", [LANES, RING, GROUP, SLOTS])
        product = ph.sbuf("product", [SLOTS, 2, GROUP, D])
        score = ph.sbuf("score", [SLOTS, 2, GROUP, HEADS])
        message = ph.sbuf("message", [SLOTS, RING, GROUP, wide])
        turned_bank = ph.psum("turned_bank", [128, GROUP, SLOTS])
        query_bank = ph.psum("query_bank", [128, 2, GROUP, D])
        sums = ph.psum("sums", [128, 2, 512])
        block = ph.block()

        def sums_of_pair(s, p):
            return sums[0:LANES, s, p * wide:(p + 1) * wide]

        @block.scalar
        def _(act):
            for s in (index_ready, turned_ready, exp_ready):
                act.sem_inc(s, CREDIT)

            def copy_turned(k, s, used):
                act.wait_ge(onehot_turned, made(k))
                act.wait_ge(queries_ready, free(k))
                act.copy(turned[:, s, :, :], turned_bank[0:LANES, :, :]).then_inc(turned_ready, 1)

            def exponentials(k, s, used):
                act.wait_ge(clipped, made(k))
                act.wait_ge(summed, free(k))
                act.activation(message[:, s, :, D:wide], score[:, s % 2, :, :], ACT.Exp, scale=HEAD ** -0.5)\
                    .then_inc(exp_ready, 1)

            in_steps(act, GROUPS, [(0, index_stage(act, m, index, m.receiver, gathered, index_ready)),
                                   (4, exponentials), (2, copy_turned)])

        @block.gpsimd
        def _(pool):
            in_steps(pool, GROUPS, [(0, gather_stage(pool, table, rows, index, gathered, index_ready,
                                                     messages_ready))])

        @block.tensor
        def _(pe):
            for s in (onehot_turned, queries_ready, summed):
                pe.sem_inc(s, CREDIT)

            def turn(k, s, used):
                pe.wait_ge(onehot_ready, made(k))
                pe.wait_ge(turned_ready, free(k, 1))
                for j in range(GROUP):
                    last = pe.transpose(turned_bank[0:LANES, j, :], onehot[:, s, j, :], m.ident[:, :])
                last.then_inc(onehot_turned, 1)

            def queries(k, s, used):
                for j in range(GROUP):
                    if j % PAIR == 0:
                        b = pe.value_load(m.sender_block[0:1, ds(k * GROUP_PAIRS + j // PAIR, 1)], min_val=0,
                                          max_val=BLOCKS - 1)
                    if j == 0:
                        pe.wait_ge(turned_ready, made(k))
                        pe.nop(nofuse=True)
                        pe.wait_ge(product_ready, free(k, 2))
                        pe.nop(nofuse=True)
                    last = pe.matmul(query_bank[:, s % 2, j, :], turned[:, s, j, :], m.query[:, ds(b, 1), :],
                                     start=True, stop=True)
                last.then_inc(queries_ready, 1)

            def sum_tiles(k, s, used):
                pe.wait_ge(messages_ready, made(k))
                pe.wait_ge(added, free(k, 2))
                sum_pairs(pe, lambda j: onehot[:, s, j, :], lambda j: message[:, s, j, :], sums_of_pair, s)\
                    .then_inc(summed, 1)

            in_steps(pe, GROUPS, [(2, queries), (4, sum_tiles), (1, turn)])

        @block.vector
        def _(dve):
            dve.memset(m.acc[:, :, 0:wide], 0.0).then_inc(cleared, 1)
            dve.wait_ge(cleared, 1)
            for s in (onehot_ready, product_ready, score_ready, clipped, messages_ready, first_added, added):
                dve.sem_inc(s, CREDIT)

            def multiply(k, s, used):
                dve.wait_ge(gathered[s], used * (16 * GROUP) + 16 * GROUP)
                dve.nop(nofuse=True)
                dve.wait_ge(queries_ready, made(k))
                dve.nop(nofuse=True)
                dve.tensor_tensor(product[:, s % 2, :, :], query_bank[:, s % 2, :, :], rows[:, s, :, 0:D], ALU.mult)\
                    .then_inc(product_ready, 1)

            def scores(k, s, used):
                dve.wait_ge(product_ready, made(k))
                dve.nop(nofuse=True)
                dve.wait_ge(exp_ready, free(k, 2))
                dve.nop(nofuse=True)
                dve.tensor_reduce(score[:, s % 2, :, :],
                                  product[:, s % 2, :, :].rearrange("p j (h c) -> p j h c", h=HEADS), AX.X, ALU.add)\
                    .then_inc(score_ready, 1)

            def clip(k, s, used):
                dve.wait_ge(score_ready, made(k))
                dve.nop(nofuse=True)
                dve.tensor_scalar(score[:, s % 2, :, :], score[:, s % 2, :, :], -10.0 * HEAD ** 0.5,
                                  10.0 * HEAD ** 0.5, ALU.max, ALU.min).then_inc(clipped, 1)

            def messages(k, s, used):
                dve.wait_ge(exp_ready, made(k))
                dve.nop(nofuse=True)
                dve.tensor_tensor(message[:, s, :, 0:D].rearrange("p j (h c) -> p j h c", h=HEADS),
                                  rows[:, s, :, D:2 * D].rearrange("p j (h c) -> p j h c", h=HEADS),
                                  message[:, s, :, D:wide].unsqueeze(3).to_broadcast([SLOTS, GROUP, HEADS, HEAD]),
                                  ALU.mult).then_inc(messages_ready, 1)

            read_first, read_second, add = add_stages(dve, m, m.sender_block, wide, sums_of_pair, summed, first_added,
                                                      added)
            in_steps(dve, GROUPS, [
                (5, read_first), (3, multiply), (5, read_second), (4, messages), (3, scores), (5, add),
                (1, match_stage(dve, m, onehot, m.sender_place, onehot_ready, summed)), (3, clip)])


def attention_nodes(nc, m, gamma, beta):
    with Phase(nc, "attention_nodes") as ph:
        loaded, step = ph.sem("loaded"), ph.sem("step")
        gamma_t, beta_t = (ph.sbuf(n, [LANES, D]) for n in ("gamma", "beta"))
        r = ph.sbuf("r", [LANES, BLOCKS, D])
        norms = Norms(ph, [1e-6, 1e-5])
        block = ph.block()

        @block.sync
        def _(sp):
            sp.dma_start(gamma_t[:, :], row_of(gamma, LANES)).then_inc(loaded, 16)
            sp.dma_start(beta_t[:, :], row_of(beta, LANES)).then_inc(loaded, 16)

        @block.vector
        def _(dve):
            chain = Chain(dve, step)
            sums = m.acc[:, :, D:D + HEADS]
            chain(dve.tensor_scalar(sums, sums, 1e-8, None, ALU.add))
            chain(dve.reciprocal(sums, sums))
            for h in range(HEADS):
                at = slice(h * HEAD, (h + 1) * HEAD)
                chain(dve.tensor_tensor(r[:, :, at], m.acc[:, :, at],
                                        m.acc[:, :, D + h:D + h + 1].to_broadcast([LANES, BLOCKS, HEAD]), ALU.mult))
            chain(dve.tensor_tensor(r[:, :, :], r[:, :, :], m.x[:, :, :], ALU.add))
            norms.normalize(dve, chain, r[:, :, :])
            dve.wait_ge(loaded, 32)
            chain(dve.tensor_tensor(r[:, :, :], r[:, :, :], per_column(gamma_t[:, :]), ALU.mult))
            chain(dve.tensor_tensor(r[:, :, :], r[:, :, :], per_column(beta_t[:, :]), ALU.add))
            chain(dve.tensor_tensor(m.x[:, :, :], m.x[:, :, :], r[:, :, :], ALU.add))
            norms.normalize(dve, chain, m.x[:, :, :])

        @block.scalar
        def _(act):
            norms.roots(act)


WIDE = D + 2


def edge_logits(nc, m, layers):
    with Phase(nc, "edge_logits") as ph:
        loaded, step, spread, asked = (ph.sem(n) for n in ("loaded", "step", "spread", "asked"))
        we_t = ph.sbuf("we", [3, 3, D])
        ae_t = ph.sbuf("ae", [3, 3, D])
        factor = ph.sbuf("factor", [3, 3])
        diagonal = ph.sbuf("diagonal", [3, 3, 3])
        factors = ph.sbuf("factors", [128, 9])
        total = ph.sbuf("total", [SLOTS, 3])
        empty = ph.sbuf("empty", [SLOTS, TILES])
        bank = ph.psum("bank", [128, 2, 512])
        block = ph.block()

        @block.sync
        def _(sp):
            for n, (we, ae) in enumerate(layers):
                sp.dma_start(we_t[:, n, :], we).then_inc(loaded, 16)
                sp.dma_start(ae_t[:, n, :], row_of(ae, 3)).then_inc(loaded, 16)

        @block.vector
        def _(dve):
            chain = Chain(dve, step)
            dve.wait_ge(loaded, 96)
            chain(dve.tensor_tensor(we_t[:, :, :], we_t[:, :, :], ae_t[:, :, :], ALU.mult))
            chain(dve.tensor_reduce(factor[:, :], we_t[:, :, :], AX.X, ALU.add))
            for n in range(3):
                chain(dve.tensor_scalar(diagonal[:, n, :], m.ident[0:3, 0:3], factor[:, n:n + 1], None, ALU.mult))
            dve.sem_inc(asked, 1)
            dve.wait_ge(spread, 1)
            chain(dve.tensor_copy(factors[:, :], bank[:, 0, 0:9]))
            for n in range(3):
                chain(dve.tensor_scalar(m.edge_logit[:, n, :], m.record[:, :, 2], factors[:, 3 * n:3 * n + 1], None,
                                        ALU.mult))
                for a in (1, 2):
                    chain(dve.scalar_tensor_tensor(m.edge_logit[:, n, :], m.record[:, :, 2 + a],
                                                   factors[:, 3 * n + a:3 * n + a + 1], m.edge_logit[:, n, :],
                                                   ALU.mult, ALU.add))
            chain(dve.tensor_reduce(total[:, :], m.edge_logit[:, :, :], AX.X, ALU.add))
            dve.sem_inc(asked, 1)
            chain(dve.tensor_scalar(empty[:, :], m.record[:, :, 1], 0.0, FAR, ALU.is_equal, ALU.mult))
            for n in range(3):
                chain(dve.tensor_tensor(m.edge_logit[:, n, :], m.edge_logit[:, n, :], empty[:, :], ALU.add))
            dve.wait_ge(spread, 2)
            chain(dve.tensor_scalar(m.mean_logit[:, :], bank[0:LANES, 1, 0:3], 1.0 / EDGES, None, ALU.mult))

        @block.tensor
        def _(pe):
            pe.wait_ge(asked, 1)
            pe.matmul(bank[:, 0, 0:9], m.ones[0:3, :], diagonal[:, :, :].rearrange("p n a -> p (n a)"), start=True,
                      stop=True).then_inc(spread, 1)
            pe.wait_ge(asked, 2)
            pe.matmul(bank[0:LANES, 1, 0:3], m.ones[:, 0:LANES], total[:, :], start=True, stop=True)\
                .then_inc(spread, 1)


def gat_sources(nc, m, source, w, a_src, a_dst, table):
    with Phase(nc, f"gat{m.layer}_sources") as ph:
        stored, loaded, step, h_done = ph.sem("stored"), ph.sem("loaded"), ph.sem("step"), ph.sem("h_done")
        w_t = ph.sbuf("w", [D, D + 3])
        a_t = ph.sbuf("a", [D, 2, D])
        product = ph.sbuf("product", [D, 2, D])
        by_block = ph.sbuf("by_block", [BLOCKS, LANES])
        bank = ph.psum("bank", [128, 2, 512])
        w_ready, al_d_ready, turned, copied, al_d_spread = (
            ph.sem(x) for x in ("w_ready", "al_d_ready", "turned", "copied", "al_d_spread"))
        block = ph.block()
        holder = {}

        def evacuate(b, s, outs):
            return holder["dve"].tensor_copy(m.h[:, ds(b, 1), :], outs[:, 0, 0:D + 3])

        dve_steps, act_steps, pe_steps = projections(ph, "h", source, [w_t], D + 3, 2, evacuate, "dve")

        @block.vector
        def _(dve):
            holder["dve"] = dve
            chain = Chain(dve, step)
            dve.wait_ge(loaded, 48)
            chain(dve.memset(w_t[:, D:D + 1], 0.0))
            chain(dve.tensor_tensor(product[:, :, :], a_t[:, :, :],
                                    w_t[:, 0:D].unsqueeze(1).to_broadcast([D, 2, D]), ALU.mult))
            chain(dve.tensor_reduce(w_t[:, D + 1:D + 3], product[:, :, :], AX.X, ALU.add))
            dve.sem_inc(w_ready, 1)
            dve_steps(dve, m)
            chain(dve.memset(m.h[:, :, D:D + 1], 1.0))
            dve.sem_inc(h_done, 1)
            chain(dve.tensor_copy(m.al_d[:, :], m.h[:, :, D + 2]))
            dve.sem_inc(al_d_ready, 1)
            chain(dve.memset(m.node_terms[:, 0:1, :], FAR))
            dve.wait_ge(turned, 1)
            chain(dve.tensor_copy(by_block[:, :], bank[0:BLOCKS, 0, 0:LANES]))
            dve.sem_inc(copied, 1)
            dve.wait_ge(al_d_spread, 1)
            chain(dve.tensor_copy(m.node_terms[:, 1:1 + PAIRS, 1], bank[0:LANES, 1, 0:PAIRS]))

        @block.scalar
        def _(act):
            act_steps(act, m)

        @block.tensor
        def _(pe):
            pe.wait_ge(w_ready, 1)
            pe_steps(pe, m)
            pe.wait_ge(al_d_ready, 1)
            pe.transpose(bank[0:BLOCKS, 0, 0:LANES], m.al_d[:, :], m.ident[0:LANES, 0:LANES]).then_inc(turned, 1)
            pe.wait_ge(copied, 1)
            pe.matmul(bank[0:LANES, 1, 0:PAIRS], by_block[:, :], m.pair_is[:, :], start=True, stop=True)\
                .then_inc(al_d_spread, 1)

        @block.sync
        def _(sp):
            sp.dma_start(w_t[:, 0:D], w).then_inc(loaded, 16)
            sp.dma_start(a_t[:, 0, :], row_of(a_src, D)).then_inc(loaded, 16)
            sp.dma_start(a_t[:, 1, :], row_of(a_dst, D)).then_inc(loaded, 16)
            sp.wait_ge(h_done, 1)
            sp.dma_start(table.rearrange("(b p) f -> p b f", p=LANES), m.h[:, :, 0:WIDE]).then_inc(stored, 16)
            sp.wait_ge(stored, 16)


def gat_messages(nc, m, table):
    with Phase(nc, f"gat{m.layer}") as ph:
        gathered = software_dma_sems(nc, m, ph, DEEP)
        (index_ready, other_ready, other_turned, turned_ready, source_ready, masked_ready, masked_turned, found,
         with_al_d, found_alpha, top_ready, first_drop, drop_ready, scale_ready, terms_spread, edge_sum, edge_alpha,
         shift_ready, exp_ready, weighted_ready, summed, first_added, added, first_stored, stored,
         cleared) = (
            ph.sem(x) for x in (
                "index_ready", "other_ready", "other_turned", "turned_ready", "source_ready", "masked_ready",
                "masked_turned", "found", "with_al_d", "found_alpha", "top_ready", "first_drop", "drop_ready",
                "scale_ready", "terms_spread", "edge_sum", "edge_alpha", "shift_ready", "exp_ready",
                "weighted_ready", "summed", "first_added", "added", "first_stored", "stored",
                "cleared"))
        index = ph.sbuf("index", [SLOTS, DEEP, GROUP], I32)
        rows = ph.sbuf("rows", [SLOTS, DEEP, GROUP, WIDE])
        other = ph.sbuf("other", [SLOTS, DEEP, GROUP, LANES])
        turned = ph.sbuf("turned", [LANES, RING, GROUP, SLOTS])
        masked = ph.sbuf("masked", [SLOTS, 2, GROUP, LANES])
        weighted = ph.sbuf("weighted", [SLOTS, 2, GROUP, LANES])
        source = ph.sbuf("source", [SLOTS, RING, GROUP])
        alpha = ph.sbuf("alpha", [SLOTS, 2, GROUP])
        weight = ph.sbuf("weight", [SLOTS, 2, GROUP])
        top = ph.sbuf("top", [LANES, 2, GROUP_PAIRS])
        drop = ph.sbuf("drop", [LANES, 2, GROUP_PAIRS])
        scale = ph.sbuf("scale", [LANES, RING, GROUP_PAIRS])
        run = ph.sbuf("run", [LANES, RING, GROUP_PAIRS, D + 1])
        turned_bank = ph.psum("turned_bank", [128, GROUP, SLOTS])
        masked_bank = ph.psum("masked_bank", [128, GROUP, SLOTS])
        terms_bank = ph.psum("terms_bank", [128, 2, 512])
        sums = ph.psum("sums", [128, 2, 512])
        block = ph.block()

        def sums_of_pair(s, p):
            return sums[0:LANES, s, p * (D + 1):(p + 1) * (D + 1)]

        def spread(s):
            return terms_bank[:, s, 0:2 * GROUP].rearrange("p (j t) -> p j t", t=2)

        @block.scalar
        def _(act):
            for s in (index_ready, turned_ready, scale_ready, exp_ready, first_stored, stored):
                act.sem_inc(s, CREDIT)

            def turn_over(k, s, used):
                s = s % RING
                act.wait_ge(other_turned, made(k))
                act.wait_ge(terms_spread, free(k))
                act.activation(turned[:, s, :, :], turned_bank[0:LANES, :, :], ACT.Copy, bias=1.0, scale=-1.0)\
                    .then_inc(turned_ready, 1)

            def scales(k, s, used):
                act.wait_ge(drop_ready, made(k))
                act.wait_ge(added, free(k))
                act.activation(scale[:, s % RING, :], drop[:, s % 2, :], ACT.Exp).then_inc(scale_ready, 1)

            def exponentials(k, s, used):
                act.wait_ge(shift_ready, made(k))
                act.activation(weight[:, s % 2, :], weight[:, s % 2, :], ACT.Exp).then_inc(exp_ready, 1)

            def store(k, s, used):
                for p in range(GROUP_PAIRS):
                    b = act.value_load(m.receiver_block[0:1, ds(k * GROUP_PAIRS + p, 1)], min_val=0,
                                       max_val=BLOCKS - 1)
                    if p == 0:
                        act.wait_ge(added, made(k))
                        act.nop(nofuse=True)
                    act.wait_ge(*((stored, free(k, 1)) if p == 0 else (first_stored, made(k))))
                    act.nop(nofuse=True)
                    act.copy(m.acc[:, ds(b, 1), 0:D + 1], run[:, s % RING, p, :])
                    act.copy(m.top[:, ds(b, 1)], m.node_terms[:, ds(k * GROUP_PAIRS + (p + 1), 1), 0])\
                        .then_inc(first_stored if p == 0 else stored, 1)

            act.wait_ge(cleared, 4)
            in_steps(act, GROUPS, [(0, index_stage(act, m, index, m.sender, gathered, index_ready)),
                                   (3, turn_over), (8, store), (6, exponentials), (5, scales)], DEEP)

        @block.gpsimd
        def _(pool):
            in_steps(pool, GROUPS, [(0, gather_stage(pool, table, rows, index, gathered, index_ready, summed, DEEP))],
                     DEEP)

        @block.tensor
        def _(pe):
            for s in (other_turned, masked_turned, terms_spread, summed):
                pe.sem_inc(s, CREDIT)

            def turn(k, s, used):
                pe.wait_ge(other_ready, made(k))
                pe.wait_ge(turned_ready, free(k, 1))
                for j in range(GROUP):
                    last = pe.transpose(turned_bank[0:LANES, j, :], other[:, s, j, :], m.ident[:, :])
                last.then_inc(other_turned, 1)

            def turn_masked(k, s, used):
                pe.wait_ge(masked_ready, made(k))
                pe.wait_ge(found, free(k, 1))
                for j in range(GROUP):
                    last = pe.transpose(masked_bank[0:LANES, j, :], masked[:, s % 2, j, :], m.ident[:, :])
                last.then_inc(masked_turned, 1)

            def spread_terms(k, s, used):
                pe.wait_ge(top_ready, made(k))
                pe.wait_ge(turned_ready, made(k))
                pe.wait_ge(shift_ready, free(k, 2))
                pe.nop(nofuse=True)
                for j in range(GROUP):
                    last = pe.matmul(spread(s % 2)[:, j, :], turned[:, s % RING, j, :],
                                     m.node_terms[:, ds(k * GROUP_PAIRS + (1 + j // PAIR), 1), :], start=True,
                                     stop=True)
                last.then_inc(terms_spread, 1)

            def sum_tiles(k, s, used):
                pe.wait_ge(weighted_ready, made(k))
                pe.wait_ge(added, free(k, 2))
                sum_pairs(pe, lambda j: weighted[:, s % 2, j, :], lambda j: rows[:, s, j, 0:D + 1], sums_of_pair, s)\
                    .then_inc(summed, 1)

            in_steps(pe, GROUPS, [(0, turn), (1, turn_masked), (4, sum_tiles), (2, spread_terms)], DEEP)

        @block.vector
        def _(dve):
            dve.memset(m.acc[:, :, 0:D + 1], 0.0).then_inc(cleared, 1)
            dve.memset(run[:, RING - 1, GROUP_PAIRS - 1, :], 0.0).then_inc(cleared, 1)
            dve.memset(m.node_terms[:, 0:1, :], FAR).then_inc(cleared, 1)
            dve.memset(m.top[:, :], FAR).then_inc(cleared, 1)
            dve.wait_ge(cleared, 4)
            for s in (other_ready, source_ready, masked_ready, found, with_al_d, found_alpha, top_ready, first_drop,
                      drop_ready, edge_sum, edge_alpha, shift_ready, weighted_ready, first_added, added):
                dve.sem_inc(s, CREDIT)

            def wait(sem, value):
                dve.wait_ge(sem, value)
                dve.nop(nofuse=True)

            def match(k, s, used):
                wait(other_turned, free(k, DEEP))
                dve.tensor_tensor(
                    other[:, s, :, :], m.ramp[:, 1:1 + LANES].unsqueeze(1).to_broadcast([SLOTS, GROUP, LANES]),
                    m.record[:, ds(k * GROUP, GROUP), 1:2].to_broadcast([SLOTS, GROUP, LANES]), ALU.not_equal)\
                    .then_inc(other_ready, 1)

            def sources(k, s, used):
                wait(gathered[s], used * (16 * GROUP) + 16 * GROUP)
                dve.tensor_tensor(source[:, s % RING, :], rows[:, s, :, D + 1],
                                  m.edge_logit[:, m.layer, ds(k * GROUP, GROUP)], ALU.add).then_inc(source_ready, 1)

            def mask(k, s, used):
                wait(source_ready, made(k))
                wait(masked_turned, free(k, 2))
                dve.scalar_tensor_tensor(masked[:, s % 2, :, :], other[:, s, :, :], FAR,
                                         source[:, s % RING, :].unsqueeze(2).to_broadcast([SLOTS, GROUP, LANES]),
                                         ALU.mult, ALU.add).then_inc(masked_ready, 1)

            def find(k, s, used):
                wait(masked_turned, made(k))
                dve.tensor_reduce(top[:, s % 2, :], masked_bank[0:LANES, :, :].rearrange(
                    "p (q j) s -> p q (j s)", q=GROUP_PAIRS), AX.X, ALU.max).then_inc(found, 1)

            def add_al_d(k, s, used):
                wait(found, made(k))
                dve.tensor_tensor(top[:, s % 2, :], top[:, s % 2, :],
                                  m.node_terms[:, ds(k * GROUP_PAIRS + 1, GROUP_PAIRS), 1], ALU.add)\
                    .then_inc(with_al_d, 1)

            def rectify_found(k, s, used):
                wait(with_al_d, made(k))
                dve.scalar_tensor_tensor(top[:, s % 2, :], top[:, s % 2, :], 0.2, top[:, s % 2, :], ALU.mult,
                                         ALU.max).then_inc(found_alpha, 1)

            def run_top(k, s, used):
                wait(found_alpha, made(k))
                dve.tensor_tensor_scan(m.node_terms[:, ds(k * GROUP_PAIRS + 1, GROUP_PAIRS), 0],
                                       m.reset[0:LANES, ds(k * GROUP_PAIRS, GROUP_PAIRS)], top[:, s % 2, :],
                                       m.node_terms[:, ds(k * GROUP_PAIRS, 1), 0], ALU.add, ALU.max)\
                    .then_inc(top_ready, 1)

            def drops(k, s, used):
                wait(top_ready, made(k))
                wait(scale_ready, free(k, 2))
                for p in range(GROUP_PAIRS):
                    dve.scalar_tensor_tensor(drop[:, s % 2, p:p + 1], m.node_terms[:, ds(k * GROUP_PAIRS + p, 1), 0],
                                             m.reset[0:LANES, ds(k * GROUP_PAIRS + p, 1)],
                                             m.node_terms[:, ds(k * GROUP_PAIRS + (p + 1), 1), 0], ALU.add,
                                             ALU.subtract).then_inc(first_drop if p == 0 else drop_ready, 1)

            def edge_sums(k, s, used):
                wait(terms_spread, made(k))
                dve.tensor_tensor(alpha[:, s % 2, :], source[:, s % RING, :], spread(s % 2)[:, :, 1], ALU.add)\
                    .then_inc(edge_sum, 1)

            def edge_alphas(k, s, used):
                wait(edge_sum, made(k))
                dve.scalar_tensor_tensor(alpha[:, s % 2, :], alpha[:, s % 2, :], 0.2, alpha[:, s % 2, :], ALU.mult,
                                         ALU.max).then_inc(edge_alpha, 1)

            def shifts(k, s, used):
                wait(edge_alpha, made(k))
                dve.tensor_tensor(weight[:, s % 2, :], alpha[:, s % 2, :], spread(s % 2)[:, :, 0], ALU.subtract)\
                    .then_inc(shift_ready, 1)

            def weigh(k, s, used):
                wait(exp_ready, made(k))
                wait(summed, free(k, 2))
                dve.scalar_tensor_tensor(weighted[:, s % 2, :, :], other[:, s, :, :], 0.0,
                                         weight[:, s % 2, :].unsqueeze(2).to_broadcast([SLOTS, GROUP, LANES]),
                                         ALU.is_equal, ALU.mult).then_inc(weighted_ready, 1)

            def add_first(k, s, used):
                wait(added, free(k, 1))
                wait(summed, made(k))
                wait(scale_ready, made(k))
                wait(stored, free(k))
                dve.scalar_tensor_tensor(run[:, s % RING, 0, :], run[:, (s - 1) % RING, GROUP_PAIRS - 1, :],
                                         scale[:, s % RING, 0:1], sums_of_pair(s % 2, 0), ALU.mult, ALU.add)\
                    .then_inc(first_added, 1)

            def add_second(k, s, used):
                wait(first_added, made(k))
                dve.scalar_tensor_tensor(run[:, s % RING, 1, :], run[:, s % RING, 0, :], scale[:, s % RING, 1:2],
                                         sums_of_pair(s % 2, 1), ALU.mult, ALU.add).then_inc(added, 1)

            in_steps(dve, GROUPS, [
                (1, sources), (2, find), (0, match), (2, add_al_d), (3, edge_sums), (1, mask), (2, rectify_found),
                (3, edge_alphas), (4, weigh), (2, run_top), (3, shifts), (5, add_first), (2, drops),
                (5, add_second)], DEEP)


def gat_nodes(nc, m, target, bias, gamma, beta, x_out=None):
    with Phase(nc, f"gat{m.layer}_nodes") as ph:
        loaded, step, asked, answered, stored, x_done = (
            ph.sem(n) for n in ("loaded", "step", "asked", "answered", "stored", "x_done"))
        totals_asked, totals_ready = ph.sem("totals_asked"), ph.sem("totals_ready")
        bias_t, gamma_t, beta_t = (ph.sbuf(n, [LANES, D]) for n in ("bias", "gamma", "beta"))
        own, peak, inverse = (ph.sbuf(n, [LANES, BLOCKS]) for n in ("own", "peak", "inverse"))
        drop = ph.sbuf("drop", [LANES, 2, BLOCKS])
        column = ph.sbuf("column", [LANES, D])
        mean, inv_std, std = (ph.sbuf(n, [LANES, D]) for n in ("mean", "inv_std", "std"))
        square = ph.sbuf("square", [LANES, BLOCKS, D])
        norms = Norms(ph, [1e-5]) if x_out is not None else None
        bank = ph.psum("bank", [128, 512])
        block = ph.block()

        @block.sync
        def _(sp):
            for tile, source in ((bias_t, bias), (gamma_t, gamma), (beta_t, beta)):
                sp.dma_start(tile[:, :], row_of(source, LANES)).then_inc(loaded, 16)
            if x_out is not None:
                sp.wait_ge(x_done, 1)
                sp.dma_start(x_out.rearrange("(b p) f -> p b f", p=LANES), m.x[:, :, :]).then_inc(stored, 16)
                sp.wait_ge(stored, 16)

        @block.vector
        def _(dve):
            chain = Chain(dve, step)
            t = target[:, :, 0:D]
            sums, exps, tops = m.acc[:, :, 0:D], m.acc[:, :, D], m.top[:, :]
            chain(dve.tensor_tensor(own[:, :], m.h[:, :, D + 1], m.al_d[:, :], ALU.add))
            chain(dve.tensor_scalar(own[:, :], own[:, :], m.mean_logit[:, m.layer:m.layer + 1], None, ALU.add))
            chain(dve.scalar_tensor_tensor(own[:, :], own[:, :], 0.2, own[:, :], ALU.mult, ALU.max))
            chain(dve.tensor_tensor(peak[:, :], own[:, :], tops, ALU.max))
            chain(dve.tensor_tensor(drop[:, 0, :], tops, peak[:, :], ALU.subtract))
            chain(dve.tensor_tensor(drop[:, 1, :], own[:, :], peak[:, :], ALU.subtract))
            dve.sem_inc(asked, 1)
            dve.wait_ge(answered, 1)
            chain(dve.tensor_tensor(exps, exps, drop[:, 0, :], ALU.mult))
            chain(dve.tensor_tensor(exps, exps, drop[:, 1, :], ALU.add))
            chain(dve.tensor_scalar(exps, exps, 1e-16, None, ALU.add))
            chain(dve.reciprocal(inverse[:, :], exps))
            chain(dve.tensor_tensor(drop[:, 0, :], drop[:, 0, :], inverse[:, :], ALU.mult))
            chain(dve.tensor_tensor(drop[:, 1, :], drop[:, 1, :], inverse[:, :], ALU.mult))
            chain(dve.tensor_tensor(sums, sums, per_node(drop[:, 0, :]), ALU.mult))
            chain(dve.tensor_tensor(square[:, :, :], m.h[:, :, 0:D], per_node(drop[:, 1, :]), ALU.mult))
            chain(dve.tensor_tensor(t, sums, square[:, :, :], ALU.add))
            dve.wait_ge(loaded, 48)
            chain(dve.tensor_tensor(t, t, per_column(bias_t[:, :]), ALU.add))
            chain(dve.scalar_tensor_tensor(t, t, 0.01, t, ALU.mult, ALU.max))
            chain(dve.tensor_reduce(column[:, :], t.rearrange("p b f -> p f b"), AX.X, ALU.add))
            dve.sem_inc(totals_asked, 1)
            dve.wait_ge(totals_ready, 1)
            chain(dve.tensor_scalar(mean[:, :], bank[0:LANES, 0:D], 1.0 / NODES, None, ALU.mult))
            chain(dve.tensor_tensor(t, t, per_column(mean[:, :]), ALU.subtract))
            chain(dve.tensor_tensor(square[:, :, :], t, t, ALU.mult))
            chain(dve.tensor_reduce(column[:, :], square[:, :, :].rearrange("p b f -> p f b"), AX.X, ALU.add))
            dve.sem_inc(totals_asked, 1)
            dve.wait_ge(totals_ready, 2)
            chain(dve.tensor_scalar(inv_std[:, :], bank[0:LANES, D:2 * D], 1.0 / NODES, 1e-5, ALU.mult, ALU.add))
            dve.sem_inc(asked, 1)
            dve.wait_ge(answered, 2)
            chain(dve.reciprocal(inv_std[:, :], std[:, :]))
            chain(dve.tensor_tensor(inv_std[:, :], inv_std[:, :], gamma_t[:, :], ALU.mult))
            chain(dve.tensor_tensor(t, t, per_column(inv_std[:, :]), ALU.mult))
            chain(dve.tensor_tensor(t, t, per_column(beta_t[:, :]), ALU.add))
            if x_out is not None:
                chain(dve.tensor_tensor(m.x[:, :, :], m.x[:, :, :], t, ALU.add))
                norms.normalize(dve, chain, m.x[:, :, :])
                dve.sem_inc(x_done, 1)

        @block.scalar
        def _(act):
            act.wait_ge(asked, 1)
            act.activation(drop[:, :, :], drop[:, :, :], ACT.Exp).then_inc(answered, 1)
            act.wait_ge(asked, 2)
            act.activation(std[:, :], inv_std[:, :], ACT.Sqrt).then_inc(answered, 1)
            if x_out is not None:
                norms.roots(act)

        @block.tensor
        def _(pe):
            for n in range(2):
                pe.wait_ge(totals_asked, n + 1)
                pe.matmul(bank[0:LANES, n * D:(n + 1) * D], m.ones[0:LANES, 0:LANES], column[:, :], start=True,
                          stop=True).then_inc(totals_ready, 1)


class Memory:
    pass


def gnn(nc, x, src, dst, edge_attr_3, edge_attr_4, edge_attr_8, node_type_4, *rest):
    *w, out = rest
    stack = ExitStack()
    with stack:
        m = Memory()
        m.kept = stack

        def sbuf(name, shape, dtype=F32):
            return stack.enter_context(nc.sbuf_tensor(name, shape, dtype))

        m.ident = sbuf("ident", [128, 128])
        m.ones = sbuf("ones", [128, 128])
        m.earlier = sbuf("earlier", [128, 128])
        m.ramp = sbuf("ramp", [128, PAIRS])
        m.lane = sbuf("lane", [128, 1])
        m.record = sbuf("records", [SLOTS, TILES, RECORD])
        m.sender = sbuf("sender", [SLOTS, TILES], I32)
        m.receiver_block = sbuf("receiver_block", [1, PAIRS], I32)
        m.reset = sbuf("reset", [SLOTS, PAIRS])
        m.pair_is = sbuf("pair_is", [BLOCKS, PAIRS])
        m.acc = sbuf("acc", [LANES, BLOCKS, 2 * D])
        m.receiver = sbuf("receiver", [SLOTS, TILES], I32)
        m.sender_place = sbuf("by_sender", [SLOTS, TILES, 2])
        m.sender_block = sbuf("sender_block", [1, PAIRS], I32)
        constants(nc, m)
        order_edges(nc, m, src, dst, edge_attr_3, edge_attr_4, edge_attr_8)
        m.x = sbuf("nodes", [LANES, BLOCKS, D])
        sum_neighbours(nc, m, x)
        gin_nodes(nc, m, x, *w[0:7])
        with ExitStack() as layer:
            def own(name, shape, dtype=F32):
                return layer.enter_context(nc.sbuf_tensor(name, shape, dtype))

            m.up_skip = own("up_skip", [D, D + SPECIES * SKIP])
            m.down = own("down", [D, 2, SKIP])
            m.radial1 = own("radial1", [GROUP * RECORD, GROUP * RADIAL])
            m.radial2 = own("radial2", [GROUP * RADIAL, GROUP * D])
            m.is_species = own("is_species", [LANES, BLOCKS, SPECIES])
            m.skip = own("skip", [LANES, BLOCKS, SKIP])
            sources = nc.dram_tensor("equivariant_table", [NODES, D], F32, kind="Internal").ap()
            equivariant_weights(nc, m, *w[7:15], node_type_4)
            equivariant_sources(nc, m, sources)
            equivariant_messages(nc, m, sources)
            equivariant_nodes(nc, m)
        with ExitStack() as layer:
            m.qkv = layer.enter_context(nc.sbuf_tensor("qkv", [D, 3 * D], F32))
            m.qkv_bias = layer.enter_context(nc.sbuf_tensor("qkv_bias", [LANES, 3 * D], F32))
            m.query = layer.enter_context(nc.sbuf_tensor("query", [LANES, BLOCKS, D], F32))
            sources = nc.dram_tensor("attention_table", [NODES, 2 * D], F32, kind="Internal").ap()
            attention_weights(nc, m, *w[15:21])
            attention_sources(nc, m, sources)
            attention_messages(nc, m, sources)
            attention_nodes(nc, m, *w[21:23])
        m.edge_logit = sbuf("edge_logit", [SLOTS, 3, TILES])
        m.mean_logit = sbuf("mean_logit", [LANES, 3])
        m.h = sbuf("h", [LANES, BLOCKS, D + 3])
        m.node_terms = sbuf("node_terms", [LANES, 1 + PAIRS, 2])
        m.top = sbuf("top", [LANES, BLOCKS])
        m.al_d = sbuf("al_d", [LANES, BLOCKS])
        gat_in = sbuf("gat_in", [LANES, BLOCKS, D])
        gat = [w[23 + 8 * n:31 + 8 * n] for n in range(3)]
        edge_logits(nc, m, [(we, ae) for _, _, _, we, ae, _, _, _ in gat])
        for m.layer, (wn, a_src, a_dst, _, _, bias, gamma, beta) in enumerate(gat):
            sources = nc.dram_tensor(f"gat_table{m.layer}", [NODES, WIDE], F32, kind="Internal").ap()
            gat_sources(nc, m, m.x if m.layer == 0 else gat_in, wn, a_src, a_dst, sources)
            gat_messages(nc, m, sources)
            gat_nodes(nc, m, gat_in, bias, gamma, beta, out if m.layer == 2 else None)

def kernel(**inputs):
    import numpy as np
    import concourse.bacc as bacc
    from concourse.bass_utils import run_bass_kernel_spmd

    nc = bacc.Bacc("TRN2", target_bir_lowering=False, num_devices=1)
    arrays, args = {}, []
    for name, value in inputs.items():
        a = np.ascontiguousarray(value)
        a = a.reshape(1) if a.ndim == 0 else a
        arrays[f"in_{name}"] = a
        args.append(nc.dram_tensor(f"in_{name}", a.shape, mybir.dt.from_np(a.dtype), kind="ExternalInput").ap())
    args.append(nc.dram_tensor("out_nodes", (NODES, D), F32, kind="ExternalOutput").ap())
    gnn(nc, *args)
    return run_bass_kernel_spmd(nc, [arrays], core_ids=[0]).results[0]["out_nodes"]
```
